# Optimizing a Trainium2 kernel written in Bass

```python
import numpy as np
import jax
import jax.numpy as jnp

def _softmax(x, axis=-1):
    return jax.nn.softmax(x, axis=axis)

def _gelu(x):
    return jax.nn.gelu(x, approximate=True)

def _silu(x):
    return jax.nn.silu(x)

def _sigmoid(x):
    return jax.nn.sigmoid(x)

def _layernorm(x, axis=-1, eps=1e-05):
    m = jnp.mean(x, axis=axis, keepdims=True)
    v = jnp.var(x, axis=axis, keepdims=True)
    return (x - m) / jnp.sqrt(v + eps)

def _scatter_add(tgt, idx, src, axis=0):
    return tgt.at[idx].add(src)

def _segment_sum(src, seg, n):
    return jax.ops.segment_sum(src, seg, n)
kernel_name = 'mk_gnn_preln_d2_gnn_r64_ae30d5'

def setup_inputs(seed: int=0):
    np.random.seed(seed)
    _w = jnp.asarray

    def _rec_inputs():
        import jax
        import jax.numpy as jnp
        _gk = jax.random.key(seed)
        x = -0.000202 + 1 * jax.random.normal(jax.random.fold_in(_gk, 1), (100000, 128), jnp.float32)
        src = jax.random.randint(jax.random.fold_in(_gk, 2), (50000,), 0, 100000, jnp.int32)
        dst = jnp.minimum((100000 * jax.random.uniform(jax.random.fold_in(_gk, 3), (50000,)) ** 2.0).astype(jnp.int32), 99999)
        _o = jnp.argsort(dst, stable=True)
        src = src[_o]
        dst = dst[_o]
        edge_type_8 = jax.random.randint(jax.random.fold_in(_gk, 12), (50000,), 0, 8, jnp.int32)
        return (x, src, dst, edge_type_8)
    x, src, dst, edge_type_8 = _rec_inputs()

    def _L0_gnn_setup():
        import jax, jax.numpy as jnp
        import numpy as np
        NUM_NODES = 50000
        NUM_EDGES = 25000
        DIM = 128
        NUM_REL = 8
        NUM_LAYERS = 2

        def _rgcn_conv(x, W, root, bias, src, dst, etype):
            R, N = (W.shape[0], x.shape[0])
            xW = jnp.einsum('ni,rio->rno', x, W)
            msgs = xW[etype, src]
            seg = etype * N + dst
            agg = jax.ops.segment_sum(msgs, seg, num_segments=R * N)
            cnt = jax.ops.segment_sum(jnp.ones_like(seg, dtype=x.dtype), seg, num_segments=R * N)
            agg = agg / jnp.maximum(cnt, 1.0)[:, None]
            agg = agg.reshape(R, N, -1).sum(axis=0)
            return agg + x @ root + bias
        key = jax.random.key(seed)
        ks = jax.random.split(key, 8)
        x = jax.random.normal(ks[0], (NUM_NODES, DIM), dtype=jnp.float32)
        edge_index = jax.random.randint(ks[1], (2, NUM_EDGES), 0, NUM_NODES, dtype=jnp.int32)
        edge_types = jax.random.randint(ks[2], (NUM_EDGES,), 0, NUM_REL, dtype=jnp.int32)
        scale = 1.0 / np.sqrt(DIM)
        weights = jax.random.normal(ks[3], (NUM_LAYERS, NUM_REL, DIM, DIM), dtype=jnp.float32) * scale
        roots = jax.random.normal(ks[4], (NUM_LAYERS, DIM, DIM), dtype=jnp.float32) * scale
        biases = jnp.zeros((NUM_LAYERS, DIM), dtype=jnp.float32)
        return {'x': x, 'weights': weights, 'roots': roots, 'biases': biases, 'edge_index': edge_index, 'edge_types': edge_types}
    _L0_gnn_all = _L0_gnn_setup()
    _L0_gnn_in = {k: v for k, v in _L0_gnn_all.items() if k in ('weights', 'roots', 'biases')}
    del _L0_gnn_all

    def _L1_gnn_setup():
        import jax, jax.numpy as jnp
        import numpy as np
        N_NODES = 50000
        N_EDGES = 25000
        IN_F = 128
        HEADS = 4
        OUT_F = 32
        NEG_SLOPE = 0.2
        key = jax.random.key(seed)
        k1, k2, k3, k4 = jax.random.split(key, 4)
        x = jax.random.normal(k1, (N_NODES, IN_F), dtype=jnp.float32)
        indices = jax.random.randint(k2, (2, N_EDGES), 0, N_NODES, dtype=jnp.int64)
        weight = jax.random.normal(k3, (IN_F, HEADS * OUT_F), dtype=jnp.float32) * (1.0 / np.sqrt(IN_F))
        att = jax.random.normal(k4, (1, HEADS, 2 * OUT_F), dtype=jnp.float32) * (1.0 / np.sqrt(2 * OUT_F))
        bias = jnp.zeros((HEADS * OUT_F,), dtype=jnp.float32)
        return {'x': x, 'indices': indices, 'weight': weight, 'att': att, 'bias': bias}
    _L1_gnn_all = _L1_gnn_setup()
    _L1_gnn_in = {k: v for k, v in _L1_gnn_all.items() if k in ('weight', 'att', 'bias')}
    del _L1_gnn_all
    return {'x': x, 'src': src, 'dst': dst, 'edge_type_8': edge_type_8, 'L0_gnn_weights': _L0_gnn_in['weights'], 'L0_gnn_roots': _L0_gnn_in['roots'], 'L0_gnn_biases': _L0_gnn_in['biases'], 'L1_gnn_weight': _L1_gnn_in['weight'], 'L1_gnn_att': _L1_gnn_in['att'], 'L1_gnn_bias': _L1_gnn_in['bias']}

def reference(x, src, dst, edge_type_8, L0_gnn_weights, L0_gnn_roots, L0_gnn_biases, L1_gnn_weight, L1_gnn_att, L1_gnn_bias):
    import jax
    import jax.numpy as jnp

    def _L0_gnn_ref(x, weights, roots, biases, edge_index, edge_types):
        import jax, jax.numpy as jnp
        import numpy as np
        NUM_NODES = 50000
        NUM_EDGES = 25000
        DIM = 128
        NUM_REL = 8
        NUM_LAYERS = 2

        def _rgcn_conv(x, W, root, bias, src, dst, etype):
            R, N = (W.shape[0], x.shape[0])
            xW = jnp.einsum('ni,rio->rno', x, W)
            msgs = xW[etype, src]
            seg = etype * N + dst
            agg = jax.ops.segment_sum(msgs, seg, num_segments=R * N)
            cnt = jax.ops.segment_sum(jnp.ones_like(seg, dtype=x.dtype), seg, num_segments=R * N)
            agg = agg / jnp.maximum(cnt, 1.0)[:, None]
            agg = agg.reshape(R, N, -1).sum(axis=0)
            return agg + x @ root + bias
        src, dst = (edge_index[0], edge_index[1])
        h = x
        for l in range(NUM_LAYERS - 1):
            h = _rgcn_conv(h, weights[l], roots[l], biases[l], src, dst, edge_types)
            h = jax.nn.relu(h)
        h = _rgcn_conv(h, weights[-1], roots[-1], biases[-1], src, dst, edge_types)
        return h

    def _L1_gnn_ref(x, indices, weight, att, bias):
        import jax, jax.numpy as jnp
        import numpy as np
        N_NODES = 50000
        N_EDGES = 25000
        IN_F = 128
        HEADS = 4
        OUT_F = 32
        NEG_SLOPE = 0.2
        N = x.shape[0]
        H = att.shape[1]
        F = att.shape[2] // 2
        h = (x @ weight).reshape(N, H, F)
        att_src = att[0, :, :F]
        att_dst = att[0, :, F:]
        e_src = jnp.einsum('nhf,hf->nh', h, att_src)
        e_dst = jnp.einsum('nhf,hf->nh', h, att_dst)
        row = indices[0]
        col = indices[1]
        alpha = e_src[row] + e_dst[col]
        alpha = jnp.where(alpha >= 0, alpha, NEG_SLOPE * alpha)
        amax = jax.ops.segment_max(alpha, row, num_segments=N)
        ex = jnp.exp(alpha - amax[row])
        denom = jax.ops.segment_sum(ex, row, num_segments=N)
        alpha = ex / (denom[row] + 1e-16)
        out = jax.ops.segment_sum(alpha[:, :, None] * h[col], row, num_segments=N)
        out = out.reshape(N, H * F) + bias
        return out
    edge_index = jnp.stack([src, dst])
    h = jnp.maximum(_layernorm(x, axis=-1), 0.0)
    x = x + _L0_gnn_ref(h, L0_gnn_weights, L0_gnn_roots, L0_gnn_biases, edge_index, edge_type_8)
    h = jnp.maximum(_layernorm(x, axis=-1), 0.0)
    x = x + _L1_gnn_ref(h, edge_index, L1_gnn_weight, L1_gnn_att, L1_gnn_bias)
    return x

_drawn_inputs = setup_inputs


def setup_inputs(seed=0):
    import zlib

    import numpy as np

    out = dict(_drawn_inputs(seed))
    spreads = {'L0_gnn_biases': (0.0, 0.1), 'L1_gnn_bias': (0.0, 0.1)}
    factors = {'L1_gnn_att': 3.878}
    for name, (base, spread) in spreads.items():
        noise = np.random.default_rng([zlib.crc32(name.encode()), seed]).standard_normal(out[name].shape)
        drawn = base * np.exp(spread * noise) if base else spread * noise
        out[name] = jnp.asarray(drawn.astype(out[name].dtype))
    for name, factor in factors.items():
        out[name] = (out[name] * factor).astype(out[name].dtype)
    return out
```

```python
import concourse.bass as bass
from concourse import mybir
from contextlib import ExitStack, contextmanager

N = 100000
E = 50000
D = 128
R = 8
H = 4
F = D // H
P = 128
SLOPE = 0.2
EPS = 1e-5
TINY = 1e-16
NEG = 1e38

KSHIFT = 17
NODE_PAD = (1 << KSHIFT) - 1
LOGN = 16
FREE = (1 << LOGN) // P
LOADP, LOADF = 125, 400
U = 4
GA = 100
TA = GA * U
GC = 98
TC = GC * U
RB = 8
NB = 98
BLK = P * RB


def gnn_program(nc, x, src, dst, etype, w_rel, roots, biases, w_gat, att, b_gat, out):
    f32, i32 = mybir.dt.float32, mybir.dt.int32
    ALU, ACT, AX = mybir.AluOpType, mybir.ActivationFunctionType, mybir.AxisListType

    y_dram = nc.dram_tensor("y_scratch", (N + P, D), f32, kind="Internal").ap()
    g_dram = nc.dram_tensor("g_scratch", (TC * P, D), f32, kind="Internal").ap()
    g_tiles = g_dram.rearrange("(g u q) d -> g q u d", u=U, q=P)

    ctx = ExitStack()
    with ctx:
        def sb(name, shape, dt=f32):
            return ctx.enter_context(nc.sbuf_tensor(name, shape, dt))

        def sem(name):
            return ctx.enter_context(nc.semaphore(name))

        def chain_of(eng, s, start=0):
            count = [start]

            def link(ins):
                count[0] += 1
                ins.then_inc(s, 1)
                eng.wait_ge(s, count[0])
            return link

        ident = sb("ident", [P, P])
        ones = sb("ones", [P, P])
        epsc = sb("epsc", [P, 1])
        W = sb("W", [P, 2, R * D])
        root = sb("root", [P, 2, D])
        bias_bc = sb("bias_bc", [P, 3, D])
        wg = sb("wg", [P, D + 2 * H])
        att_bc = sb("att_bc", [P, H, 2 * F])
        key_a = sb("key_a", [P, TA])
        w_a = sb("w_a", [P, TA])
        gat_a = sb("gat_a", [P, TA])
        put_a = sb("put_a", [P, TA])
        rel_a = sb("rel_a", [1, TA], i32)
        key_c = sb("key_c", [P, TC])
        gat_c = sb("gat_c", [P, TC])
        own_c = sb("own_c", [P, TC])
        put_c = sb("put_c", [P, TC])
        score = sb("score", [P, H, TC])

        ps = [ctx.enter_context(nc.psum_tensor(f"ps{i}", [P, 512], f32)) for i in range(8)]
        up_c, down_c = sb("up_c", [P, FREE]), sb("down_c", [P, FREE])

        s_w, s_id, s_dump, s_set = sem("weights_loaded"), sem("constants"), sem("dump_cleared"), sem("setup_step")
        with (nc.sbuf_tensor("wa_tmp", [P, H, 2, F], f32) as wa_tmp, nc.sbuf_tensor("zeros", [P, D], f32) as zeros,
              nc.Block() as block):
            @block.scalar
            def _(act):
                act.wait_ge(s_id, 4)
                act.dma_start(y_dram[N:N + P, :], zeros[:, :]).then_inc(s_dump, 16)
                act.dma_start(out[N:N + P, :], zeros[:, :]).then_inc(s_dump, 16)
                act.wait_ge(s_dump, 32)

            @block.sync
            def _(sp):
                for l in range(2):
                    for r in range(R):
                        sp.dma_start(W[:, l, r * D:(r + 1) * D], w_rel[l, r, :, :]).then_inc(s_w, 16)
                    sp.dma_start(root[:, l, :], roots[l, :, :]).then_inc(s_w, 16)
                sp.dma_start(wg[:, 0:D], w_gat).then_inc(s_w, 16)
                sp.dma_start(bias_bc[:, 0:2, :], biases.rearrange("(a l) d -> a l d", a=1).to_broadcast([P, 2, D])).then_inc(s_w, 16)
                sp.dma_start(bias_bc[:, 2, :], b_gat.rearrange("(a d) -> a d", a=1).to_broadcast([P, D])).then_inc(s_w, 16)
                sp.dma_start(att_bc[:, :, :], att.to_broadcast([P, H, 2 * F])).then_inc(s_w, 16)
                sp.wait_ge(s_w, 16 * (2 * (R + 1) + 4))

            @block.gpsimd
            def _(pool):
                pool.memset(ident[:, :], 0.0).then_inc(s_id, 1)
                pool.memset(ones[:, :], 1.0).then_inc(s_id, 1)
                pool.memset(epsc[:, :], EPS).then_inc(s_id, 1)
                pool.memset(zeros[:, :], 0.0).then_inc(s_id, 1)
                pool.wait_ge(s_id, 4)
                pool.affine_select(out=ident[:, :], in_=ident[:, :], compare_op=ALU.not_equal, fill=1.0,
                                   base=0, pattern=[[-1, P]], channel_multiplier=1).then_inc(s_id, 1)

            @block.vector
            def _(dve):
                link = chain_of(dve, s_set)
                dve.wait_ge(s_w, 16 * (2 * (R + 1) + 4))
                wv = wg[:, 0:D].rearrange("p (h f) -> p h f", h=H)
                for side, col in ((1, 0), (0, 1)):
                    link(nc.vector.tensor_tensor(wa_tmp[:, :, side, :], wv, att_bc[:, :, side * F:(side + 1) * F], ALU.mult))
                    link(nc.vector.tensor_reduce(wg[:, D + col * H:D + (col + 1) * H], wa_tmp[:, :, side, :], AX.X, ALU.add))

        sort_edges(nc, sb, sem, chain_of, ps, ident, ones, src, dst, etype,
                   key_a, w_a, gat_a, put_a, rel_a, key_c, gat_c, own_c, put_c, up_c, down_c)

        with phase_semaphores(nc, ctx) as phase:
            dense_pass(nc, phase, ps, ident, x, None, y_dram, root[:, 0, :], bias_bc, epsc, 1)
        with phase_semaphores(nc, ctx) as phase:
            rgcn_edges(nc, phase, ps, ident, x, y_dram, W, 0, epsc, key_a, w_a, gat_a, put_a, rel_a)
        with phase_semaphores(nc, ctx) as phase:
            dense_pass(nc, phase, ps, ident, y_dram, x, out, root[:, 1, :], bias_bc, epsc, 2)
        with phase_semaphores(nc, ctx) as phase:
            rgcn_edges(nc, phase, ps, ident, y_dram, out, W, 1, epsc, key_a, w_a, gat_a, put_a, rel_a)
        with phase_semaphores(nc, ctx) as phase:
            gat_scores(nc, phase, ps, ident, out, g_tiles, wg, bias_bc, epsc, gat_c, own_c, score)
        with phase_semaphores(nc, ctx) as phase:
            gat_softmax(nc, phase, chain_of, ps, ident, up_c, down_c, score)
        with phase_semaphores(nc, ctx) as phase:
            gat_edges(nc, phase, ps, ident, g_tiles, out, score, key_c, put_c)


@contextmanager
def phase_semaphores(nc, keep):
    with ExitStack() as held:
        mine = []

        def sem(name):
            if name[:-1].endswith(("gathered", "stored", "put")):
                return keep.enter_context(nc.semaphore(name))
            mine.append(held.enter_context(nc.semaphore(name)))
            return mine[-1]
        yield sem
        with nc.Block() as block:
            @block.gpsimd
            def _(pool):
                for s in mine:
                    pool.sem_clear(s)


def sort_steps():
    for phase in range(1, LOGN + 1):
        if phase >= 10:
            yield "turn", 0
            for bit in range(phase - 1, 8, -1):
                yield "stage", 1 << (bit - 9)
            yield "turn", 0
        for bit in range(min(phase, 9) - 1, -1, -1):
            yield "stage", 1 << bit
        if phase < LOGN:
            yield "flip", phase


def totals_vector(nc, dve, link, asked, turned, n, ps, v, res, up, down, tmp, small, rows, heads, parts, biggest):
    f32 = mybir.dt.float32
    ALU, AX = mybir.AluOpType, mybir.AxisListType
    V = nc.vector
    ends, carry = small[0:parts, 0:2 * heads], small[0:parts, 2 * heads:3 * heads]
    flag = small[0:parts, 3 * heads:3 * heads + 1]
    rflag, rsh = rows[0:heads, 0, 0:parts], rows[0:heads, 1, :]
    for back in (0, 1):
        if back:
            link(V.tensor_scalar(tmp[0:parts, 0, :], down, -1.0, 1.0, ALU.mult, ALU.add))
            link(V.tensor_tensor(v, res, tmp[0:parts, 0:1, :].to_broadcast([parts, heads, FREE]), ALU.mult))
            cont, op0, op1, neutral, same = down, ALU.mult, ALU.add, 0.0, down
        elif biggest:
            link(V.tensor_scalar(tmp[0:parts, 0, :], up, NEG, -NEG, ALU.mult, ALU.add))
            cont, op0, op1, neutral, same = tmp[0:parts, 0, :], ALU.add, ALU.max, -NEG, up
        else:
            cont, op0, op1, neutral, same = up, ALU.mult, ALU.add, 0.0, up
        way = slice(None, None, -1) if back else slice(None)
        edge = slice(0, 1) if back else slice(FREE - 1, FREE)
        for h in range(heads):
            last = V.tensor_tensor_scan(res[:, h, way], cont[:, way], v[:, h, way], neutral, op0, op1)
        link(last)
        link(V.tensor_reduce(flag, same, AX.X, ALU.min))
        V.tensor_copy(ends[:, 0:heads], res[:, :, edge].rearrange("p h o -> p (h o)"))
        n += 1
        V.tensor_copy(ends[:, heads:2 * heads], flag.to_broadcast([parts, heads])).then_inc(asked, 1)
        dve.wait_ge(turned, n)
        if biggest and not back:
            link(V.tensor_scalar(rflag, ps[1][0:heads, 0:parts], NEG, -NEG, ALU.mult, ALU.add))
        else:
            link(V.tensor_copy(rflag, ps[1][0:heads, 0:parts]))
        link(V.memset(rsh, neutral))
        n += 1
        into = rsh[:, 0:parts - 1] if back else rsh[:, 1:parts]
        of = slice(1, parts) if back else slice(0, parts - 1)
        V.tensor_tensor_scan(into[:, way], rflag[:, of][:, way], ps[0][0:heads, of][:, way],
                             neutral, op0, op1).then_inc(asked, 1)
        dve.wait_ge(turned, n)
        link(V.tensor_copy(carry, ps[2][0:parts, 0:heads]))
        for h in range(heads):
            last = V.tensor_tensor_scan(res[:, h, way], cont[:, way], v[:, h, way], carry[:, h:h + 1], op0, op1)
        link(last)
    return n


def totals_tensor(nc, pe, asked, turned, n, ps, ident, small, rows, heads, parts):
    for _ in range(2):
        n += 1
        pe.wait_ge(asked, n)
        nc.tensor.transpose(ps[0][0:heads, 0:parts], small[0:parts, 0:heads], ident[0:parts, 0:parts])
        nc.tensor.transpose(ps[1][0:heads, 0:parts], small[0:parts, heads:2 * heads], ident[0:parts, 0:parts]).then_inc(turned, 1)
        n += 1
        pe.wait_ge(asked, n)
        nc.tensor.transpose(ps[2][0:parts, 0:heads], rows[0:heads, 1, 0:parts], ident[0:heads, 0:heads]).then_inc(turned, 1)
    return n


def sort_edges(nc, sb, sem, chain_of, ps, ident, ones, src, dst, etype,
               key_a, w_a, gat_a, put_a, rel_a, key_c, gat_c, own_c, put_c, up_c, down_c):
    f32, i32 = mybir.dt.float32, mybir.dt.int32
    ALU, AX = mybir.AluOpType, mybir.AxisListType
    S2 = 2 * FREE
    BIG = float(R * (1 << KSHIFT) + NODE_PAD)
    v = nc.vector
    with ExitStack() as st:
        def tb(name, shape, dt=f32):
            return st.enter_context(nc.sbuf_tensor(name, shape, dt))
        K = [tb(f"K{i}", [P, S2]) for i in range(2)]
        V = [tb(f"V{i}", [P, S2]) for i in range(2)]
        m, dv = tb("m", [P, FREE]), tb("dv", [P, FREE])
        raw = tb("raw", [P, 3, LOADF], i32)
        rawf = tb("rawf", [P, 3, LOADF])
        is_rel = tb("is_rel", [P, R, LOADF])
        cnt, pad, rkey = tb("cnt", [P, R]), tb("pad", [P, R]), tb("rkey", [P, R])
        cnti, ridx = tb("cnti", [P, R], i32), tb("ridx", [P, R], i32)
        pidx, pidxf = tb("pidx", [P, 1], i32), tb("pidxf", [P, 1])
        pbit, psgn, pstep = tb("pbit", [P, 8], i32), tb("psgn", [P, 8]), tb("pstep", [P, 8])
        edge_cols, shift_l, shift_r = tb("edge_cols", [P, 4]), tb("shift_l", [4, P]), tb("shift_r", [4, P])
        near = tb("near", [P, 8])
        up_a, down_a = tb("up_a", [P, FREE]), tb("down_a", [P, FREE])
        one_a, tot_a = tb("one_a", [P, 1, FREE]), tb("tot_a", [P, 1, FREE])
        seg_tmp, seg_small, seg_rows = tb("seg_tmp", [P, 1, FREE]), tb("seg_small", [P, 8]), tb("seg_rows", [4, 2, P])
        lead_a, lead_c = tb("lead_a", [P, TA]), tb("lead_c", [P, TC])
        keyi, node = tb("keyi", [P, TA], i32), tb("node", [P, TA])
        last_q, dump = tb("last_q", [P, 1]), tb("dump", [P, 1])
        t1, t2 = tb("t1", [P, TA]), tb("t2", [P, TA])
        relf = tb("relf", [1, TA])

        s_ld, s_io, s_v = sem("edges_loaded"), sem("numbered"), sem("sort_step")
        asked, turned, counted, summed = sem("turn_asked"), sem("turned"), sem("counted"), sem("summed")
        steps = list(sort_steps())
        turns = sum(what == "turn" for what, _ in steps)
        order = (sum(what == "stage" for what, _ in steps)) % 2
        with nc.Block() as block:
            @block.sync
            def _(sp):
                for i, a in enumerate((src, dst, etype)):
                    sp.dma_start(raw[0:LOADP, i, :], a.rearrange("(p f) -> p f", p=LOADP)).then_inc(s_ld, 16)

            @block.gpsimd
            def _(pool):
                pool.iota(pidx[:, :], pattern=[[0, 1]], base=0, channel_multiplier=1).then_inc(s_io, 1)
                pool.iota(ridx[:, :], pattern=[[1, R]], base=0, channel_multiplier=0).then_inc(s_io, 1)

            @block.vector
            def _(dve):
                link = chain_of(dve, s_v)
                link(v.memset(K[0][:, :], BIG))
                link(v.memset(V[0][:, :], 0.0))
                link(v.memset(cnt[:, :], 0.0))
                dve.wait_ge(s_io, 2)
                dve.wait_ge(s_ld, 48)
                link(v.tensor_copy(rawf[0:LOADP, :, :], raw[0:LOADP, :, :]))
                v.scalar_tensor_tensor(out=K[0][0:LOADP, 0:LOADF], in0=rawf[0:LOADP, 2, :], scalar=float(1 << KSHIFT),
                                       in1=rawf[0:LOADP, 1, :], op0=ALU.mult, op1=ALU.add)
                v.tensor_copy(K[0][0:LOADP, FREE:FREE + LOADF], rawf[0:LOADP, 0, :])
                v.tensor_copy(V[0][0:LOADP, 0:LOADF], rawf[0:LOADP, 0, :])
                link(v.tensor_copy(V[0][0:LOADP, FREE:FREE + LOADF], rawf[0:LOADP, 1, :]))
                for r in range(R):
                    last = v.tensor_scalar(is_rel[0:LOADP, r, :], rawf[0:LOADP, 2, :], float(r), None, ALU.is_equal)
                link(last)
                v.tensor_reduce(cnt[0:LOADP, :], is_rel[0:LOADP, :, :], AX.X, ALU.add).then_inc(counted, 1)
                dve.wait_ge(summed, 1)
                link(v.tensor_scalar(cnti[:, :], ps[0][:, 0:R], -1.0, float(1 << 20), ALU.mult, ALU.add))
                link(v.tensor_scalar(cnti[:, :], cnti[:, :], P - 1, None, ALU.bitwise_and))
                v.tensor_copy(pad[:, :], cnti[:, :])
                v.tensor_copy(pidxf[:, :], pidx[:, :])
                link(v.tensor_copy(rkey[:, :], ridx[:, :]))
                v.tensor_scalar(pad[:, :], pad[:, :], pidxf[:, 0:1], None, ALU.is_gt)
                link(v.tensor_scalar(rkey[:, :], rkey[:, :], float(1 << KSHIFT), float(NODE_PAD) - BIG, ALU.mult, ALU.add))
                link(v.tensor_tensor(rkey[:, :], rkey[:, :], pad[:, :], ALU.mult))
                link(v.tensor_scalar(K[0][:, LOADF:LOADF + R], rkey[:, :], BIG, None, ALU.add))
                for b in range(8):
                    last = v.tensor_scalar(pbit[:, b:b + 1], pidx[:, :], b, 1, ALU.logical_shift_right, ALU.bitwise_and)
                link(last)
                link(v.tensor_scalar(psgn[:, :], pbit[:, :], -2.0, 1.0, ALU.mult, ALU.add))
                link(v.tensor_tensor(pstep[:, 0:7], psgn[:, 0:7], psgn[:, 1:8], ALU.mult))
                kk = K[0][:, :].rearrange("p (b h k) -> p b h k", h=2, k=2)
                link(v.tensor_scalar(kk[:, :, 1, :], kk[:, :, 1, :], -1.0, None, ALU.mult))
                asks, cur = 0, 0
                for i, (what, k) in enumerate(steps):
                    ask = i + 1 < len(steps) and steps[i + 1][0] == "turn"
                    if what == "stage":
                        pair = [t[:, :].rearrange("p (b h k) -> p b h k", h=2, k=k) for t in (K[cur], V[cur], K[1 - cur], V[1 - cur])]
                        ka, kb = pair[0][:, :, 0, :], pair[0][:, :, 1, :]
                        va, vb = pair[1][:, :, 0, :], pair[1][:, :, 1, :]
                        mm = m[:, :].rearrange("p (b k) -> p b k", k=k)
                        dd = dv[:, :].rearrange("p (b k) -> p b k", k=k)
                        v.tensor_tensor(mm, ka, kb, ALU.is_gt)
                        v.tensor_tensor(dd, vb, va, ALU.subtract)
                        v.tensor_tensor(pair[2][:, :, 0, :], ka, kb, ALU.min)
                        link(v.tensor_tensor(pair[2][:, :, 1, :], ka, kb, ALU.max))
                        link(v.tensor_tensor(dd, dd, mm, ALU.mult))
                        v.tensor_tensor(pair[3][:, :, 0, :], va, dd, ALU.add)
                        last = v.tensor_tensor(pair[3][:, :, 1, :], vb, dd, ALU.subtract)
                        cur = 1 - cur
                    elif what == "turn":
                        dve.wait_ge(turned, asks)
                        for b in range(4):
                            last = v.tensor_copy((K, V)[b // 2][cur][:, (b % 2) * FREE:(b % 2 + 1) * FREE], ps[b][:, :])
                    elif k < 8:
                        q = 1 << k
                        kk = K[cur][:, :].rearrange("p (b k) -> p b k", k=4 * q)
                        last = v.tensor_scalar(kk[:, :, q:3 * q], kk[:, :, q:3 * q], -1.0, None, ALU.mult)
                    elif k == 8:
                        kk = K[cur][:, :].rearrange("p (b h k) -> p b h k", h=2, k=256)
                        link(v.tensor_scalar(kk[:, :, 1, :], kk[:, :, 1, :], -1.0, None, ALU.mult))
                        last = v.tensor_scalar(K[cur][:, :], K[cur][:, :], psgn[:, 0:1], None, ALU.mult)
                    else:
                        last = v.tensor_scalar(K[cur][:, :], K[cur][:, :], pstep[:, k - 9:k - 8], None, ALU.mult)
                    if ask:
                        asks += 1
                        last.then_inc(asked, 1)
                    else:
                        link(last)
                assert cur == order

                v.tensor_copy(edge_cols[:, 0:2], K[cur][:, 0::FREE])
                v.memset(shift_l[:, :], -1.0)
                v.memset(shift_r[:, :], -1.0)
                asks += 1
                v.tensor_copy(edge_cols[:, 2:4], K[cur][:, FREE - 1::FREE]).then_inc(asked, 1)
                dve.wait_ge(turned, asks)
                v.tensor_copy(shift_l[:, 0:P - 1], ps[0][0:4, 1:P])
                asks += 1
                v.tensor_copy(shift_r[:, 1:P], ps[0][0:4, 0:P - 1]).then_inc(asked, 1)
                dve.wait_ge(turned, asks)
                link(v.tensor_copy(near[:, :], ps[1][:, 0:8]))
                for s, (up, down) in enumerate(((up_a, down_a), (up_c, down_c))):
                    ks = K[cur][:, s * FREE:(s + 1) * FREE]
                    v.tensor_tensor(up[:, 1:FREE], ks[:, 1:FREE], ks[:, 0:FREE - 1], ALU.is_equal)
                    v.tensor_tensor(up[:, 0:1], ks[:, 0:1], near[:, 4 + 2 + s:4 + 3 + s], ALU.is_equal)
                    v.tensor_tensor(down[:, 0:FREE - 1], ks[:, 1:FREE], ks[:, 0:FREE - 1], ALU.is_equal)
                    last = v.tensor_tensor(down[:, FREE - 1:FREE], ks[:, FREE - 1:FREE], near[:, s:s + 1], ALU.is_equal)
                link(last)
                link(v.memset(one_a[:, :, :], 1.0))
                n = totals_vector(nc, dve, link, asked, turned, asks, ps, one_a[:, :, :], tot_a[:, :, :],
                                  up_a[:, :], down_a[:, :], seg_tmp, seg_small, seg_rows, 1, P, False)
                asks = n + 1
                v.reciprocal(tot_a[:, 0, :], tot_a[:, 0, :]).then_inc(asked, 1)
                dve.wait_ge(turned, asks)

                def tiles(of, n):
                    return of[:, :].rearrange("q (c p) -> q c p", c=U)[:, :, 0:n // U]

                def cols(of):
                    return of[:, :].rearrange("q (p c) -> q c p", c=U)

                v.tensor_copy(cols(key_a), tiles(ps[0], TA))
                v.tensor_copy(cols(gat_a), tiles(ps[1], TA))
                v.tensor_copy(cols(w_a), tiles(ps[2], TA))
                v.tensor_copy(cols(lead_a), tiles(ps[3], TA))
                v.tensor_copy(cols(key_c), tiles(ps[4], TC))
                v.tensor_copy(cols(gat_c), tiles(ps[5], TC))
                v.tensor_copy(cols(lead_c), tiles(ps[6], TC))
                v.tensor_scalar(last_q[:, :], pidxf[:, :], float(P - 1), None, ALU.is_equal)
                link(v.tensor_scalar(dump[:, :], pidxf[:, :], float(N), None, ALU.add))
                v.tensor_scalar(lead_a[:, :], lead_a[:, :], -1.0, 1.0, ALU.mult, ALU.add)
                v.tensor_scalar(lead_c[:, :], lead_c[:, :], -1.0, 1.0, ALU.mult, ALU.add)
                link(v.tensor_copy(keyi[:, :], key_a[:, :]))
                link(v.tensor_scalar(keyi[:, :], keyi[:, :], NODE_PAD, None, ALU.bitwise_and))
                link(v.tensor_copy(node[:, :], keyi[:, :]))
                for nd, lead, put, n in ((node, lead_a, put_a, TA), (key_c, lead_c, put_c, TC)):
                    link(v.tensor_scalar(t1[:, 0:n], nd[:, 0:n], float(N), None, ALU.is_lt))
                    if n == TA:
                        link(v.tensor_tensor(w_a[:, :], w_a[:, :], t1[:, :], ALU.mult))
                    link(v.scalar_tensor_tensor(out=t1[:, 0:n], in0=lead[:, :], scalar=last_q[:, 0:1], in1=t1[:, 0:n],
                                                op0=ALU.max, op1=ALU.mult))
                    link(v.scalar_tensor_tensor(out=t2[:, 0:n], in0=nd[:, 0:n], scalar=dump[:, 0:1], in1=t1[:, 0:n],
                                                op0=ALU.subtract, op1=ALU.mult))
                    link(v.tensor_scalar(t2[:, 0:n], t2[:, 0:n], dump[:, 0:1], None, ALU.add))
                    link(v.tensor_copy(put[:, :], t2[:, 0:n]))
                link(v.tensor_scalar(t1[:, 0:TC], key_c[:, :], float(N - 1), None, ALU.min))
                link(v.tensor_copy(own_c[:, :], t1[:, 0:TC]))
                link(v.tensor_copy(keyi[0:1, :], key_a[0:1, :]))
                link(v.tensor_scalar(keyi[0:1, :], keyi[0:1, :], KSHIFT, None, ALU.logical_shift_right))
                link(v.tensor_copy(relf[:, :], keyi[0:1, :]))
                link(v.tensor_scalar(relf[:, :], relf[:, :], float(R - 1), None, ALU.min))
                link(v.tensor_copy(rel_a[:, :], relf[:, :]))

            @block.tensor
            def _(pe):
                pe.wait_ge(counted, 1)
                nc.tensor.matmul(ps[0][:, 0:R], ones[:, :], cnt[:, :], start=True, stop=True).then_inc(summed, 1)
                asks, cur = 0, 0
                for what, _ in steps:
                    if what == "stage":
                        cur = 1 - cur
                    elif what == "turn":
                        asks += 1
                        pe.wait_ge(asked, asks)
                        for b in range(4):
                            for c in range(4):
                                at = (b % 2) * FREE + c * P
                                last = nc.tensor.transpose(ps[b][:, c * P:(c + 1) * P], (K, V)[b // 2][cur][:, at:at + P], ident[:, :])
                        last.then_inc(turned, 1)
                asks += 1
                pe.wait_ge(asked, asks)
                nc.tensor.transpose(ps[0][0:4, 0:P], edge_cols[:, :], ident[:, :]).then_inc(turned, 1)
                asks += 1
                pe.wait_ge(asked, asks)
                nc.tensor.transpose(ps[1][:, 0:4], shift_l[:, :], ident[0:4, 0:4])
                nc.tensor.transpose(ps[1][:, 4:8], shift_r[:, :], ident[0:4, 0:4]).then_inc(turned, 1)
                asks = totals_tensor(nc, pe, asked, turned, asks, ps, ident, seg_small, seg_rows, 1, P)
                asks += 1
                pe.wait_ge(asked, asks)
                for b, a in enumerate((K[cur][:, 0:FREE], V[cur][:, 0:FREE], tot_a[:, 0, :], down_a[:, :],
                                       K[cur][:, FREE:S2], V[cur][:, FREE:S2], down_c[:, :])):
                    for c in range(4):
                        last = nc.tensor.transpose(ps[b][:, c * P:(c + 1) * P], a[:, c * P:(c + 1) * P], ident[:, :])
                last.then_inc(turned, 1)


def pairs(eng, count, body):
    for half in range(2):
        body(0, half, False)
    with eng.Fori(1, count - 1) as j:
        for half in range(2):
            body(j, half, False)
    for half in range(2):
        body(count - 1, half, True)


def after(eng, s, value):
    if not isinstance(value, int) or value > 0:
        eng.wait_ge(s, value)


def following(j, half, last):
    if half == 0:
        return j, 1
    return None if last else (j + 1, 0)


def norm_vector(nc, dve, j, half, rows, x, stats, mv, rstd, nbias, aggr, var_ready, std_ready, norm_ready, passed):
    ALU = mybir.AluOpType
    v = nc.vector
    for r in range(rows):
        last = v.bn_stats(stats[:, r, :], x[half][:, r, :])
    last.then_inc(aggr[half], 1)
    dve.wait_ge(aggr[half], 2 * j + 1)
    dve.sem_inc(passed, 1)
    for r in range(rows):
        last = v.bn_aggr(mv[half][:, r, :], stats[:, r, :])
    last.then_inc(var_ready[half], 1)
    dve.wait_ge(std_ready[half], j + 1)
    v.reciprocal(rstd[half][:, :], rstd[half][:, :]).then_inc(aggr[half], 1)
    dve.wait_ge(aggr[half], 2 * j + 2)
    v.scalar_tensor_tensor(out=nbias[half][:, :], in0=mv[half][:, :, 0], scalar=-1.0, in1=rstd[half][:, :],
                           op0=ALU.mult, op1=ALU.mult).then_inc(norm_ready[half], 1)


def norm_scalar(nc, act, j, half, rows, x, hid, mv, rstd, nbias, epsc, var_ready, std_ready, norm_ready, hid_ready):
    ACT = mybir.ActivationFunctionType
    act.wait_ge(var_ready[half], j + 1)
    nc.scalar.activation(rstd[half][:, :], mv[half][:, :, 1], ACT.Sqrt, bias=epsc[:, :]).then_inc(std_ready[half], 1)
    act.wait_ge(norm_ready[half], j + 1)
    for r in range(rows):
        last = nc.scalar.activation(hid[half][:, r, :], x[half][:, r, :], ACT.Relu,
                                    bias=nbias[half][:, r:r + 1], scale=rstd[half][:, r:r + 1])
    last.then_inc(hid_ready[half], 1)


def dense_pass(nc, sem, ps, ident, inp, res, outp, root, bias_bc, epsc, nr):
    f32 = mybir.dt.float32
    ALU, ACT = mybir.AluOpType, mybir.ActivationFunctionType
    v = nc.vector
    nm = f"d{nr}_"
    with ExitStack() as st:
        def two(name, shape, dt=f32):
            return [st.enter_context(nc.sbuf_tensor(f"{nm}{name}{i}", shape, dt)) for i in range(2)]

        def sems(name):
            return [sem(f"{nm}{name}{i}") for i in range(2)]
        xin, yo, hidT = two("xin", [P, RB, D]), two("yo", [P, RB, D]), two("hidT", [P, RB, D])
        rin = two("rin", [P, RB, D]) if nr == 2 else None
        hid = two("hid", [P, RB, D]) if nr == 1 else None
        stats = st.enter_context(nc.sbuf_tensor(nm + "stats", [P, RB, 6], f32))
        bsum = st.enter_context(nc.sbuf_tensor(nm + "bsum", [P, D], f32))
        mv, rstd, nbias = two("mv", [P, RB, 2]), two("rstd", [P, RB]), two("nbias", [P, RB])
        loaded, stored, res_ready, y_ready = sems("loaded"), sems("stored"), sems("res"), sems("y")
        aggr, var_ready, std_ready, norm_ready = sems("aggr"), sems("var"), sems("std"), sems("norm")
        passed, started = sem(nm + "passed"), sem(nm + "started")
        hid_ready, turned, hidT_ready, prod = sems("hid"), sems("turned"), sems("hidT"), sems("prod")
        bias_ready = sem(nm + "bias")
        halves = NB // 2
        per = 16 * nr

        def rows_of(t, j, half, last):
            at = N - BLK if last and half else (j * 2 + half) * BLK
            return t[bass.ds(at, BLK), :].rearrange("(p r) d -> p r d", r=RB)

        with nc.Block() as block:
            @block.sync
            def _(sp):
                def body(j, half, last):
                    if nr == 1:
                        after(sp, hid_ready[half], j)
                    else:
                        after(sp, turned[half], 2 * j)
                    sp.dma_start(xin[half][:, :, :], rows_of(inp, j, half, last)).then_inc(loaded[half], 16)
                    if nr == 2:
                        after(sp, y_ready[half], j)
                        sp.dma_start(rin[half][:, :, :], rows_of(res, j, half, last)).then_inc(loaded[half], 16)
                pairs(sp, halves, body)

            @block.gpsimd
            def _(pool):
                def body(j, half, last):
                    if nr == 2:
                        pool.wait_ge(loaded[half], per * (j + 1))
                        nc.gpsimd.tensor_tensor(rin[half][:, :, :], rin[half][:, :, :],
                                                bsum[:, :].rearrange("p (o d) -> p o d", o=1).to_broadcast([P, RB, D]),
                                                ALU.add).then_inc(res_ready[half], 1)
                    pool.wait_ge(y_ready[half], j + 1)
                    if last and half:
                        pool.wait_ge(stored[0], 16 * halves)
                    pool.dma_start(rows_of(outp, j, half, last), yo[half][:, :, :]).then_inc(stored[half], 16)
                if nr == 2:
                    nc.gpsimd.tensor_tensor(bsum[:, :], bias_bc[:, 1, :], bias_bc[:, 2, :], ALU.add).then_inc(bias_ready, 1)
                    pool.wait_ge(bias_ready, 1)
                pairs(pool, halves, body)
                for half in range(2):
                    pool.wait_ge(stored[half], 16 * halves)

            @block.vector
            def _(dve):
                def norm(j, half):
                    dve.wait_ge(loaded[half], per * (j + 1))
                    norm_vector(nc, dve, j, half, RB, xin, stats, mv, rstd, nbias, aggr, var_ready, std_ready, norm_ready, passed)

                def body(j, half, last):
                    nxt = following(j, half, last)
                    if nr == 1 and nxt:
                        norm(*nxt)
                    if nr == 2:
                        dve.wait_ge(res_ready[half], j + 1)
                    after(dve, stored[half], 16 * j)
                    for k in range(2):
                        dve.wait_ge(prod[half], 2 * j + k + 1)
                        sl = slice(k * 4, k * 4 + 4)
                        pv = ps[4 + 2 * half + k][:, :].rearrange("p (r d) -> p r d", r=4)
                        other = bias_bc[:, 0:1, :].to_broadcast([P, 4, D]) if nr == 1 else rin[half][:, sl, :]
                        add = v.tensor_tensor(yo[half][:, sl, :], pv, other, ALU.add)
                    add.then_inc(y_ready[half], 1)
                if nr == 1:
                    norm(0, 0)
                pairs(dve, halves, body)

            @block.scalar
            def _(act):
                def norm(j, half):
                    after(act, turned[half], 2 * j)
                    norm_scalar(nc, act, j, half, RB, xin, hid, mv, rstd, nbias, epsc, var_ready, std_ready, norm_ready, hid_ready)

                def body(j, half, last):
                    nxt = following(j, half, last)
                    if nr == 1 and nxt:
                        norm(*nxt)
                    after(act, prod[half], 2 * j)
                    for k in range(2):
                        act.wait_ge(turned[half], 2 * j + k + 1)
                        nc.scalar.activation(hidT[half][:, k * 4:k * 4 + 4, :],
                                             ps[2 * half + k][:, :].rearrange("p (r d) -> p r d", r=4),
                                             ACT.Copy if nr == 1 else ACT.Relu).then_inc(hidT_ready[half], 1)
                if nr == 1:
                    norm(0, 0)
                pairs(act, halves, body)

            @block.tensor
            def _(pe):
                def turn(j, half):
                    if nr == 1:
                        pe.wait_ge(hid_ready[half], j + 1)
                    else:
                        pe.wait_ge(loaded[half], per * (j + 1))
                    after(pe, hidT_ready[half], 2 * j)
                    of = (hid if nr == 1 else xin)[half]
                    for k in range(2):
                        for r in range(4):
                            t = nc.tensor.transpose(ps[2 * half + k][:, r * D:(r + 1) * D], of[:, k * 4 + r, :], ident[:, :])
                        t.then_inc(turned[half], 1)

                def body(j, half, last):
                    nxt = following(j, half, last)
                    if nxt:
                        turn(*nxt)
                    after(pe, y_ready[half], j)
                    for k in range(2):
                        pe.wait_ge(hidT_ready[half], 2 * j + k + 1)
                        for r in range(4):
                            mm = nc.tensor.matmul(ps[4 + 2 * half + k][:, r * D:(r + 1) * D], hidT[half][:, k * 4 + r, :],
                                                  root, start=True, stop=True)
                        mm.then_inc(prod[half], 1)
                turn(0, 0)
                pairs(pe, halves, body)


def rgcn_edges(nc, sem, ps, ident, rows, target, W, layer, epsc, key_a, w_a, gat_a, put_a, rel_a):
    f32, i32 = mybir.dt.float32, mybir.dt.int32
    ALU, ACT = mybir.AluOpType, mybir.ActivationFunctionType
    v = nc.vector
    nm = f"e{layer}_"
    with ExitStack() as st:
        def two(name, shape, dt=f32):
            return [st.enter_context(nc.sbuf_tensor(f"{nm}{name}{i}", shape, dt)) for i in range(2)]

        def sems(name):
            return [sem(f"{nm}{name}{i}") for i in range(2)]
        xin, hid, Sw, CT, msg = (two(n, [P, U, D]) for n in ("xin", "hid", "Sw", "CT", "msg"))
        gidx, pidx, kw = two("gidx", [P, U], i32), two("pidx", [P, U], i32), two("kw", [P, 2, U])
        stats = st.enter_context(nc.sbuf_tensor(nm + "stats", [P, U, 6], f32))
        mv, rstd, nbias = two("mv", [P, U, 2]), two("rstd", [P, U]), two("nbias", [P, U])
        gidx_ready, gathered, put, kw_ready = sems("gidx"), sems("gathered"), sems("put"), sems("kw")
        pidx_ready, keyT, S_ready, hid_ready = sems("pidx"), sems("keyT"), sems("S"), sems("hid")
        cprod, CT_ready, mprod, msg_ready = sems("cprod"), sems("CT"), sems("mprod"), sems("msg")
        aggr, var_ready, std_ready, norm_ready = sems("aggr"), sems("var"), sems("std"), sems("norm")
        passed, started = sem(nm + "passed"), sem(nm + "started")
        halves = GA // 2
        ln = layer == 0

        with nc.Block() as block:
            @block.gpsimd
            def _(pool):
                def gather(j, half, u):
                    if u == 0:
                        pool.wait_ge(gidx_ready[half], j + 1)
                        after(pool, hid_ready[half], j)
                        pool.sem_inc(started, 1)
                    nc.gpsimd.indirect_dma_start(xin[half][:, u, :], None, rows,
                                                 bass.IndirectOffsetOnAxis(ap=gidx[half][:, u:u + 1], axis=0)).then_inc(gathered[half], 16)

                def body(j, half, last):
                    nxt = following(j, half, last)
                    for u in range(U):
                        if nxt:
                            gather(*nxt, u)
                        if u == 0:
                            pool.wait_ge(msg_ready[half], j + 1)
                            pool.wait_ge(pidx_ready[half], j + 1)
                        if u:
                            pool.wait_ge(put[half], 64 * j + 16 * u)
                        else:
                            after(pool, put[1 - half], 64 * (j + half))
                        pool.sem_inc(started, 1)
                        nc.gpsimd.indirect_dma_start(target, bass.IndirectOffsetOnAxis(ap=pidx[half][:, u:u + 1], axis=0),
                                                     msg[half][:, u, :], None, compute_op=ALU.add).then_inc(put[half], 16)
                for u in range(U):
                    gather(0, 0, u)
                pairs(pool, halves, body)
                for half in range(2):
                    pool.wait_ge(put[half], 64 * halves)

            @block.vector
            def _(dve):
                def gather_list(j, half):
                    after(dve, gathered[half], 64 * j)
                    v.tensor_copy(gidx[half][:, :], gat_a[:, bass.ds((j * 2 + half) * U, U)]).then_inc(gidx_ready[half], 1)

                def prepare(j, half):
                    at = bass.ds((j * 2 + half) * U, U)
                    after(dve, S_ready[half], j)
                    v.tensor_copy(kw[half][:, 0, :], key_a[:, at])
                    v.tensor_copy(kw[half][:, 1, :], w_a[:, at]).then_inc(kw_ready[half], 1)
                    dve.wait_ge(gathered[half], 64 * (j + 1))
                    if ln:
                        norm_vector(nc, dve, j, half, U, xin, stats, mv, rstd, nbias, aggr, var_ready, std_ready, norm_ready, passed)
                    after(dve, cprod[half], j)
                    dve.wait_ge(keyT[half], j + 1)
                    dve.wait_ge(kw_ready[half], j + 1)
                    for u in range(U):
                        eq = v.tensor_scalar(Sw[half][:, u, :], ps[half][:, u * P:(u + 1) * P], kw[half][:, 0, u:u + 1],
                                             kw[half][:, 1, u:u + 1], ALU.is_equal, ALU.mult)
                    eq.then_inc(S_ready[half], 1)
                    after(dve, put[half], 64 * j)
                    v.tensor_copy(pidx[half][:, :], put_a[:, at]).then_inc(pidx_ready[half], 1)

                def body(j, half, last):
                    nxt = following(j, half, last)
                    if not last:
                        gather_list(j + 1, half)
                    if nxt:
                        prepare(*nxt)
                gather_list(0, 0)
                gather_list(0, 1)
                prepare(0, 0)
                pairs(dve, halves, body)

            @block.scalar
            def _(act):
                def norm(j, half):
                    after(act, cprod[half], j)
                    if ln:
                        norm_scalar(nc, act, j, half, U, xin, hid, mv, rstd, nbias, epsc, var_ready, std_ready, norm_ready, hid_ready)
                    else:
                        act.wait_ge(gathered[half], 64 * (j + 1))
                        nc.scalar.activation(hid[half][:, :, :], xin[half][:, :, :], ACT.Relu).then_inc(hid_ready[half], 1)

                def body(j, half, last):
                    act.wait_ge(cprod[half], j + 1)
                    after(act, mprod[half], j)
                    nc.scalar.activation(CT[half][:, :, :], ps[2 + half][:, :].rearrange("p (u d) -> p u d", u=U),
                                         ACT.Copy).then_inc(CT_ready[half], 1)
                    act.wait_ge(mprod[half], j + 1)
                    after(act, put[half], 64 * j)
                    nc.scalar.activation(msg[half][:, :, :], ps[4 + half][:, :].rearrange("p (u d) -> p u d", u=U),
                                         ACT.Copy).then_inc(msg_ready[half], 1)
                    nxt = following(j, half, last)
                    if nxt:
                        norm(*nxt)
                norm(0, 0)
                pairs(act, halves, body)

            @block.tensor
            def _(pe):
                def keys(j, half):
                    pe.wait_ge(kw_ready[half], j + 1)
                    after(pe, S_ready[half], j)
                    for u in range(U):
                        t = nc.tensor.transpose(ps[half][:, u * P:(u + 1) * P],
                                                kw[half][:, 0, u:u + 1].to_broadcast([P, P]), ident[:, :])
                    t.then_inc(keyT[half], 1)

                def body(j, half, last):
                    rel = [pe.value_load(rel_a[0:1, bass.ds((j * 2 + half) * U + u, 1)], min_val=0, max_val=R - 1) for u in range(U)]
                    pe.wait_ge(hid_ready[half], j + 1)
                    pe.wait_ge(S_ready[half], j + 1)
                    after(pe, CT_ready[half], j)
                    for u in range(U):
                        mm = nc.tensor.matmul(ps[2 + half][:, u * P:(u + 1) * P], hid[half][:, u, :], Sw[half][:, u, :],
                                              start=True, stop=True)
                    mm.then_inc(cprod[half], 1)
                    pe.wait_ge(CT_ready[half], j + 1)
                    after(pe, msg_ready[half], j)
                    for u in range(U):
                        mm = nc.tensor.matmul(ps[4 + half][:, u * P:(u + 1) * P], CT[half][:, u, :],
                                              W[:, layer, bass.ds(rel[u] * D, D)], start=True, stop=True)
                    mm.then_inc(mprod[half], 1)
                    nxt = following(j, half, last)
                    if nxt:
                        keys(*nxt)
                keys(0, 0)
                pairs(pe, halves, body)


def gat_scores(nc, sem, ps, ident, rows, g_tiles, wg, bias_bc, epsc, gat_c, own_c, score):
    f32, i32 = mybir.dt.float32, mybir.dt.int32
    ALU, ACT = mybir.AluOpType, mybir.ActivationFunctionType
    v = nc.vector
    nm = "s_"
    U2 = 2 * U
    with ExitStack() as st:
        def two(name, shape, dt=f32):
            return [st.enter_context(nc.sbuf_tensor(f"{nm}{name}{i}", shape, dt)) for i in range(2)]

        def sems(name):
            return [sem(f"{nm}{name}{i}") for i in range(2)]
        xin, hid, hidT = (two(n, [P, U2, D]) for n in ("xin", "hid", "hidT"))
        gout = two("gout", [P, U, D])
        gidx = two("gidx", [P, 2, U], i32)
        stats = st.enter_context(nc.sbuf_tensor(nm + "stats", [P, U2, 6], f32))
        mv, rstd, nbias = two("mv", [P, U2, 2]), two("rstd", [P, U2]), two("nbias", [P, U2])
        gidx_ready, gathered, bias_off, hid_ready = sems("gidx"), sems("gathered"), sems("bias_off"), sems("hid")
        turned, hidT_ready, prod, g_ready = sems("turned"), sems("hidT"), sems("prod"), sems("g")
        score_ready, stored = sems("score"), sems("stored")
        aggr, var_ready, std_ready, norm_ready = sems("aggr"), sems("var"), sems("std"), sems("norm")
        passed, started = sem(nm + "passed"), sem(nm + "started")
        halves = GC // 2

        with nc.Block() as block:
            @block.gpsimd
            def _(pool):
                def body(j, half, last):
                    pool.wait_ge(gidx_ready[half], j + 1)
                    after(pool, hid_ready[half], j)
                    pool.sem_inc(started, 1)
                    for side in range(2):
                        for u in range(U):
                            nc.gpsimd.indirect_dma_start(
                                xin[half][:, side * U + u, :], None, rows,
                                bass.IndirectOffsetOnAxis(ap=gidx[half][:, side, u:u + 1], axis=0)).then_inc(gathered[half], 16)
                pairs(pool, halves, body)

            @block.sync
            def _(sp):
                def body(j, half, last):
                    sp.wait_ge(g_ready[half], j + 1)
                    sp.dma_start(g_tiles[bass.ds(j * 2 + half, 1), :, :, :].rearrange("o q u d -> (o q) u d"),
                                 gout[half][:, :, :]).then_inc(stored[half], 16)
                pairs(sp, halves, body)
                for half in range(2):
                    sp.wait_ge(stored[half], 16 * halves)

            @block.vector
            def _(dve):
                def gather_list(j, half):
                    at = bass.ds((j * 2 + half) * U, U)
                    after(dve, gathered[half], 128 * j)
                    v.tensor_copy(gidx[half][:, 0, :], gat_c[:, at])
                    v.tensor_copy(gidx[half][:, 1, :], own_c[:, at]).then_inc(gidx_ready[half], 1)

                def prepare(j, half):
                    dve.wait_ge(gathered[half], 128 * (j + 1))
                    v.tensor_tensor(xin[half][:, :, :], xin[half][:, :, :], bias_bc[:, 2:3, :].to_broadcast([P, U2, D]),
                                    ALU.subtract).then_inc(bias_off[half], 1)
                    dve.wait_ge(bias_off[half], j + 1)
                    norm_vector(nc, dve, j, half, U2, xin, stats, mv, rstd, nbias, aggr, var_ready, std_ready, norm_ready, passed)

                def body(j, half, last):
                    if not last:
                        gather_list(j + 1, half)
                    nxt = following(j, half, last)
                    if nxt:
                        prepare(*nxt)
                    dve.wait_ge(prod[half], j + 1)
                    v.tensor_copy(score[:, :, bass.ds((j * 2 + half) * U, U)],
                                  ps[6 + half][:, 0:U * H].rearrange("p (u h) -> p h u", u=U)).then_inc(score_ready[half], 1)
                gather_list(0, 0)
                gather_list(0, 1)
                prepare(0, 0)
                pairs(dve, halves, body)

            @block.scalar
            def _(act):
                def norm(j, half):
                    after(act, turned[half], 2 * j)
                    norm_scalar(nc, act, j, half, U2, xin, hid, mv, rstd, nbias, epsc, var_ready, std_ready, norm_ready, hid_ready)

                def body(j, half, last):
                    after(act, prod[half], j)
                    for k in range(2):
                        act.wait_ge(turned[half], 2 * j + k + 1)
                        nc.scalar.activation(hidT[half][:, k * U:(k + 1) * U, :],
                                             ps[2 * half + k][:, :].rearrange("p (u d) -> p u d", u=U),
                                             ACT.Copy).then_inc(hidT_ready[half], 1)
                    act.wait_ge(prod[half], j + 1)
                    after(act, stored[half], 16 * j)
                    nc.scalar.activation(gout[half][:, :, :], ps[4 + half][:, :].rearrange("p (u d) -> p u d", u=U),
                                         ACT.Copy).then_inc(g_ready[half], 1)
                    nxt = following(j, half, last)
                    if nxt:
                        norm(*nxt)
                norm(0, 0)
                pairs(act, halves, body)

            @block.tensor
            def _(pe):
                def body(j, half, last):
                    pe.wait_ge(hid_ready[half], j + 1)
                    after(pe, hidT_ready[half], 2 * j)
                    for k in range(2):
                        for u in range(U):
                            t = nc.tensor.transpose(ps[2 * half + k][:, u * P:(u + 1) * P], hid[half][:, k * U + u, :], ident[:, :])
                        t.then_inc(turned[half], 1)
                    pe.wait_ge(hidT_ready[half], 2 * j + 2)
                    after(pe, g_ready[half], j)
                    after(pe, score_ready[half], j)
                    for u in range(U):
                        nc.tensor.matmul(ps[4 + half][:, u * D:(u + 1) * D], hidT[half][:, u, :], wg[:, 0:D], start=True, stop=True)
                        nc.tensor.matmul(ps[6 + half][:, u * H:(u + 1) * H], hidT[half][:, u, :], wg[:, D:D + H],
                                         start=True, stop=False)
                        mm = nc.tensor.matmul(ps[6 + half][:, u * H:(u + 1) * H], hidT[half][:, U + u, :], wg[:, D + H:D + 2 * H],
                                              start=False, stop=True)
                    mm.then_inc(prod[half], 1)
                pairs(pe, halves, body)


def gat_softmax(nc, sem, chain_of, ps, ident, up_c, down_c, score):
    f32 = mybir.dt.float32
    ALU, ACT = mybir.AluOpType, mybir.ActivationFunctionType
    v = nc.vector
    PC = TC // U
    step, asked, turned, shifted, exped = sem("sm_step"), sem("sm_asked"), sem("sm_turned"), sem("sm_shifted"), sem("sm_exp")
    with ExitStack() as st:
        def tb(name, shape):
            return st.enter_context(nc.sbuf_tensor("sm_" + name, shape, f32))
        a, b, res = tb("a", [PC, H, FREE]), tb("b", [PC, H, FREE]), tb("res", [PC, H, FREE])
        tmp, small, rows = tb("tmp", [P, 1, FREE]), tb("small", [P, 4 * H]), tb("rows", [H, 2, P])
        up, down = up_c[0:PC, :], down_c[0:PC, :]
        with nc.Block() as block:
            @block.vector
            def _(dve):
                link = chain_of(dve, step)
                dve.wait_ge(turned, 1)
                for h in range(H):
                    cp = v.tensor_copy(a[:, h, :], ps[h][0:PC, :])
                link(cp)
                link(v.scalar_tensor_tensor(out=a[:, :, :], in0=a[:, :, :], scalar=SLOPE, in1=a[:, :, :],
                                            op0=ALU.mult, op1=ALU.max))
                link(v.tensor_copy(b[:, :, :], a[:, :, :]))
                n = totals_vector(nc, dve, link, asked, turned, 1, ps, b[:, :, :], res[:, :, :], up, down,
                                  tmp, small, rows, H, PC, True)
                v.tensor_tensor(a[:, :, :], a[:, :, :], res[:, :, :], ALU.subtract).then_inc(shifted, 1)
                dve.wait_ge(exped, 1)
                link(v.tensor_copy(b[:, :, :], a[:, :, :]))
                n = totals_vector(nc, dve, link, asked, turned, n, ps, b[:, :, :], res[:, :, :], up, down,
                                  tmp, small, rows, H, PC, False)
                link(v.tensor_scalar(res[:, :, :], res[:, :, :], TINY, None, ALU.add))
                link(v.reciprocal(res[:, :, :], res[:, :, :]))
                n += 1
                v.tensor_tensor(a[:, :, :], a[:, :, :], res[:, :, :], ALU.mult).then_inc(asked, 1)
                dve.wait_ge(turned, n)
                for h in range(H):
                    cp = v.tensor_copy(score[:, h, :].rearrange("q (p c) -> q c p", c=U),
                                       ps[4 + h][:, 0:TC].rearrange("q (c p) -> q c p", c=U))
                link(cp)

            @block.scalar
            def _(act):
                act.wait_ge(shifted, 1)
                nc.scalar.activation(a[:, :, :], a[:, :, :], ACT.Exp).then_inc(exped, 1)

            @block.tensor
            def _(pe):
                for h in range(H):
                    for c in range(U):
                        t = nc.tensor.transpose(ps[h][0:PC, c * P:(c + 1) * P], score[:, h, c::U], ident[:, :])
                t.then_inc(turned, 1)
                n = totals_tensor(nc, pe, asked, turned, 0, ps, ident, small, rows, H, PC)
                n = totals_tensor(nc, pe, asked, turned, n, ps, ident, small, rows, H, PC)
                pe.wait_ge(asked, n + 1)
                for h in range(H):
                    for c in range(U):
                        t = nc.tensor.transpose(ps[4 + h][:, c * PC:(c + 1) * PC], a[:, h, c * P:(c + 1) * P], ident[0:PC, 0:PC])
                t.then_inc(turned, 1)


def gat_edges(nc, sem, ps, ident, g_tiles, target, score, key_c, put_c):
    f32, i32 = mybir.dt.float32, mybir.dt.int32
    ALU, ACT = mybir.AluOpType, mybir.ActivationFunctionType
    v = nc.vector
    nm = "g_"
    with ExitStack() as st:
        def two(name, shape, dt=f32):
            return [st.enter_context(nc.sbuf_tensor(f"{nm}{name}{i}", shape, dt)) for i in range(2)]

        def sems(name):
            return [sem(f"{nm}{name}{i}") for i in range(2)]
        gin, gs, S, msg = (two(n, [P, U, D]) for n in ("gin", "gs", "S", "msg"))
        pidx, kcol, co = two("pidx", [P, U], i32), two("kcol", [P, U]), two("co", [P, U, H])
        loaded, slots, keyT, S_ready, scaled = sems("loaded"), sems("slots"), sems("keyT"), sems("S"), sems("scaled")
        pidx_ready, prod, msg_ready, put = sems("pidx"), sems("prod"), sems("msg"), sems("put")
        started = sem(nm + "started")
        halves = GC // 2

        with nc.Block() as block:
            @block.sync
            def _(sp):
                def body(j, half, last):
                    after(sp, scaled[half], j)
                    sp.dma_start(gin[half][:, :, :], g_tiles[bass.ds(j * 2 + half, 1), :, :, :].rearrange("o q u d -> (o q) u d")
                                 ).then_inc(loaded[half], 16)
                pairs(sp, halves, body)

            @block.gpsimd
            def _(pool):
                def body(j, half, last):
                    pool.wait_ge(msg_ready[half], j + 1)
                    pool.wait_ge(pidx_ready[half], j + 1)
                    for u in range(U):
                        if u:
                            pool.wait_ge(put[half], 64 * j + 16 * u)
                        else:
                            after(pool, put[1 - half], 64 * (j + half))
                        pool.sem_inc(started, 1)
                        nc.gpsimd.indirect_dma_start(target, bass.IndirectOffsetOnAxis(ap=pidx[half][:, u:u + 1], axis=0),
                                                     msg[half][:, u, :], None, compute_op=ALU.add).then_inc(put[half], 16)
                pairs(pool, halves, body)
                for half in range(2):
                    pool.wait_ge(put[half], 64 * halves)

            @block.vector
            def _(dve):
                def body(j, half, last):
                    at = bass.ds((j * 2 + half) * U, U)
                    v.tensor_copy(kcol[half][:, :], key_c[:, at])
                    v.tensor_copy(co[half][:, :, :], score[:, :, at].rearrange("p h u -> p u h")).then_inc(slots[half], 1)
                    dve.wait_ge(slots[half], j + 1)
                    dve.wait_ge(loaded[half], 16 * (j + 1))
                    after(dve, prod[half], j)
                    v.tensor_tensor(gs[half][:, :, :].rearrange("p u (h f) -> p (u h) f", h=H),
                                    gin[half][:, :, :].rearrange("p u (h f) -> p (u h) f", h=H),
                                    co[half][:, :, :].rearrange("p u (h o) -> p (u h) o", o=1).to_broadcast([P, U * H, F]),
                                    ALU.mult).then_inc(scaled[half], 1)
                    dve.wait_ge(keyT[half], j + 1)
                    for u in range(U):
                        eq = v.tensor_scalar(S[half][:, u, :], ps[half][:, u * P:(u + 1) * P], kcol[half][:, u:u + 1],
                                             None, ALU.is_equal)
                    eq.then_inc(S_ready[half], 1)
                    after(dve, put[half], 64 * j)
                    v.tensor_copy(pidx[half][:, :], put_c[:, at]).then_inc(pidx_ready[half], 1)
                pairs(dve, halves, body)

            @block.scalar
            def _(act):
                def body(j, half, last):
                    act.wait_ge(prod[half], j + 1)
                    after(act, put[half], 64 * j)
                    nc.scalar.activation(msg[half][:, :, :], ps[2 + half][:, :].rearrange("p (u d) -> p u d", u=U),
                                         ACT.Copy).then_inc(msg_ready[half], 1)
                pairs(act, halves, body)

            @block.tensor
            def _(pe):
                def body(j, half, last):
                    pe.wait_ge(slots[half], j + 1)
                    after(pe, S_ready[half], j)
                    for u in range(U):
                        t = nc.tensor.transpose(ps[half][:, u * P:(u + 1) * P], kcol[half][:, u:u + 1].to_broadcast([P, P]), ident[:, :])
                    t.then_inc(keyT[half], 1)
                    pe.wait_ge(S_ready[half], j + 1)
                    pe.wait_ge(scaled[half], j + 1)
                    after(pe, msg_ready[half], j)
                    for u in range(U):
                        mm = nc.tensor.matmul(ps[2 + half][:, u * D:(u + 1) * D], S[half][:, u, :], gs[half][:, u, :],
                                              start=True, stop=True)
                    mm.then_inc(prod[half], 1)
                pairs(pe, halves, body)


_INS = ["x", "src", "dst", "edge_type_8", "L0_gnn_weights", "L0_gnn_roots", "L0_gnn_biases",
        "L1_gnn_weight", "L1_gnn_att", "L1_gnn_bias"]


def kernel(**inputs):
    import numpy as _np
    import concourse.bacc as _bacc
    from concourse import mybir as _mybir
    from concourse.bass_utils import run_bass_kernel_spmd as _run

    nc = _bacc.Bacc("TRN2", target_bir_lowering=False, num_devices=1)
    arrays, args = {}, []
    for name in _INS:
        a = _np.ascontiguousarray(inputs[name])
        arrays[f"in_{name}"] = a
        args.append(nc.dram_tensor(f"in_{name}", a.shape, _mybir.dt.from_np(a.dtype), kind="ExternalInput").ap())
    args.append(nc.dram_tensor("out_0", (N + P, D), _mybir.dt.float32, kind="ExternalOutput").ap())
    gnn_program(nc, *args)
    r = _run(nc, [arrays], core_ids=[0])
    return r.results[0]["out_0"][:N]
```

```python
import concourse.bass as bass
from concourse import mybir
from contextlib import ExitStack, contextmanager

N = 100000
E = 50000
D = 128
R = 8
H = 4
F = D // H
P = 128
SLOPE = 0.2
EPS = 1e-5
TINY = 1e-16
NEG = 1e38

KSHIFT = 17
NODE_PAD = (1 << KSHIFT) - 1
LOGN = 16
FREE = (1 << LOGN) // P
LOADP, LOADF = 125, 400
U = 4
GRP = U * P
GA = (E + R * (GRP - 1)) // GRP
TA = GA * U
GC = -(-E // GRP)
TC = GC * U
RING = 4
DUMP = RING * U * P
DW = -(-TA // (RING * U)) * RING * U
RB = 8
NB = 98
BLK = P * RB


def gnn_program(nc, x, src, dst, etype, w_rel, roots, biases, w_gat, att, b_gat, out):
    f32, i32 = mybir.dt.float32, mybir.dt.int32
    ALU, ACT, AX = mybir.AluOpType, mybir.ActivationFunctionType, mybir.AxisListType

    y_dram = nc.dram_tensor("y_scratch", (N + DUMP, D), f32, kind="Internal").ap()
    g_dram = nc.dram_tensor("g_scratch", (TC * P, D), f32, kind="Internal").ap()
    g_tiles = g_dram.rearrange("(g u q) d -> g q u d", u=U, q=P)

    ctx = ExitStack()
    with ctx:
        def sb(name, shape, dt=f32):
            return ctx.enter_context(nc.sbuf_tensor(name, shape, dt))

        def sem(name):
            return ctx.enter_context(nc.semaphore(name))

        def chain_of(eng, s, start=0):
            count = [start]

            def link(ins):
                count[0] += 1
                ins.then_inc(s, 1)
                eng.wait_ge(s, count[0])
            return link

        ident = sb("ident", [P, P])
        ones = sb("ones", [P, P])
        epsc = sb("epsc", [P, 1])
        W = sb("W", [P, 2, R * D])
        root = sb("root", [P, 2, D])
        bias_bc = sb("bias_bc", [P, 3, D])
        wg = sb("wg", [P, D + 2 * H])
        att_bc = sb("att_bc", [P, H, 2 * F])
        key_a = sb("key_a", [P, TA])
        w_a = sb("w_a", [P, TA])
        gat_a = sb("gat_a", [P, TA])
        put_a = sb("put_a", [P, TA])
        rel_a = sb("rel_a", [1, GA], i32)
        key_c = sb("key_c", [P, TC])
        gat_c = sb("gat_c", [P, TC])
        own_c = sb("own_c", [P, TC])
        put_c = sb("put_c", [P, TC])
        score = sb("score", [P, H, TC])

        ps = [ctx.enter_context(nc.psum_tensor(f"ps{i}", [P, 512], f32)) for i in range(8)]
        up_c, down_c = sb("up_c", [P, FREE]), sb("down_c", [P, FREE])

        s_w, s_id, s_dump, s_set = sem("weights_loaded"), sem("constants"), sem("dump_cleared"), sem("setup_step")
        with (nc.sbuf_tensor("wa_tmp", [P, H, 2, F], f32) as wa_tmp, nc.sbuf_tensor("zeros", [P, DUMP // P, D], f32) as zeros,
              nc.Block() as block):
            @block.scalar
            def _(act):
                act.wait_ge(s_id, 4)
                act.dma_start(y_dram[N:N + DUMP, :].rearrange("(p r) d -> p r d", p=P), zeros[:, :, :]).then_inc(s_dump, 16)
                act.dma_start(out[N:N + DUMP, :].rearrange("(p r) d -> p r d", p=P), zeros[:, :, :]).then_inc(s_dump, 16)
                act.wait_ge(s_dump, 32)

            @block.sync
            def _(sp):
                for l in range(2):
                    for r in range(R):
                        sp.dma_start(W[:, l, r * D:(r + 1) * D], w_rel[l, r, :, :]).then_inc(s_w, 16)
                    sp.dma_start(root[:, l, :], roots[l, :, :]).then_inc(s_w, 16)
                sp.dma_start(wg[:, 0:D], w_gat).then_inc(s_w, 16)
                sp.dma_start(bias_bc[:, 0:2, :], biases.rearrange("(a l) d -> a l d", a=1).to_broadcast([P, 2, D])).then_inc(s_w, 16)
                sp.dma_start(bias_bc[:, 2, :], b_gat.rearrange("(a d) -> a d", a=1).to_broadcast([P, D])).then_inc(s_w, 16)
                sp.dma_start(att_bc[:, :, :], att.to_broadcast([P, H, 2 * F])).then_inc(s_w, 16)
                sp.wait_ge(s_w, 16 * (2 * (R + 1) + 4))

            @block.gpsimd
            def _(pool):
                pool.memset(ident[:, :], 0.0).then_inc(s_id, 1)
                pool.memset(ones[:, :], 1.0).then_inc(s_id, 1)
                pool.memset(epsc[:, :], EPS).then_inc(s_id, 1)
                pool.memset(zeros[:, :, :], 0.0).then_inc(s_id, 1)
                pool.wait_ge(s_id, 4)
                pool.affine_select(out=ident[:, :], in_=ident[:, :], compare_op=ALU.not_equal, fill=1.0,
                                   base=0, pattern=[[-1, P]], channel_multiplier=1).then_inc(s_id, 1)

            @block.vector
            def _(dve):
                link = chain_of(dve, s_set)
                dve.wait_ge(s_w, 16 * (2 * (R + 1) + 4))
                wv = wg[:, 0:D].rearrange("p (h f) -> p h f", h=H)
                for side, col in ((1, 0), (0, 1)):
                    link(nc.vector.tensor_tensor(wa_tmp[:, :, side, :], wv, att_bc[:, :, side * F:(side + 1) * F], ALU.mult))
                    link(nc.vector.tensor_reduce(wg[:, D + col * H:D + (col + 1) * H], wa_tmp[:, :, side, :], AX.X, ALU.add))

        sort_edges(nc, sb, sem, chain_of, ps, ident, ones, src, dst, etype,
                   key_a, w_a, gat_a, put_a, rel_a, key_c, gat_c, own_c, put_c, up_c, down_c)

        with phase_semaphores(nc, ctx) as phase:
            dense_pass(nc, phase, ps, ident, x, None, y_dram, root[:, 0, :], bias_bc, epsc, 1)
        with phase_semaphores(nc, ctx) as phase:
            rgcn_edges(nc, phase, ps, ident, x, y_dram, W, 0, epsc, key_a, w_a, gat_a, put_a, rel_a)
        with phase_semaphores(nc, ctx) as phase:
            dense_pass(nc, phase, ps, ident, y_dram, x, out, root[:, 1, :], bias_bc, epsc, 2)
        with phase_semaphores(nc, ctx) as phase:
            rgcn_edges(nc, phase, ps, ident, y_dram, out, W, 1, epsc, key_a, w_a, gat_a, put_a, rel_a)
        with phase_semaphores(nc, ctx) as phase:
            gat_scores(nc, phase, ps, ident, out, g_tiles, wg, bias_bc, epsc, gat_c, own_c, score)
        with phase_semaphores(nc, ctx) as phase:
            gat_softmax(nc, phase, chain_of, ps, ident, up_c, down_c, score)
        with phase_semaphores(nc, ctx) as phase:
            gat_edges(nc, phase, ps, ident, g_tiles, out, score, key_c, put_c)


@contextmanager
def phase_semaphores(nc, keep):
    with ExitStack() as held:
        mine = []

        def sem(name):
            if name[:-1].endswith(("gathered", "stored", "put")):
                return keep.enter_context(nc.semaphore(name))
            mine.append(held.enter_context(nc.semaphore(name)))
            return mine[-1]
        yield sem
        with nc.Block() as block:
            @block.gpsimd
            def _(pool):
                for s in mine:
                    pool.sem_clear(s)


def sort_steps():
    for phase in range(1, LOGN + 1):
        if phase >= 10:
            yield "turn", 0
            for bit in range(phase - 1, 8, -1):
                yield "stage", 1 << (bit - 9)
            yield "turn", 0
        for bit in range(min(phase, 9) - 1, -1, -1):
            yield "stage", 1 << bit
        if phase < LOGN:
            yield "flip", phase


def totals_vector(nc, dve, link, asked, turned, n, ps, v, res, up, down, tmp, small, rows, heads, parts, biggest):
    f32 = mybir.dt.float32
    ALU, AX = mybir.AluOpType, mybir.AxisListType
    V = nc.vector
    ends, carry = small[0:parts, 0:2 * heads], small[0:parts, 2 * heads:3 * heads]
    flag = small[0:parts, 3 * heads:3 * heads + 1]
    rflag, rsh = rows[0:heads, 0, 0:parts], rows[0:heads, 1, :]
    for back in (0, 1):
        if back:
            link(V.tensor_scalar(tmp[0:parts, 0, :], down, -1.0, 1.0, ALU.mult, ALU.add))
            link(V.tensor_tensor(v, res, tmp[0:parts, 0:1, :].to_broadcast([parts, heads, FREE]), ALU.mult))
            cont, op0, op1, neutral, same = down, ALU.mult, ALU.add, 0.0, down
        elif biggest:
            link(V.tensor_scalar(tmp[0:parts, 0, :], up, NEG, -NEG, ALU.mult, ALU.add))
            cont, op0, op1, neutral, same = tmp[0:parts, 0, :], ALU.add, ALU.max, -NEG, up
        else:
            cont, op0, op1, neutral, same = up, ALU.mult, ALU.add, 0.0, up
        way = slice(None, None, -1) if back else slice(None)
        edge = slice(0, 1) if back else slice(FREE - 1, FREE)
        for h in range(heads):
            last = V.tensor_tensor_scan(res[:, h, way], cont[:, way], v[:, h, way], neutral, op0, op1)
        link(last)
        link(V.tensor_reduce(flag, same, AX.X, ALU.min))
        V.tensor_copy(ends[:, 0:heads], res[:, :, edge].rearrange("p h o -> p (h o)"))
        n += 1
        V.tensor_copy(ends[:, heads:2 * heads], flag.to_broadcast([parts, heads])).then_inc(asked, 1)
        dve.wait_ge(turned, n)
        if biggest and not back:
            link(V.tensor_scalar(rflag, ps[1][0:heads, 0:parts], NEG, -NEG, ALU.mult, ALU.add))
        else:
            link(V.tensor_copy(rflag, ps[1][0:heads, 0:parts]))
        link(V.memset(rsh, neutral))
        n += 1
        into = rsh[:, 0:parts - 1] if back else rsh[:, 1:parts]
        of = slice(1, parts) if back else slice(0, parts - 1)
        V.tensor_tensor_scan(into[:, way], rflag[:, of][:, way], ps[0][0:heads, of][:, way],
                             neutral, op0, op1).then_inc(asked, 1)
        dve.wait_ge(turned, n)
        link(V.tensor_copy(carry, ps[2][0:parts, 0:heads]))
        for h in range(heads):
            last = V.tensor_tensor_scan(res[:, h, way], cont[:, way], v[:, h, way], carry[:, h:h + 1], op0, op1)
        link(last)
    return n


def totals_tensor(nc, pe, asked, turned, n, ps, ident, small, rows, heads, parts):
    for _ in range(2):
        n += 1
        pe.wait_ge(asked, n)
        nc.tensor.transpose(ps[0][0:heads, 0:parts], small[0:parts, 0:heads], ident[0:parts, 0:parts])
        nc.tensor.transpose(ps[1][0:heads, 0:parts], small[0:parts, heads:2 * heads], ident[0:parts, 0:parts]).then_inc(turned, 1)
        n += 1
        pe.wait_ge(asked, n)
        nc.tensor.transpose(ps[2][0:parts, 0:heads], rows[0:heads, 1, 0:parts], ident[0:heads, 0:heads]).then_inc(turned, 1)
    return n


def sort_edges(nc, sb, sem, chain_of, ps, ident, ones, src, dst, etype,
               key_a, w_a, gat_a, put_a, rel_a, key_c, gat_c, own_c, put_c, up_c, down_c):
    f32, i32 = mybir.dt.float32, mybir.dt.int32
    ALU, AX = mybir.AluOpType, mybir.AxisListType
    S2 = 2 * FREE
    BIG = float(R * (1 << KSHIFT) + NODE_PAD)
    v = nc.vector
    with ExitStack() as st:
        def tb(name, shape, dt=f32):
            return st.enter_context(nc.sbuf_tensor(name, shape, dt))
        K = [tb(f"K{i}", [P, S2]) for i in range(2)]
        V = [tb(f"V{i}", [P, S2]) for i in range(2)]
        m, dv = tb("m", [P, FREE]), tb("dv", [P, FREE])
        raw = tb("raw", [P, 3, LOADF], i32)
        rawf = tb("rawf", [P, 3, LOADF])
        is_rel = tb("is_rel", [P, R, LOADF])
        cnt, rkey = tb("cnt", [P, R]), tb("rkey", [P, R])
        pad, pkey = tb("pad", [P, R, U]), tb("pkey", [P, R, U])
        cnti, ridx = tb("cnti", [P, R], i32), tb("ridx", [P, R], i32)
        pidx, pidxf = tb("pidx", [P, 1], i32), tb("pidxf", [P, 1])
        pbit, psgn, pstep = tb("pbit", [P, 8], i32), tb("psgn", [P, 8]), tb("pstep", [P, 8])
        edge_cols, shift_l, shift_r = tb("edge_cols", [P, 4]), tb("shift_l", [4, P]), tb("shift_r", [4, P])
        near = tb("near", [P, 8])
        up_a, down_a = tb("up_a", [P, FREE]), tb("down_a", [P, FREE])
        one_a, tot_a = tb("one_a", [P, 1, FREE]), tb("tot_a", [P, 1, FREE])
        seg_tmp, seg_small, seg_rows = tb("seg_tmp", [P, 1, FREE]), tb("seg_small", [P, 8]), tb("seg_rows", [4, 2, P])
        lead_a, lead_c = tb("lead_a", [P, TA]), tb("lead_c", [P, TC])
        keyi, node = tb("keyi", [P, TA], i32), tb("node", [P, TA])
        dump, dumpi = tb("dump", [P, DW]), tb("dumpi", [P, DW], i32)
        t1, t2 = tb("t1", [P, TA]), tb("t2", [P, TA])
        relf, reli = tb("relf", [1, GA]), tb("reli", [1, GA], i32)

        s_ld, s_io, s_v = sem("edges_loaded"), sem("numbered"), sem("sort_step")
        asked, turned, counted, summed = sem("turn_asked"), sem("turned"), sem("counted"), sem("summed")
        steps = list(sort_steps())
        turns = sum(what == "turn" for what, _ in steps)
        order = (sum(what == "stage" for what, _ in steps)) % 2
        with nc.Block() as block:
            @block.sync
            def _(sp):
                for i, a in enumerate((src, dst, etype)):
                    sp.dma_start(raw[0:LOADP, i, :], a.rearrange("(p f) -> p f", p=LOADP)).then_inc(s_ld, 16)

            @block.gpsimd
            def _(pool):
                pool.iota(pidx[:, :], pattern=[[0, 1]], base=0, channel_multiplier=1).then_inc(s_io, 1)
                pool.iota(ridx[:, :], pattern=[[1, R]], base=0, channel_multiplier=0).then_inc(s_io, 1)
                pool.iota(dumpi[:, :], pattern=[[0, DW // (RING * U)], [P, RING * U]], base=N, channel_multiplier=1).then_inc(s_io, 1)

            @block.vector
            def _(dve):
                link = chain_of(dve, s_v)
                link(v.memset(K[0][:, :], BIG))
                link(v.memset(V[0][:, :], 0.0))
                link(v.memset(cnt[:, :], 0.0))
                dve.wait_ge(s_io, 3)
                dve.wait_ge(s_ld, 48)
                link(v.tensor_copy(rawf[0:LOADP, :, :], raw[0:LOADP, :, :]))
                v.scalar_tensor_tensor(out=K[0][0:LOADP, 0:LOADF], in0=rawf[0:LOADP, 2, :], scalar=float(1 << KSHIFT),
                                       in1=rawf[0:LOADP, 1, :], op0=ALU.mult, op1=ALU.add)
                v.tensor_copy(K[0][0:LOADP, FREE:FREE + LOADF], rawf[0:LOADP, 0, :])
                v.tensor_copy(V[0][0:LOADP, 0:LOADF], rawf[0:LOADP, 0, :])
                link(v.tensor_copy(V[0][0:LOADP, FREE:FREE + LOADF], rawf[0:LOADP, 1, :]))
                for r in range(R):
                    last = v.tensor_scalar(is_rel[0:LOADP, r, :], rawf[0:LOADP, 2, :], float(r), None, ALU.is_equal)
                link(last)
                v.tensor_reduce(cnt[0:LOADP, :], is_rel[0:LOADP, :, :], AX.X, ALU.add).then_inc(counted, 1)
                dve.wait_ge(summed, 1)
                link(v.tensor_scalar(cnti[:, :], ps[0][:, 0:R], -1.0, float(1 << 20), ALU.mult, ALU.add))
                link(v.tensor_scalar(cnti[:, :], cnti[:, :], GRP - 1, None, ALU.bitwise_and))
                v.tensor_copy(pidxf[:, :], pidx[:, :])
                for c in range(U):
                    wanted = v.tensor_scalar(pad[:, :, c], cnti[:, :], float(c * P), None, ALU.subtract)
                link(wanted)
                link(v.tensor_copy(rkey[:, :], ridx[:, :]))
                v.tensor_scalar(pad[:, :, :], pad[:, :, :], pidxf[:, 0:1], None, ALU.is_gt)
                link(v.tensor_scalar(rkey[:, :], rkey[:, :], float(1 << KSHIFT), float(NODE_PAD) - BIG, ALU.mult, ALU.add))
                link(v.tensor_tensor(pkey[:, :, :], pad[:, :, :], rkey[:, :].rearrange("p (r o) -> p r o", o=1).to_broadcast([P, R, U]),
                                     ALU.mult))
                link(v.tensor_scalar(K[0][:, LOADF:LOADF + R * U], pkey[:, :, :].rearrange("p r c -> p (r c)"), BIG, None, ALU.add))
                for b in range(8):
                    last = v.tensor_scalar(pbit[:, b:b + 1], pidx[:, :], b, 1, ALU.logical_shift_right, ALU.bitwise_and)
                link(last)
                link(v.tensor_scalar(psgn[:, :], pbit[:, :], -2.0, 1.0, ALU.mult, ALU.add))
                link(v.tensor_tensor(pstep[:, 0:7], psgn[:, 0:7], psgn[:, 1:8], ALU.mult))
                kk = K[0][:, :].rearrange("p (b h k) -> p b h k", h=2, k=2)
                link(v.tensor_scalar(kk[:, :, 1, :], kk[:, :, 1, :], -1.0, None, ALU.mult))
                asks, cur = 0, 0
                for i, (what, k) in enumerate(steps):
                    ask = i + 1 < len(steps) and steps[i + 1][0] == "turn"
                    if what == "stage":
                        pair = [t[:, :].rearrange("p (b h k) -> p b h k", h=2, k=k) for t in (K[cur], V[cur], K[1 - cur], V[1 - cur])]
                        ka, kb = pair[0][:, :, 0, :], pair[0][:, :, 1, :]
                        va, vb = pair[1][:, :, 0, :], pair[1][:, :, 1, :]
                        mm = m[:, :].rearrange("p (b k) -> p b k", k=k)
                        dd = dv[:, :].rearrange("p (b k) -> p b k", k=k)
                        v.tensor_tensor(mm, ka, kb, ALU.is_gt)
                        v.tensor_tensor(dd, vb, va, ALU.subtract)
                        v.tensor_tensor(pair[2][:, :, 0, :], ka, kb, ALU.min)
                        link(v.tensor_tensor(pair[2][:, :, 1, :], ka, kb, ALU.max))
                        link(v.tensor_tensor(dd, dd, mm, ALU.mult))
                        v.tensor_tensor(pair[3][:, :, 0, :], va, dd, ALU.add)
                        last = v.tensor_tensor(pair[3][:, :, 1, :], vb, dd, ALU.subtract)
                        cur = 1 - cur
                    elif what == "turn":
                        dve.wait_ge(turned, asks)
                        for b in range(4):
                            last = v.tensor_copy((K, V)[b // 2][cur][:, (b % 2) * FREE:(b % 2 + 1) * FREE], ps[b][:, :])
                    elif k < 8:
                        q = 1 << k
                        kk = K[cur][:, :].rearrange("p (b k) -> p b k", k=4 * q)
                        last = v.tensor_scalar(kk[:, :, q:3 * q], kk[:, :, q:3 * q], -1.0, None, ALU.mult)
                    elif k == 8:
                        kk = K[cur][:, :].rearrange("p (b h k) -> p b h k", h=2, k=256)
                        link(v.tensor_scalar(kk[:, :, 1, :], kk[:, :, 1, :], -1.0, None, ALU.mult))
                        last = v.tensor_scalar(K[cur][:, :], K[cur][:, :], psgn[:, 0:1], None, ALU.mult)
                    else:
                        last = v.tensor_scalar(K[cur][:, :], K[cur][:, :], pstep[:, k - 9:k - 8], None, ALU.mult)
                    if ask:
                        asks += 1
                        last.then_inc(asked, 1)
                    else:
                        link(last)
                assert cur == order

                v.tensor_copy(edge_cols[:, 0:2], K[cur][:, 0::FREE])
                v.memset(shift_l[:, :], -1.0)
                v.memset(shift_r[:, :], -1.0)
                asks += 1
                v.tensor_copy(edge_cols[:, 2:4], K[cur][:, FREE - 1::FREE]).then_inc(asked, 1)
                dve.wait_ge(turned, asks)
                v.tensor_copy(shift_l[:, 0:P - 1], ps[0][0:4, 1:P])
                asks += 1
                v.tensor_copy(shift_r[:, 1:P], ps[0][0:4, 0:P - 1]).then_inc(asked, 1)
                dve.wait_ge(turned, asks)
                link(v.tensor_copy(near[:, :], ps[1][:, 0:8]))
                for s, (up, down) in enumerate(((up_a, down_a), (up_c, down_c))):
                    ks = K[cur][:, s * FREE:(s + 1) * FREE]
                    v.tensor_tensor(up[:, 1:FREE], ks[:, 1:FREE], ks[:, 0:FREE - 1], ALU.is_equal)
                    v.tensor_tensor(up[:, 0:1], ks[:, 0:1], near[:, 4 + 2 + s:4 + 3 + s], ALU.is_equal)
                    v.tensor_tensor(down[:, 0:FREE - 1], ks[:, 1:FREE], ks[:, 0:FREE - 1], ALU.is_equal)
                    last = v.tensor_tensor(down[:, FREE - 1:FREE], ks[:, FREE - 1:FREE], near[:, s:s + 1], ALU.is_equal)
                link(last)
                link(v.memset(one_a[:, :, :], 1.0))
                n = totals_vector(nc, dve, link, asked, turned, asks, ps, one_a[:, :, :], tot_a[:, :, :],
                                  up_a[:, :], down_a[:, :], seg_tmp, seg_small, seg_rows, 1, P, False)
                v.memset(down_a[:, FREE - 1:FREE], 0.0)
                asks = n + 1
                v.reciprocal(tot_a[:, 0, :], tot_a[:, 0, :]).then_inc(asked, 1)
                dve.wait_ge(turned, asks)

                def tiles(of, n):
                    return of[:, :].rearrange("q (c p) -> q c p", c=U)[:, :, 0:n // U]

                def cols(of):
                    return of[:, :].rearrange("q (p c) -> q c p", c=U)

                v.tensor_copy(cols(key_a), tiles(ps[0], TA))
                v.tensor_copy(cols(gat_a), tiles(ps[1], TA))
                v.tensor_copy(cols(w_a), tiles(ps[2], TA))
                v.tensor_copy(cols(lead_a), tiles(ps[3], TA))
                v.tensor_copy(cols(key_c), tiles(ps[4], TC))
                v.tensor_copy(cols(gat_c), tiles(ps[5], TC))
                v.tensor_copy(cols(lead_c), tiles(ps[6], TC))
                link(v.tensor_copy(dump[:, :], dumpi[:, :]))
                v.tensor_scalar(lead_a[:, :], lead_a[:, :], -1.0, 1.0, ALU.mult, ALU.add)
                v.tensor_scalar(lead_c[:, :], lead_c[:, :], -1.0, 1.0, ALU.mult, ALU.add)
                link(v.tensor_copy(keyi[:, :], key_a[:, :]))
                link(v.tensor_scalar(keyi[:, :], keyi[:, :], NODE_PAD, None, ALU.bitwise_and))
                link(v.tensor_copy(node[:, :], keyi[:, :]))
                for nd, lead, put, n in ((node, lead_a, put_a, TA), (key_c, lead_c, put_c, TC)):
                    link(v.tensor_scalar(t1[:, 0:n], nd[:, 0:n], float(N), None, ALU.is_lt))
                    if n == TA:
                        link(v.tensor_tensor(w_a[:, :], w_a[:, :], t1[:, :], ALU.mult))
                    link(v.tensor_tensor(t1[:, 0:n], lead[:, :], t1[:, 0:n], ALU.mult))
                    link(v.tensor_tensor(t2[:, 0:n], nd[:, 0:n], dump[:, 0:n], ALU.subtract))
                    link(v.tensor_tensor(t2[:, 0:n], t2[:, 0:n], t1[:, 0:n], ALU.mult))
                    link(v.tensor_tensor(t2[:, 0:n], t2[:, 0:n], dump[:, 0:n], ALU.add))
                    link(v.tensor_copy(put[:, :], t2[:, 0:n]))
                link(v.tensor_scalar(t1[:, 0:TC], key_c[:, :], float(N - 1), None, ALU.min))
                link(v.tensor_copy(own_c[:, :], t1[:, 0:TC]))
                link(v.tensor_copy(reli[:, :], key_a[0:1, 0::U]))
                link(v.tensor_scalar(reli[:, :], reli[:, :], KSHIFT, None, ALU.logical_shift_right))
                link(v.tensor_copy(relf[:, :], reli[:, :]))
                link(v.tensor_scalar(relf[:, :], relf[:, :], float(R - 1), None, ALU.min))
                link(v.tensor_copy(rel_a[:, :], relf[:, :]))

            @block.tensor
            def _(pe):
                pe.wait_ge(counted, 1)
                nc.tensor.matmul(ps[0][:, 0:R], ones[:, :], cnt[:, :], start=True, stop=True).then_inc(summed, 1)
                asks, cur = 0, 0
                for what, _ in steps:
                    if what == "stage":
                        cur = 1 - cur
                    elif what == "turn":
                        asks += 1
                        pe.wait_ge(asked, asks)
                        for b in range(4):
                            for c in range(4):
                                at = (b % 2) * FREE + c * P
                                last = nc.tensor.transpose(ps[b][:, c * P:(c + 1) * P], (K, V)[b // 2][cur][:, at:at + P], ident[:, :])
                        last.then_inc(turned, 1)
                asks += 1
                pe.wait_ge(asked, asks)
                nc.tensor.transpose(ps[0][0:4, 0:P], edge_cols[:, :], ident[:, :]).then_inc(turned, 1)
                asks += 1
                pe.wait_ge(asked, asks)
                nc.tensor.transpose(ps[1][:, 0:4], shift_l[:, :], ident[0:4, 0:4])
                nc.tensor.transpose(ps[1][:, 4:8], shift_r[:, :], ident[0:4, 0:4]).then_inc(turned, 1)
                asks = totals_tensor(nc, pe, asked, turned, asks, ps, ident, seg_small, seg_rows, 1, P)
                asks += 1
                pe.wait_ge(asked, asks)
                for b, a in enumerate((K[cur][:, 0:FREE], V[cur][:, 0:FREE], tot_a[:, 0, :], down_a[:, :],
                                       K[cur][:, FREE:S2], V[cur][:, FREE:S2], down_c[:, :])):
                    for c in range(4):
                        last = nc.tensor.transpose(ps[b][:, c * P:(c + 1) * P], a[:, c * P:(c + 1) * P], ident[:, :])
                last.then_inc(turned, 1)


def pipeline(eng, count, *stages):
    def step(j, s):
        for lag, stage in stages:
            jj, ss = (j, s - lag) if s >= lag else (j - 1, s - lag + RING)
            b = jj * RING + ss if isinstance(jj, int) else None
            if b is None or 0 <= b < count:
                stage(jj, ss, b)

    for k in range(2 * RING):
        step(k // RING, k % RING)
    with eng.Fori(2, count // RING) as j:
        for s in range(RING):
            step(j, s)
    for k in range(count // RING * RING, count + max(lag for lag, _ in stages)):
        step(k // RING, k % RING)


def after(eng, s, value):
    if not isinstance(value, int) or value > 0:
        eng.wait_ge(s, value)


def two_before(sems, j, s, per=1):
    return (sems[s - 2], per * (j + 1)) if s >= 2 else (sems[s + 2], per * j)


def one_before(sems, j, s, per=1):
    return (sems[s - 1], per * (j + 1)) if s >= 1 else (sems[RING - 1], per * j)


def at_block(j, s):
    return j * RING + s


def norm_stats(nc, dve, j, s, rows, x, stats, mv, aggr, passed, var_ready):
    v = nc.vector
    after(dve, var_ready[s], j)
    for r in range(rows):
        last = v.bn_stats(stats[s][:, r, :], x[s][:, r, :])
    last.then_inc(aggr[s], 1)
    dve.wait_ge(aggr[s], 2 * j + 1)
    dve.sem_inc(passed, 1)
    for r in range(rows):
        last = v.bn_aggr(mv[s][:, r, :], stats[s][:, r, :])
    last.then_inc(var_ready[s], 1)


def norm_factors(nc, dve, j, s, mv, rstd, nbias, aggr, std_ready, norm_ready):
    ALU = mybir.AluOpType
    v = nc.vector
    dve.wait_ge(std_ready[s], j + 1)
    v.reciprocal(rstd[s][:, :], rstd[s][:, :]).then_inc(aggr[s], 1)
    dve.wait_ge(aggr[s], 2 * j + 2)
    v.scalar_tensor_tensor(out=nbias[s][:, :], in0=mv[s][:, :, 0], scalar=-1.0, in1=rstd[s][:, :],
                           op0=ALU.mult, op1=ALU.mult).then_inc(norm_ready[s], 1)


def norm_std(nc, act, j, s, mv, rstd, epsc, var_ready, std_ready):
    act.wait_ge(var_ready[s], j + 1)
    nc.scalar.activation(rstd[s][:, :], mv[s][:, :, 1], mybir.ActivationFunctionType.Sqrt,
                         bias=epsc[:, :]).then_inc(std_ready[s], 1)


def norm_rows(nc, act, j, s, rows, x, hid, rstd, nbias, norm_ready, hid_ready):
    act.wait_ge(norm_ready[s], j + 1)
    for r in range(rows):
        last = nc.scalar.activation(hid[s][:, r, :], x[s][:, r, :], mybir.ActivationFunctionType.Relu,
                                    bias=nbias[s][:, r:r + 1], scale=rstd[s][:, r:r + 1])
    last.then_inc(hid_ready[s], 1)


def dense_pass(nc, sem, ps, ident, inp, res, outp, root, bias_bc, epsc, nr):
    f32 = mybir.dt.float32
    ALU, ACT = mybir.AluOpType, mybir.ActivationFunctionType
    v = nc.vector
    nm = f"d{nr}_"
    with ExitStack() as st:
        def ring(name, shape, n=RING):
            return [st.enter_context(nc.sbuf_tensor(f"{nm}{name}{i}", shape, f32)) for i in range(n)]

        def sems(name):
            return [sem(f"{nm}{name}{i}") for i in range(RING)]
        xin, yo = ring("xin", [P, RB, D]), ring("yo", [P, RB, D])
        hidT = ring("hidT", [P, RB, D], 2)
        rin = ring("rin", [P, RB, D]) if nr == 2 else None
        hid = ring("hid", [P, RB, D]) if nr == 1 else None
        stats, bsum = ring("stats", [P, RB, 6]), ring("bsum", [P, D], 1)[0]
        mv, rstd, nbias = ring("mv", [P, RB, 2]), ring("rstd", [P, RB]), ring("nbias", [P, RB])
        loaded, stored, y_ready = sems("loaded"), sems("stored"), sems("y")
        turned, hidT_ready, prod = sems("turned"), sems("hidT"), sems("prod")
        if nr == 1:
            aggr, var_ready, std_ready, norm_ready, hid_ready = (sems("aggr"), sems("var"), sems("std"), sems("norm"),
                                                                 sems("hid"))
        else:
            res_ready = sems("res")
        passed, bias_ready = sem(nm + "passed"), sem(nm + "bias")
        per = 16 * nr

        def rows_of(t, j, s, b):
            at = N - BLK if b == NB - 1 else at_block(j, s) * BLK
            return t[bass.ds(at, BLK), :].rearrange("(p r) d -> p r d", r=RB)

        with nc.Block() as block:
            @block.sync
            def _(sp):
                def load(j, s, b):
                    if nr == 1:
                        after(sp, hid_ready[s], j)
                    else:
                        after(sp, turned[s], 2 * j)
                    sp.dma_start(xin[s][:, :, :], rows_of(inp, j, s, b)).then_inc(loaded[s], 16)
                    if nr == 2:
                        after(sp, prod[s], 2 * j)
                        sp.dma_start(rin[s][:, :, :], rows_of(res, j, s, b)).then_inc(loaded[s], 16)
                pipeline(sp, NB, (0, load))

            @block.gpsimd
            def _(pool):
                def bias(j, s, b):
                    pool.wait_ge(loaded[s], per * (j + 1))
                    nc.gpsimd.tensor_tensor(rin[s][:, :, :], rin[s][:, :, :],
                                            bsum[:, :].rearrange("p (o d) -> p o d", o=1).to_broadcast([P, RB, D]),
                                            ALU.add).then_inc(res_ready[s], 1)

                def store(j, s, b):
                    pool.wait_ge(y_ready[s], nr * (j + 1))
                    if b == NB - 1:
                        pool.wait_ge(*one_before(stored, j, s, 16))
                    pool.dma_start(rows_of(outp, j, s, b), yo[s][:, :, :]).then_inc(stored[s], 16)
                if nr == 2:
                    nc.gpsimd.tensor_tensor(bsum[:, :], bias_bc[:, 1, :], bias_bc[:, 2, :], ALU.add).then_inc(bias_ready, 1)
                    pool.wait_ge(bias_ready, 1)
                    pipeline(pool, NB, (0, bias), (2, store))
                else:
                    pipeline(pool, NB, (0, store))
                for s in range(RING):
                    pool.wait_ge(stored[s], 16 * len(range(s, NB, RING)))

            @block.vector
            def _(dve):
                def stat(j, s, b):
                    dve.wait_ge(loaded[s], per * (j + 1))
                    norm_stats(nc, dve, j, s, RB, xin, stats, mv, aggr, passed, var_ready)

                def factors(j, s, b):
                    norm_factors(nc, dve, j, s, mv, rstd, nbias, aggr, std_ready, norm_ready)

                def add(j, s, b):
                    after(dve, stored[s], 16 * j)
                    for k in range(2):
                        dve.wait_ge(prod[s], 2 * j + k + 1)
                        t = v.tensor_tensor(yo[s][:, k * 4:k * 4 + 4, :],
                                            ps[4 + 2 * (s % 2) + k][:, :].rearrange("p (r d) -> p r d", r=4),
                                            bias_bc[:, 0:1, :].to_broadcast([P, 4, D]), ALU.add)
                    t.then_inc(y_ready[s], 1)
                if nr == 1:
                    pipeline(dve, NB, (0, stat), (1, factors), (4, add))

            @block.scalar
            def _(act):
                def std(j, s, b):
                    norm_std(nc, act, j, s, mv, rstd, epsc, var_ready, std_ready)

                def norm(j, s, b):
                    after(act, turned[s], 2 * j)
                    norm_rows(nc, act, j, s, RB, xin, hid, rstd, nbias, norm_ready, hid_ready)

                def copy_T(j, s, b):
                    after(act, *two_before(prod, j, s, 2))
                    for k in range(2):
                        act.wait_ge(turned[s], 2 * j + k + 1)
                        nc.scalar.activation(hidT[s % 2][:, k * 4:k * 4 + 4, :],
                                             ps[2 * (s % 2) + k][:, :].rearrange("p (r d) -> p r d", r=4),
                                             ACT.Copy if nr == 1 else ACT.Relu).then_inc(hidT_ready[s], 1)

                def copy_y(j, s, b):
                    after(act, stored[s], 16 * j)
                    for k in range(2):
                        act.wait_ge(prod[s], 2 * j + k + 1)
                        nc.scalar.activation(yo[s][:, k * 4:k * 4 + 4, :],
                                             ps[4 + 2 * (s % 2) + k][:, :].rearrange("p (r d) -> p r d", r=4),
                                             ACT.Copy).then_inc(y_ready[s], 1)
                if nr == 1:
                    pipeline(act, NB, (2, norm), (3, copy_T), (0, std))
                else:
                    pipeline(act, NB, (0, copy_T), (1, copy_y))

            @block.tensor
            def _(pe):
                def turn(j, s, b):
                    if nr == 1:
                        pe.wait_ge(hid_ready[s], j + 1)
                    else:
                        pe.wait_ge(loaded[s], per * (j + 1))
                    after(pe, *two_before(hidT_ready, j, s, 2))
                    of = (hid if nr == 1 else xin)[s]
                    for k in range(2):
                        for r in range(4):
                            t = nc.tensor.transpose(ps[2 * (s % 2) + k][:, r * D:(r + 1) * D], of[:, k * 4 + r, :], ident[:, :])
                        t.then_inc(turned[s], 1)

                def products(j, s, b):
                    after(pe, *two_before(y_ready, j, s, nr))
                    if nr == 2:
                        pe.wait_ge(res_ready[s], j + 1)
                    for k in range(2):
                        pe.wait_ge(hidT_ready[s], 2 * j + k + 1)
                        bank = ps[4 + 2 * (s % 2) + k]
                        for r in range(4):
                            mm = nc.tensor.matmul(bank[:, r * D:(r + 1) * D], hidT[s % 2][:, k * 4 + r, :], root,
                                                  start=True, stop=nr == 1)
                            if nr == 2:
                                mm = nc.tensor.matmul(bank[:, r * D:(r + 1) * D], ident[:, :], rin[s][:, k * 4 + r, :],
                                                      start=False, stop=True)
                        mm.then_inc(prod[s], 1)
                pipeline(pe, NB, (0, turn), (1, products))


def rgcn_edges(nc, sem, ps, ident, rows, target, W, layer, epsc, key_a, w_a, gat_a, put_a, rel_a):
    f32, i32 = mybir.dt.float32, mybir.dt.int32
    ALU, ACT = mybir.AluOpType, mybir.ActivationFunctionType
    v = nc.vector
    nm = f"e{layer}_"
    with ExitStack() as st:
        def ring(name, shape, n=RING, dt=f32):
            return [st.enter_context(nc.sbuf_tensor(f"{nm}{name}{i}", shape, dt)) for i in range(n)]

        def sems(name):
            return [sem(f"{nm}{name}{i}") for i in range(RING)]
        xin, msg = ring("xin", [P, U, D]), ring("msg", [P, U, D])
        hid, Sw, CT = ring("hid", [P, U, D], 2), ring("Sw", [P, U, GRP], 2), ring("CT", [P, U, D], 2)
        gidx, pidx, kw = ring("gidx", [P, U], RING, i32), ring("pidx", [P, U], RING, i32), ring("kw", [P, 2, U])
        stats = ring("stats", [P, U, 6])
        mv, rstd, nbias = ring("mv", [P, U, 2]), ring("rstd", [P, U]), ring("nbias", [P, U])
        gidx_ready, gathered, put, kw_ready = sems("gidx"), sems("gathered"), sems("put"), sems("kw")
        pidx_ready, keyT, S_ready, hid_ready = sems("pidx"), sems("keyT"), sems("S"), sems("hid")
        cprod, CT_ready, mprod, msg_ready = sems("cprod"), sems("CT"), sems("mprod"), sems("msg")
        if layer == 0:
            aggr, var_ready, std_ready, norm_ready = sems("aggr"), sems("var"), sems("std"), sems("norm")
        passed, started = sem(nm + "passed"), sem(nm + "started")

        with nc.Block() as block:
            @block.gpsimd
            def _(pool):
                def gather(j, s, b):
                    pool.wait_ge(gidx_ready[s], j + 1)
                    after(pool, hid_ready[s], j)
                    pool.sem_inc(started, 1)
                    for u in range(U):
                        nc.gpsimd.indirect_dma_start(xin[s][:, u, :], None, rows,
                                                     bass.IndirectOffsetOnAxis(ap=gidx[s][:, u:u + 1], axis=0)).then_inc(gathered[s], 16)

                def scatter(j, s, b):
                    pool.wait_ge(msg_ready[s], j + 1)
                    pool.wait_ge(pidx_ready[s], j + 1)
                    after(pool, *one_before(put, j, s, 16 * U))
                    pool.sem_inc(started, 1)
                    for u in range(U):
                        nc.gpsimd.indirect_dma_start(target, bass.IndirectOffsetOnAxis(ap=pidx[s][:, u:u + 1], axis=0),
                                                     msg[s][:, u, :], None, compute_op=ALU.add).then_inc(put[s], 16)
                pipeline(pool, GA, (0, gather), (2, scatter))
                for s in range(RING):
                    pool.wait_ge(put[s], 16 * U * len(range(s, GA, RING)))

            @block.vector
            def _(dve):
                def gather_list(j, s, b):
                    after(dve, gathered[s], 16 * U * j)
                    v.tensor_copy(gidx[s][:, :], gat_a[:, bass.ds(at_block(j, s) * U, U)]).then_inc(gidx_ready[s], 1)

                def prepare(j, s, b):
                    at = bass.ds(at_block(j, s) * U, U)
                    v.tensor_copy(kw[s][:, 0, :], key_a[:, at])
                    v.tensor_copy(kw[s][:, 1, :], w_a[:, at]).then_inc(kw_ready[s], 1)
                    after(dve, put[s], 16 * U * j)
                    v.tensor_copy(pidx[s][:, :], put_a[:, at]).then_inc(pidx_ready[s], 1)
                    dve.wait_ge(gathered[s], 16 * U * (j + 1))
                    if layer == 0:
                        norm_stats(nc, dve, j, s, U, xin, stats, mv, aggr, passed, var_ready)
                        norm_factors(nc, dve, j, s, mv, rstd, nbias, aggr, std_ready, norm_ready)
                    after(dve, *two_before(cprod, j, s))
                    dve.wait_ge(keyT[s], j + 1)
                    dve.wait_ge(kw_ready[s], j + 1)
                    for u in range(U):
                        eq = v.tensor_scalar(Sw[s % 2][:, u, u * P:GRP], ps[s % 2][:, u * P:GRP], kw[s][:, 0, u:u + 1],
                                             kw[s][:, 1, u:u + 1], ALU.is_equal, ALU.mult)
                    eq.then_inc(S_ready[s], 1)
                pipeline(dve, GA, (0, gather_list), (3, prepare))

            @block.scalar
            def _(act):
                def norm(j, s, b):
                    after(act, *two_before(cprod, j, s))
                    if layer == 0:
                        norm_std(nc, act, j, s, mv, rstd, epsc, var_ready, std_ready)
                        act.wait_ge(norm_ready[s], j + 1)
                        for u in range(U):
                            t = nc.scalar.activation(hid[s % 2][:, u, :], xin[s][:, u, :], ACT.Relu,
                                                     bias=nbias[s][:, u:u + 1], scale=rstd[s][:, u:u + 1])
                        t.then_inc(hid_ready[s], 1)
                    else:
                        act.wait_ge(gathered[s], 16 * U * (j + 1))
                        nc.scalar.activation(hid[s % 2][:, :, :], xin[s][:, :, :], ACT.Relu).then_inc(hid_ready[s], 1)

                def copies(j, s, b):
                    act.wait_ge(cprod[s], j + 1)
                    after(act, *two_before(mprod, j, s))
                    nc.scalar.activation(CT[s % 2][:, :, :], ps[2 + s % 2][:, :].rearrange("p (u d) -> p u d", u=U),
                                         ACT.Copy).then_inc(CT_ready[s], 1)
                    act.wait_ge(mprod[s], j + 1)
                    after(act, put[s], 16 * U * j)
                    nc.scalar.activation(msg[s][:, :, :], ps[4 + s % 2][:, :].rearrange("p (u d) -> p u d", u=U),
                                         ACT.Copy).then_inc(msg_ready[s], 1)
                pipeline(act, GA, (0, norm), (1, copies))

            @block.tensor
            def _(pe):
                def keys(j, s, b):
                    pe.wait_ge(kw_ready[s], j + 1)
                    after(pe, *two_before(S_ready, j, s))
                    for u in range(U):
                        t = nc.tensor.transpose(ps[s % 2][:, u * P:(u + 1) * P],
                                                kw[s][:, 0, u:u + 1].to_broadcast([P, P]), ident[:, :])
                    t.then_inc(keyT[s], 1)

                def products(j, s, b):
                    rel = pe.value_load(rel_a[0:1, bass.ds(at_block(j, s), 1)], min_val=0, max_val=R - 1)
                    pe.wait_ge(hid_ready[s], j + 1)
                    pe.wait_ge(S_ready[s], j + 1)
                    after(pe, *two_before(CT_ready, j, s))
                    for u in range(U):
                        mm = nc.tensor.matmul(ps[2 + s % 2][:, u * P:GRP], hid[s % 2][:, u, :], Sw[s % 2][:, u, u * P:GRP],
                                              start=u == 0, stop=u == U - 1)
                    mm.then_inc(cprod[s], 1)
                    pe.wait_ge(CT_ready[s], j + 1)
                    after(pe, *two_before(msg_ready, j, s))
                    for u in range(U):
                        mm = nc.tensor.matmul(ps[4 + s % 2][:, u * P:(u + 1) * P], CT[s % 2][:, u, :],
                                              W[:, layer, bass.ds(rel * D, D)], start=True, stop=True)
                    mm.then_inc(mprod[s], 1)
                pipeline(pe, GA, (0, keys), (1, products))


def gat_scores(nc, sem, ps, ident, rows, g_tiles, wg, bias_bc, epsc, gat_c, own_c, score):
    f32, i32 = mybir.dt.float32, mybir.dt.int32
    ALU, ACT = mybir.AluOpType, mybir.ActivationFunctionType
    v = nc.vector
    nm = "s_"
    U2 = 2 * U
    with ExitStack() as st:
        def ring(name, shape, n=RING, dt=f32):
            return [st.enter_context(nc.sbuf_tensor(f"{nm}{name}{i}", shape, dt)) for i in range(n)]

        def sems(name):
            return [sem(f"{nm}{name}{i}") for i in range(RING)]
        xin, hid = ring("xin", [P, U2, D]), ring("hid", [P, U2, D])
        hidT, gout = ring("hidT", [P, U2, D], 2), ring("gout", [P, U, D])
        gidx = ring("gidx", [P, 2, U], RING, i32)
        stats = ring("stats", [P, U2, 6])
        mv, rstd, nbias = ring("mv", [P, U2, 2]), ring("rstd", [P, U2]), ring("nbias", [P, U2])
        gidx_ready, gathered, bias_off, hid_ready = sems("gidx"), sems("gathered"), sems("bias_off"), sems("hid")
        turned, hidT_ready, prod, g_ready = sems("turned"), sems("hidT"), sems("prod"), sems("g")
        score_ready, stored = sems("score"), sems("stored")
        aggr, var_ready, std_ready, norm_ready = sems("aggr"), sems("var"), sems("std"), sems("norm")
        passed, started = sem(nm + "passed"), sem(nm + "started")
        per = 16 * U2

        with nc.Block() as block:
            @block.gpsimd
            def _(pool):
                def gather(j, s, b):
                    pool.wait_ge(gidx_ready[s], j + 1)
                    after(pool, hid_ready[s], j)
                    pool.sem_inc(started, 1)
                    for side in range(2):
                        for u in range(U):
                            nc.gpsimd.indirect_dma_start(
                                xin[s][:, side * U + u, :], None, rows,
                                bass.IndirectOffsetOnAxis(ap=gidx[s][:, side, u:u + 1], axis=0)).then_inc(gathered[s], 16)
                pipeline(pool, GC, (0, gather))

            @block.sync
            def _(sp):
                def store(j, s, b):
                    sp.wait_ge(g_ready[s], j + 1)
                    sp.dma_start(g_tiles[bass.ds(at_block(j, s), 1), :, :, :].rearrange("o q u d -> (o q) u d"),
                                 gout[s][:, :, :]).then_inc(stored[s], 16)
                pipeline(sp, GC, (0, store))
                for s in range(RING):
                    sp.wait_ge(stored[s], 16 * len(range(s, GC, RING)))

            @block.vector
            def _(dve):
                def gather_list(j, s, b):
                    at = bass.ds(at_block(j, s) * U, U)
                    after(dve, gathered[s], per * j)
                    v.tensor_copy(gidx[s][:, 0, :], gat_c[:, at])
                    v.tensor_copy(gidx[s][:, 1, :], own_c[:, at]).then_inc(gidx_ready[s], 1)

                def stat(j, s, b):
                    dve.wait_ge(gathered[s], per * (j + 1))
                    v.tensor_tensor(xin[s][:, :, :], xin[s][:, :, :], bias_bc[:, 2:3, :].to_broadcast([P, U2, D]),
                                    ALU.subtract).then_inc(bias_off[s], 1)
                    dve.wait_ge(bias_off[s], j + 1)
                    norm_stats(nc, dve, j, s, U2, xin, stats, mv, aggr, passed, var_ready)
                    norm_factors(nc, dve, j, s, mv, rstd, nbias, aggr, std_ready, norm_ready)

                def keep(j, s, b):
                    dve.wait_ge(prod[s], j + 1)
                    v.tensor_copy(score[:, :, bass.ds(at_block(j, s) * U, U)],
                                  ps[6 + s % 2][:, 0:U * H].rearrange("p (u h) -> p h u", u=U)).then_inc(score_ready[s], 1)
                pipeline(dve, GC, (0, gather_list), (2, stat), (4, keep))

            @block.scalar
            def _(act):
                def norm(j, s, b):
                    after(act, turned[s], 2 * j)
                    norm_std(nc, act, j, s, mv, rstd, epsc, var_ready, std_ready)
                    norm_rows(nc, act, j, s, U2, xin, hid, rstd, nbias, norm_ready, hid_ready)

                def copy_T(j, s, b):
                    after(act, *two_before(prod, j, s))
                    for k in range(2):
                        act.wait_ge(turned[s], 2 * j + k + 1)
                        nc.scalar.activation(hidT[s % 2][:, k * U:(k + 1) * U, :],
                                             ps[2 * (s % 2) + k][:, :].rearrange("p (u d) -> p u d", u=U),
                                             ACT.Copy).then_inc(hidT_ready[s], 1)

                def copy_g(j, s, b):
                    act.wait_ge(prod[s], j + 1)
                    after(act, stored[s], 16 * j)
                    nc.scalar.activation(gout[s][:, :, :], ps[4 + s % 2][:, :].rearrange("p (u d) -> p u d", u=U),
                                         ACT.Copy).then_inc(g_ready[s], 1)
                pipeline(act, GC, (1, copy_T), (0, norm), (2, copy_g))

            @block.tensor
            def _(pe):
                def turn(j, s, b):
                    pe.wait_ge(hid_ready[s], j + 1)
                    after(pe, *two_before(hidT_ready, j, s, 2))
                    for k in range(2):
                        for u in range(U):
                            t = nc.tensor.transpose(ps[2 * (s % 2) + k][:, u * P:(u + 1) * P], hid[s][:, k * U + u, :], ident[:, :])
                        t.then_inc(turned[s], 1)

                def products(j, s, b):
                    pe.wait_ge(hidT_ready[s], 2 * j + 2)
                    after(pe, *two_before(g_ready, j, s))
                    after(pe, *two_before(score_ready, j, s))
                    for u in range(U):
                        nc.tensor.matmul(ps[4 + s % 2][:, u * D:(u + 1) * D], hidT[s % 2][:, u, :], wg[:, 0:D], start=True, stop=True)
                        nc.tensor.matmul(ps[6 + s % 2][:, u * H:(u + 1) * H], hidT[s % 2][:, u, :], wg[:, D:D + H],
                                         start=True, stop=False)
                        mm = nc.tensor.matmul(ps[6 + s % 2][:, u * H:(u + 1) * H], hidT[s % 2][:, U + u, :], wg[:, D + H:D + 2 * H],
                                              start=False, stop=True)
                    mm.then_inc(prod[s], 1)
                pipeline(pe, GC, (0, turn), (1, products))


def gat_softmax(nc, sem, chain_of, ps, ident, up_c, down_c, score):
    f32 = mybir.dt.float32
    ALU, ACT = mybir.AluOpType, mybir.ActivationFunctionType
    v = nc.vector
    PC = TC // U
    step, asked, turned, shifted, exped = sem("sm_step"), sem("sm_asked"), sem("sm_turned"), sem("sm_shifted"), sem("sm_exp")
    with ExitStack() as st:
        def tb(name, shape):
            return st.enter_context(nc.sbuf_tensor("sm_" + name, shape, f32))
        a, b, res = tb("a", [PC, H, FREE]), tb("b", [PC, H, FREE]), tb("res", [PC, H, FREE])
        tmp, small, rows = tb("tmp", [P, 1, FREE]), tb("small", [P, 4 * H]), tb("rows", [H, 2, P])
        up, down = up_c[0:PC, :], down_c[0:PC, :]
        with nc.Block() as block:
            @block.vector
            def _(dve):
                link = chain_of(dve, step)
                dve.wait_ge(turned, 1)
                for h in range(H):
                    cp = v.tensor_copy(a[:, h, :], ps[h][0:PC, :])
                link(cp)
                link(v.scalar_tensor_tensor(out=a[:, :, :], in0=a[:, :, :], scalar=SLOPE, in1=a[:, :, :],
                                            op0=ALU.mult, op1=ALU.max))
                link(v.tensor_copy(b[:, :, :], a[:, :, :]))
                n = totals_vector(nc, dve, link, asked, turned, 1, ps, b[:, :, :], res[:, :, :], up, down,
                                  tmp, small, rows, H, PC, True)
                v.tensor_tensor(a[:, :, :], a[:, :, :], res[:, :, :], ALU.subtract).then_inc(shifted, 1)
                dve.wait_ge(exped, 1)
                link(v.tensor_copy(b[:, :, :], a[:, :, :]))
                n = totals_vector(nc, dve, link, asked, turned, n, ps, b[:, :, :], res[:, :, :], up, down,
                                  tmp, small, rows, H, PC, False)
                link(v.tensor_scalar(res[:, :, :], res[:, :, :], TINY, None, ALU.add))
                link(v.reciprocal(res[:, :, :], res[:, :, :]))
                n += 1
                v.tensor_tensor(a[:, :, :], a[:, :, :], res[:, :, :], ALU.mult).then_inc(asked, 1)
                dve.wait_ge(turned, n)
                for h in range(H):
                    cp = v.tensor_copy(score[:, h, :].rearrange("q (p c) -> q c p", c=U),
                                       ps[4 + h][:, 0:TC].rearrange("q (c p) -> q c p", c=U))
                link(cp)

            @block.scalar
            def _(act):
                act.wait_ge(shifted, 1)
                nc.scalar.activation(a[:, :, :], a[:, :, :], ACT.Exp).then_inc(exped, 1)

            @block.tensor
            def _(pe):
                for h in range(H):
                    for c in range(U):
                        t = nc.tensor.transpose(ps[h][0:PC, c * P:(c + 1) * P], score[:, h, c::U], ident[:, :])
                t.then_inc(turned, 1)
                n = totals_tensor(nc, pe, asked, turned, 0, ps, ident, small, rows, H, PC)
                n = totals_tensor(nc, pe, asked, turned, n, ps, ident, small, rows, H, PC)
                pe.wait_ge(asked, n + 1)
                for h in range(H):
                    for c in range(U):
                        t = nc.tensor.transpose(ps[4 + h][:, c * PC:(c + 1) * PC], a[:, h, c * P:(c + 1) * P], ident[0:PC, 0:PC])
                t.then_inc(turned, 1)


def gat_edges(nc, sem, ps, ident, g_tiles, target, score, key_c, put_c):
    f32, i32 = mybir.dt.float32, mybir.dt.int32
    ALU, ACT = mybir.AluOpType, mybir.ActivationFunctionType
    v = nc.vector
    nm = "g_"
    Q3 = P - 32
    with ExitStack() as st:
        def ring(name, shape, n=RING, dt=f32):
            return [st.enter_context(nc.sbuf_tensor(f"{nm}{name}{i}", shape, dt)) for i in range(n)]

        def sems(name):
            return [sem(f"{nm}{name}{i}") for i in range(RING)]
        gin, msg = ring("gin", [P, U, D]), ring("msg", [P, U, D])
        gs, S, sumT = ring("gs", [P, U, D], 2), ring("S", [P, U, GRP], 2), ring("sumT", [P, U, P], 2)
        carry = ring("carry", [P, GRP], 2)
        pidx, kcol, co = ring("pidx", [P, U], RING, i32), ring("kcol", [P, U]), ring("co", [P, U, H])
        is_last = ring("is_last", [P, 1], 1)[0]
        loaded, slots, keyT, S_ready, scaled = sems("loaded"), sems("slots"), sems("keyT"), sems("S"), sems("scaled")
        pidx_ready, prod, sumT_ready, back = sems("pidx"), sems("prod"), sems("sumT"), sems("back")
        msg_ready, put = sems("msg"), sems("put")
        started, marked = sem(nm + "started"), sem(nm + "marked")

        with nc.Block() as block:
            @block.sync
            def _(sp):
                def load(j, s, b):
                    after(sp, scaled[s], j)
                    sp.dma_start(gin[s][:, :, :], g_tiles[bass.ds(at_block(j, s), 1), :, :, :].rearrange("o q u d -> (o q) u d")
                                 ).then_inc(loaded[s], 16)
                pipeline(sp, GC, (0, load))

            @block.gpsimd
            def _(pool):
                def scatter(j, s, b):
                    pool.wait_ge(msg_ready[s], j + 1)
                    pool.wait_ge(pidx_ready[s], j + 1)
                    pool.sem_inc(started, 1)
                    for u in range(U):
                        nc.gpsimd.indirect_dma_start(target, bass.IndirectOffsetOnAxis(ap=pidx[s][:, u:u + 1], axis=0),
                                                     msg[s][:, u, :], None, compute_op=ALU.add).then_inc(put[s], 16)
                pipeline(pool, GC, (0, scatter))
                for s in range(RING):
                    pool.wait_ge(put[s], 16 * U * len(range(s, GC, RING)))

            @block.vector
            def _(dve):
                def prepare(j, s, b):
                    at = bass.ds(at_block(j, s) * U, U)
                    v.tensor_copy(kcol[s][:, :], key_c[:, at])
                    v.tensor_copy(co[s][:, :, :], score[:, :, at].rearrange("p h u -> p u h")).then_inc(slots[s], 1)
                    after(dve, put[s], 16 * U * j)
                    v.tensor_copy(pidx[s][:, :], put_c[:, at]).then_inc(pidx_ready[s], 1)
                    dve.wait_ge(slots[s], j + 1)
                    dve.wait_ge(loaded[s], 16 * (j + 1))
                    after(dve, *two_before(prod, j, s))
                    v.tensor_tensor(gs[s % 2][:, :, :].rearrange("p u (h f) -> p (u h) f", h=H),
                                    gin[s][:, :, :].rearrange("p u (h f) -> p (u h) f", h=H),
                                    co[s][:, :, :].rearrange("p u (h o) -> p (u h) o", o=1).to_broadcast([P, U * H, F]),
                                    ALU.mult).then_inc(scaled[s], 1)
                    dve.wait_ge(keyT[s], j + 1)
                    if b != 0:
                        v.tensor_scalar(carry[s % 2][Q3:P, :], ps[s % 2][Q3:P, :], kcol[s - 1][Q3:P, U - 1:U],
                                        is_last[Q3:P, 0:1], ALU.is_equal, ALU.mult)
                    for u in range(U):
                        eq = v.tensor_scalar(S[s % 2][:, u, u * P:GRP], ps[s % 2][:, u * P:GRP], kcol[s][:, u:u + 1],
                                             None, ALU.is_equal)
                    eq.then_inc(S_ready[s], 1)
                v.tensor_copy(is_last[:, :], ident[:, P - 1:P]).then_inc(marked, 1)
                dve.wait_ge(marked, 1)
                pipeline(dve, GC, (0, prepare))

            @block.scalar
            def _(act):
                def copies(j, s, b):
                    act.wait_ge(prod[s], j + 1)
                    after(act, *two_before(back, j, s))
                    nc.scalar.activation(sumT[s % 2][:, :, :], ps[2 + s % 2][:, :].rearrange("p (u d) -> p u d", u=U),
                                         ACT.Copy).then_inc(sumT_ready[s], 1)
                    act.wait_ge(back[s], j + 1)
                    after(act, put[s], 16 * U * j)
                    nc.scalar.activation(msg[s][:, :, :], ps[4 + s % 2][:, :].rearrange("p (u d) -> p u d", u=U),
                                         ACT.Copy).then_inc(msg_ready[s], 1)
                pipeline(act, GC, (0, copies))

            @block.tensor
            def _(pe):
                def keys(j, s, b):
                    pe.wait_ge(slots[s], j + 1)
                    after(pe, *two_before(S_ready, j, s))
                    for u in range(U):
                        t = nc.tensor.transpose(ps[s % 2][:, u * P:(u + 1) * P], kcol[s][:, u:u + 1].to_broadcast([P, P]), ident[:, :])
                    t.then_inc(keyT[s], 1)

                def products(j, s, b):
                    pe.wait_ge(S_ready[s], j + 1)
                    pe.wait_ge(scaled[s], j + 1)
                    after(pe, *two_before(sumT_ready, j, s))
                    for u in range(U):
                        mm = nc.tensor.matmul(ps[2 + s % 2][:, u * P:GRP], gs[s % 2][:, u, :], S[s % 2][:, u, u * P:GRP],
                                              start=u == 0, stop=u == U - 1 and b == 0)
                    if b != 0:
                        pe.wait_ge(*one_before(msg_ready, j, s))
                        mm = nc.tensor.matmul(ps[2 + s % 2][:, :], msg[s - 1][Q3:P, U - 1, :], carry[s % 2][Q3:P, :],
                                              start=False, stop=True)
                    mm.then_inc(prod[s], 1)
                    pe.wait_ge(sumT_ready[s], j + 1)
                    after(pe, *two_before(msg_ready, j, s))
                    for u in range(U):
                        t = nc.tensor.transpose(ps[4 + s % 2][:, u * D:(u + 1) * D], sumT[s % 2][:, u, :], ident[:, :])
                    t.then_inc(back[s], 1)
                pipeline(pe, GC, (0, keys), (1, products))


_INS = ["x", "src", "dst", "edge_type_8", "L0_gnn_weights", "L0_gnn_roots", "L0_gnn_biases",
        "L1_gnn_weight", "L1_gnn_att", "L1_gnn_bias"]


def kernel(**inputs):
    import numpy as _np
    import concourse.bacc as _bacc
    from concourse import mybir as _mybir
    from concourse.bass_utils import run_bass_kernel_spmd as _run

    nc = _bacc.Bacc("TRN2", target_bir_lowering=False, num_devices=1)
    arrays, args = {}, []
    for name in _INS:
        a = _np.ascontiguousarray(inputs[name])
        arrays[f"in_{name}"] = a
        args.append(nc.dram_tensor(f"in_{name}", a.shape, _mybir.dt.from_np(a.dtype), kind="ExternalInput").ap())
    args.append(nc.dram_tensor("out_0", (N + DUMP, D), _mybir.dt.float32, kind="ExternalOutput").ap())
    gnn_program(nc, *args)
    r = _run(nc, [arrays], core_ids=[0])
    return r.results[0]["out_0"][:N]
```

```python
import concourse.bass as bass
from concourse import mybir
from contextlib import ExitStack, contextmanager

N = 100000
E = 50000
D = 128
R = 8
H = 4
F = D // H
P = 128
SLOPE = 0.2
EPS = 1e-5
TINY = 1e-16
NEG = 1e38

KSHIFT = 17
NODE_PAD = (1 << KSHIFT) - 1
LOGN = 16
FREE = (1 << LOGN) // P
LOADP, LOADF = 125, 400
U = 4
GRP = U * P
GA = (E + R * (GRP - 1)) // GRP
TA = GA * U
GC = -(-E // GRP)
TC = GC * U
RING = 4
DUMP = RING * U * P
DW = -(-TA // (RING * U)) * RING * U
RB = 8
NB = 98
BLK = P * RB
EARLY = -(-GA // RING)
SORT_START = 9
SORT_TURNS = (0, 3)


def gnn_program(nc, x, src, dst, etype, w_rel, roots, biases, w_gat, att, b_gat, out):
    f32, i32 = mybir.dt.float32, mybir.dt.int32
    ALU, ACT, AX = mybir.AluOpType, mybir.ActivationFunctionType, mybir.AxisListType

    y_dram = nc.dram_tensor("y_scratch", (N + DUMP, D), f32, kind="Internal").ap()
    g_dram = nc.dram_tensor("g_scratch", (TC * P, D), f32, kind="Internal").ap()
    g_tiles = g_dram.rearrange("(g u q) d -> g q u d", u=U, q=P)

    ctx = ExitStack()
    with ctx:
        def sb(name, shape, dt=f32):
            return ctx.enter_context(nc.sbuf_tensor(name, shape, dt))

        def sem(name):
            return ctx.enter_context(nc.semaphore(name))

        def chain_of(eng, s, start=0):
            count = [start]

            def link(ins):
                count[0] += 1
                ins.then_inc(s, 1)
                eng.wait_ge(s, count[0])
            return link

        ident = sb("ident", [P, P])
        ones = sb("ones", [P, P])
        epsc = sb("epsc", [P, 1])
        W = sb("W", [P, 2, R * D])
        root = sb("root", [P, 2, D])
        bias_bc = sb("bias_bc", [P, 3, D])
        wg = sb("wg", [P, D + 2 * H])
        att_bc = sb("att_bc", [P, H, 2 * F])
        key_a = sb("key_a", [P, TA])
        w_a = sb("w_a", [P, TA])
        gat_a = sb("gat_a", [P, TA])
        put_a = sb("put_a", [P, TA])
        rel_a = sb("rel_a", [1, GA], i32)
        key_c = sb("key_c", [P, TC])
        gat_c = sb("gat_c", [P, TC])
        own_c = sb("own_c", [P, TC])
        put_c = sb("put_c", [P, TC])
        score = sb("score", [P, H, TC])

        ps = [ctx.enter_context(nc.psum_tensor(f"ps{i}", [P, 512], f32)) for i in range(8)]
        psgn, pstep = sb("psgn", [P, 8]), sb("pstep", [P, 8])
        dump = sb("dump", [P, DW])
        K_a, V_a = [sb(f"K_a{i}", [P, FREE]) for i in range(2)], [sb(f"V_a{i}", [P, FREE]) for i in range(2)]
        K_c, V_c = [sb(f"K_c{i}", [P, FREE]) for i in range(2)], [sb(f"V_c{i}", [P, FREE]) for i in range(2)]
        up_c, down_c = sb("up_c", [P, FREE]), sb("down_c", [P, FREE])

        s_w, s_id, s_dump, s_set = sem("weights_loaded"), sem("constants"), sem("dump_cleared"), sem("setup_step")
        with (nc.sbuf_tensor("wa_tmp", [P, H, 2, F], f32) as wa_tmp, nc.sbuf_tensor("zeros", [P, DUMP // P, D], f32) as zeros,
              nc.Block() as block):
            @block.scalar
            def _(act):
                act.wait_ge(s_id, 4)
                act.dma_start(y_dram[N:N + DUMP, :].rearrange("(p r) d -> p r d", p=P), zeros[:, :, :]).then_inc(s_dump, 16)
                act.dma_start(out[N:N + DUMP, :].rearrange("(p r) d -> p r d", p=P), zeros[:, :, :]).then_inc(s_dump, 16)
                act.wait_ge(s_dump, 32)

            @block.sync
            def _(sp):
                for l in range(2):
                    for r in range(R):
                        sp.dma_start(W[:, l, r * D:(r + 1) * D], w_rel[l, r, :, :]).then_inc(s_w, 16)
                    sp.dma_start(root[:, l, :], roots[l, :, :]).then_inc(s_w, 16)
                sp.dma_start(wg[:, 0:D], w_gat).then_inc(s_w, 16)
                sp.dma_start(bias_bc[:, 0:2, :], biases.rearrange("(a l) d -> a l d", a=1).to_broadcast([P, 2, D])).then_inc(s_w, 16)
                sp.dma_start(bias_bc[:, 2, :], b_gat.rearrange("(a d) -> a d", a=1).to_broadcast([P, D])).then_inc(s_w, 16)
                sp.dma_start(att_bc[:, :, :], att.to_broadcast([P, H, 2 * F])).then_inc(s_w, 16)
                sp.wait_ge(s_w, 16 * (2 * (R + 1) + 4))

            @block.gpsimd
            def _(pool):
                pool.memset(ident[:, :], 0.0).then_inc(s_id, 1)
                pool.memset(ones[:, :], 1.0).then_inc(s_id, 1)
                pool.memset(epsc[:, :], EPS).then_inc(s_id, 1)
                pool.memset(zeros[:, :, :], 0.0).then_inc(s_id, 1)
                pool.wait_ge(s_id, 4)
                pool.affine_select(out=ident[:, :], in_=ident[:, :], compare_op=ALU.not_equal, fill=1.0,
                                   base=0, pattern=[[-1, P]], channel_multiplier=1).then_inc(s_id, 1)

            @block.vector
            def _(dve):
                link = chain_of(dve, s_set)
                dve.wait_ge(s_w, 16 * (2 * (R + 1) + 4))
                wv = wg[:, 0:D].rearrange("p (h f) -> p h f", h=H)
                for side, col in ((1, 0), (0, 1)):
                    link(nc.vector.tensor_tensor(wa_tmp[:, :, side, :], wv, att_bc[:, :, side * F:(side + 1) * F], ALU.mult))
                    link(nc.vector.tensor_reduce(wg[:, D + col * H:D + (col + 1) * H], wa_tmp[:, :, side, :], AX.X, ALU.add))

        with phase_semaphores(nc, ctx) as phase:
            edge_keys(nc, phase, chain_of, ps, ones, src, dst, etype, psgn, pstep, dump, K_a, V_a, K_c, V_c)
        with phase_semaphores(nc, ctx) as phase:
            with dst_lists(nc, phase, chain_of, ps, ident, dump, K_a, V_a, key_a, w_a, gat_a, put_a, rel_a) as lists:
                dense_pass(nc, phase, ps, ident, x, None, y_dram, root[:, 0, :], bias_bc, epsc, 1,
                           (chain_of, K_a, V_a, psgn, pstep), lists=lists)
        with phase_semaphores(nc, ctx) as phase:
            rgcn_edges(nc, phase, ps, ident, x, y_dram, W, 0, epsc, key_a, w_a, gat_a, put_a, rel_a)
        with nc.sbuf_tensor("early", [P, EARLY * U, D], f32) as early:
            with phase_semaphores(nc, ctx) as phase:
                dense_pass(nc, phase, ps, ident, y_dram, x, out, root[:, 1, :], bias_bc, epsc, 2,
                           (chain_of, K_c, V_c, psgn, pstep), gat_a, early)
            with phase_semaphores(nc, ctx) as phase:
                rgcn_edges(nc, phase, ps, ident, y_dram, out, W, 1, epsc, key_a, w_a, gat_a, put_a, rel_a, early)
        with phase_semaphores(nc, ctx) as phase:
            src_lists(nc, phase, chain_of, ps, ident, dump, K_c, V_c, key_c, gat_c, own_c, put_c, up_c, down_c)
        with phase_semaphores(nc, ctx) as phase:
            gat_scores(nc, phase, ps, ident, out, g_tiles, wg, bias_bc, epsc, gat_c, own_c, score)
        with phase_semaphores(nc, ctx) as phase:
            gat_softmax(nc, phase, chain_of, ps, ident, up_c, down_c, score)
        with phase_semaphores(nc, ctx) as phase:
            gat_edges(nc, phase, ps, ident, g_tiles, out, score, key_c, put_c)


@contextmanager
def phase_semaphores(nc, keep):
    with ExitStack() as held:
        mine = []

        def sem(name):
            if name[:-1].endswith(("gathered", "stored", "put")):
                return keep.enter_context(nc.semaphore(name))
            mine.append(held.enter_context(nc.semaphore(name)))
            return mine[-1]
        yield sem
        with nc.Block() as block:
            @block.gpsimd
            def _(pool):
                for s in mine:
                    pool.sem_clear(s)


def sort_steps():
    for phase in range(1, LOGN + 1):
        if phase >= 10:
            yield "turn", 0
            for bit in range(phase - 1, 8, -1):
                yield "stage", 1 << (bit - 9)
            yield "turn", 0
        for bit in range(min(phase, 9) - 1, -1, -1):
            yield "stage", 1 << bit
        if phase < LOGN:
            yield "flip", phase


TURNS = sum(what == "turn" for what, _ in sort_steps())


def stages_to_turn(steps):
    n = 0
    for what, _ in steps:
        if what == "turn":
            break
        n += what == "stage"
    return n


FIRST = stages_to_turn(sort_steps()) % 2


def network(nc, dve, done, asked, turned, K, V, m, dv, psgn, pstep, bank_k, bank_v):
    ALU = mybir.AluOpType
    v = nc.vector
    steps = list(sort_steps())
    asks, cur, results = 0, FIRST, [0]

    def result(ins):
        results[0] += 1
        ins.then_inc(done, 1)
        return results[0]

    kk = K[cur][:, :].rearrange("p (b h k) -> p b h k", h=2, k=2)
    keys = values = result(v.tensor_scalar(kk[:, :, 1, :], kk[:, :, 1, :], -1.0, None, ALU.mult))
    for i, (what, k) in enumerate(steps):
        if what == "stage":
            pair = [t[:, :].rearrange("p (b h k) -> p b h k", h=2, k=k) for t in (K[cur], V[cur], K[1 - cur], V[1 - cur])]
            ka, kb = pair[0][:, :, 0, :], pair[0][:, :, 1, :]
            va, vb = pair[1][:, :, 0, :], pair[1][:, :, 1, :]
            mm = m[:, :].rearrange("p (b k) -> p b k", k=k)
            dd = dv[:, :].rearrange("p (b k) -> p b k", k=k)
            dve.wait_ge(done, keys)
            v.tensor_tensor(mm, ka, kb, ALU.is_gt)
            yield i
            dve.wait_ge(done, values)
            diff = result(v.tensor_tensor(dd, vb, va, ALU.subtract))
            v.tensor_tensor(pair[2][:, :, 0, :], ka, kb, ALU.min)
            yield i
            dve.wait_ge(done, diff)
            move = result(v.tensor_tensor(dd, dd, mm, ALU.mult))
            keys = result(v.tensor_tensor(pair[2][:, :, 1, :], ka, kb, ALU.max))
            yield i
            dve.wait_ge(done, move)
            v.tensor_tensor(pair[3][:, :, 0, :], va, dd, ALU.add)
            last = v.tensor_tensor(pair[3][:, :, 1, :], vb, dd, ALU.subtract)
            cur = 1 - cur
        elif what == "turn":
            dve.wait_ge(turned, asks)
            cur = stages_to_turn(steps[i + 1:]) % 2
            v.tensor_copy(K[cur][:, :], bank_k[:, :])
            last = v.tensor_copy(V[cur][:, :], bank_v[:, :])
        elif k < 8:
            q = 1 << k
            kk = K[cur][:, :].rearrange("p (b k) -> p b k", k=4 * q)
            dve.wait_ge(done, keys)
            last = v.tensor_scalar(kk[:, :, q:3 * q], kk[:, :, q:3 * q], -1.0, None, ALU.mult)
        elif k == 8:
            kk = K[cur][:, :].rearrange("p (b h k) -> p b h k", h=2, k=256)
            dve.wait_ge(done, keys)
            keys = result(v.tensor_scalar(kk[:, :, 1, :], kk[:, :, 1, :], -1.0, None, ALU.mult))
            yield i
            dve.wait_ge(done, keys)
            last = v.tensor_scalar(K[cur][:, :], K[cur][:, :], psgn[:, 0:1], None, ALU.mult)
        else:
            dve.wait_ge(done, keys)
            last = v.tensor_scalar(K[cur][:, :], K[cur][:, :], pstep[:, k - 9:k - 8], None, ALU.mult)
        if i + 1 < len(steps) and steps[i + 1][0] == "turn":
            asks += 1
            last.then_inc(asked, 1)
        elif what == "stage":
            values = result(last)
        else:
            keys = values = result(last)
        yield i + 1
    dve.wait_ge(done, values)


def blocks_due():
    at = [i for i, (what, _) in enumerate(sort_steps()) if what == "turn"]
    blocks = [(SORT_START + 2 * (t // 2)) * RING + SORT_TURNS[t % 2] + 2 for t in range(TURNS)]
    due, was, had = [], 0, 0
    for i, n in zip(at + [at[-1] + 10], blocks + [NB]):
        due += [had + (n - had) * (k + 1) / (i - was) for k in range(i - was)]
        was, had = i, n
    return due + [NB]


def network_turn(nc, K, V, bank_k, bank_v, ident):
    for bank, of in ((bank_k, K[0]), (bank_v, V[0])):
        for c in range(4):
            last = nc.tensor.transpose(bank[:, c * P:(c + 1) * P], of[:, c * P:(c + 1) * P], ident[:, :])
    return last


def totals_vector(nc, dve, link, asked, turned, n, ps, v, res, up, down, tmp, small, rows, heads, parts, biggest):
    f32 = mybir.dt.float32
    ALU, AX = mybir.AluOpType, mybir.AxisListType
    V = nc.vector
    ends, carry = small[0:parts, 0:2 * heads], small[0:parts, 2 * heads:3 * heads]
    flag = small[0:parts, 3 * heads:3 * heads + 1]
    rflag, rsh = rows[0:heads, 0, 0:parts], rows[0:heads, 1, :]
    for back in (0, 1):
        if back:
            link(V.tensor_scalar(tmp[0:parts, 0, :], down, -1.0, 1.0, ALU.mult, ALU.add))
            link(V.tensor_tensor(v, res, tmp[0:parts, 0:1, :].to_broadcast([parts, heads, FREE]), ALU.mult))
            cont, op0, op1, neutral, same = down, ALU.mult, ALU.add, 0.0, down
        elif biggest:
            link(V.tensor_scalar(tmp[0:parts, 0, :], up, NEG, -NEG, ALU.mult, ALU.add))
            cont, op0, op1, neutral, same = tmp[0:parts, 0, :], ALU.add, ALU.max, -NEG, up
        else:
            cont, op0, op1, neutral, same = up, ALU.mult, ALU.add, 0.0, up
        way = slice(None, None, -1) if back else slice(None)
        edge = slice(0, 1) if back else slice(FREE - 1, FREE)
        for h in range(heads):
            last = V.tensor_tensor_scan(res[:, h, way], cont[:, way], v[:, h, way], neutral, op0, op1)
        link(last)
        link(V.tensor_reduce(flag, same, AX.X, ALU.min))
        V.tensor_copy(ends[:, 0:heads], res[:, :, edge].rearrange("p h o -> p (h o)"))
        n += 1
        V.tensor_copy(ends[:, heads:2 * heads], flag.to_broadcast([parts, heads])).then_inc(asked, 1)
        dve.wait_ge(turned, n)
        if biggest and not back:
            link(V.tensor_scalar(rflag, ps[1][0:heads, 0:parts], NEG, -NEG, ALU.mult, ALU.add))
        else:
            link(V.tensor_copy(rflag, ps[1][0:heads, 0:parts]))
        link(V.memset(rsh, neutral))
        n += 1
        into = rsh[:, 0:parts - 1] if back else rsh[:, 1:parts]
        of = slice(1, parts) if back else slice(0, parts - 1)
        V.tensor_tensor_scan(into[:, way], rflag[:, of][:, way], ps[0][0:heads, of][:, way],
                             neutral, op0, op1).then_inc(asked, 1)
        dve.wait_ge(turned, n)
        link(V.tensor_copy(carry, ps[2][0:parts, 0:heads]))
        for h in range(heads):
            last = V.tensor_tensor_scan(res[:, h, way], cont[:, way], v[:, h, way], carry[:, h:h + 1], op0, op1)
        link(last)
    return n


def totals_tensor(nc, pe, asked, turned, n, ps, ident, small, rows, heads, parts):
    for _ in range(2):
        n += 1
        pe.wait_ge(asked, n)
        nc.tensor.transpose(ps[0][0:heads, 0:parts], small[0:parts, 0:heads], ident[0:parts, 0:parts])
        nc.tensor.transpose(ps[1][0:heads, 0:parts], small[0:parts, heads:2 * heads], ident[0:parts, 0:parts]).then_inc(turned, 1)
        n += 1
        pe.wait_ge(asked, n)
        nc.tensor.transpose(ps[2][0:parts, 0:heads], rows[0:heads, 1, 0:parts], ident[0:heads, 0:heads]).then_inc(turned, 1)
    return n


def neighbours_vector(nc, dve, link, asked, turned, n, ps, K, up, down, edge_cols, shift_l, shift_r, near):
    ALU = mybir.AluOpType
    v = nc.vector
    v.tensor_copy(edge_cols[:, 0:1], K[:, 0:1])
    v.memset(shift_l[:, :], -1.0)
    v.memset(shift_r[:, :], -1.0)
    v.tensor_copy(edge_cols[:, 1:2], K[:, FREE - 1:FREE]).then_inc(asked, 1)
    dve.wait_ge(turned, n + 1)
    v.tensor_copy(shift_l[:, 0:P - 1], ps[0][0:2, 1:P])
    v.tensor_copy(shift_r[:, 1:P], ps[0][0:2, 0:P - 1]).then_inc(asked, 1)
    dve.wait_ge(turned, n + 2)
    link(v.tensor_copy(near[:, :], ps[1][:, 0:4]))
    v.tensor_tensor(up[:, 1:FREE], K[:, 1:FREE], K[:, 0:FREE - 1], ALU.is_equal)
    v.tensor_tensor(up[:, 0:1], K[:, 0:1], near[:, 3:4], ALU.is_equal)
    v.tensor_tensor(down[:, 0:FREE - 1], K[:, 1:FREE], K[:, 0:FREE - 1], ALU.is_equal)
    link(v.tensor_tensor(down[:, FREE - 1:FREE], K[:, FREE - 1:FREE], near[:, 0:1], ALU.is_equal))
    return n + 2


def neighbours_tensor(nc, pe, asked, turned, n, ps, ident, edge_cols, shift_l, shift_r):
    pe.wait_ge(asked, n + 1)
    nc.tensor.transpose(ps[0][0:2, 0:P], edge_cols[:, :], ident[:, :]).then_inc(turned, 1)
    pe.wait_ge(asked, n + 2)
    nc.tensor.transpose(ps[1][:, 0:2], shift_l[:, :], ident[0:2, 0:2])
    nc.tensor.transpose(ps[1][:, 2:4], shift_r[:, :], ident[0:2, 0:2]).then_inc(turned, 1)
    return n + 2


def lists_vector(nc, dve, link, asked, turned, n, ps, width, lists):
    dve.wait_ge(turned, n)
    for bank, to in enumerate(lists):
        last = nc.vector.tensor_copy(to[:, :].rearrange("q (p c) -> q c p", c=U),
                                     ps[bank][:, :].rearrange("q (c p) -> q c p", c=U)[:, :, 0:width // U])
    link(last)


def lists_tensor(nc, pe, asked, turned, n, ps, ident, of):
    pe.wait_ge(asked, n)
    for bank, a in enumerate(of):
        for c in range(4):
            last = nc.tensor.transpose(ps[bank][:, c * P:(c + 1) * P], a[:, c * P:(c + 1) * P], ident[:, :])
    last.then_inc(turned, 1)


def put_rows(nc, link, node, lead, dump, t1, t2, put, n, weight=None):
    ALU = mybir.AluOpType
    v = nc.vector
    v.tensor_scalar(lead[:, :], lead[:, :], -1.0, 1.0, ALU.mult, ALU.add)
    link(v.tensor_scalar(t1[:, 0:n], node[:, 0:n], float(N), None, ALU.is_lt))
    if weight is not None:
        link(v.tensor_tensor(weight[:, :], weight[:, :], t1[:, 0:n], ALU.mult))
    link(v.tensor_tensor(t1[:, 0:n], lead[:, :], t1[:, 0:n], ALU.mult))
    link(v.tensor_tensor(t2[:, 0:n], node[:, 0:n], dump[:, 0:n], ALU.subtract))
    link(v.tensor_tensor(t2[:, 0:n], t2[:, 0:n], t1[:, 0:n], ALU.mult))
    link(v.tensor_tensor(put[:, :], t2[:, 0:n], dump[:, 0:n], ALU.add))


def edge_keys(nc, sem, chain_of, ps, ones, src, dst, etype, psgn, pstep, dump, K, V, K_c, V_c):
    f32, i32 = mybir.dt.float32, mybir.dt.int32
    ALU, AX = mybir.AluOpType, mybir.AxisListType
    BIG = float(R * (1 << KSHIFT) + NODE_PAD)
    v = nc.vector
    with ExitStack() as st:
        def tb(name, shape, dt=f32):
            return st.enter_context(nc.sbuf_tensor(name, shape, dt))
        raw = tb("raw", [P, 3, LOADF], i32)
        rawf = tb("rawf", [P, 3, LOADF])
        is_rel = tb("is_rel", [P, R, LOADF])
        cnt, rkey = tb("cnt", [P, R]), tb("rkey", [P, R])
        pad, pkey = tb("pad", [P, R, U]), tb("pkey", [P, R, U])
        cnti, ridx = tb("cnti", [P, R], i32), tb("ridx", [P, R], i32)
        pidx, pidxf = tb("pidx", [P, 1], i32), tb("pidxf", [P, 1])
        pbit, dumpi = tb("pbit", [P, 8], i32), tb("dumpi", [P, DW], i32)
        s_ld, s_io, s_v = sem("edges_loaded"), sem("numbered"), sem("key_step")
        counted, summed = sem("counted"), sem("summed")
        with nc.Block() as block:
            @block.sync
            def _(sp):
                for i, a in enumerate((src, dst, etype)):
                    sp.dma_start(raw[0:LOADP, i, :], a.rearrange("(p f) -> p f", p=LOADP)).then_inc(s_ld, 16)

            @block.gpsimd
            def _(pool):
                pool.iota(pidx[:, :], pattern=[[0, 1]], base=0, channel_multiplier=1).then_inc(s_io, 1)
                pool.iota(ridx[:, :], pattern=[[1, R]], base=0, channel_multiplier=0).then_inc(s_io, 1)
                pool.iota(dumpi[:, :], pattern=[[0, DW // (RING * U)], [P, RING * U]], base=N, channel_multiplier=1).then_inc(s_io, 1)

            @block.vector
            def _(dve):
                link = chain_of(dve, s_v)
                for k, pv in ((K, V), (K_c, V_c)):
                    v.memset(k[FIRST][:, :], BIG)
                    link(v.memset(pv[FIRST][:, :], 0.0))
                link(v.memset(cnt[:, :], 0.0))
                dve.wait_ge(s_io, 3)
                dve.wait_ge(s_ld, 48)
                link(v.tensor_copy(rawf[0:LOADP, :, :], raw[0:LOADP, :, :]))
                v.scalar_tensor_tensor(out=K[FIRST][0:LOADP, 0:LOADF], in0=rawf[0:LOADP, 2, :], scalar=float(1 << KSHIFT),
                                       in1=rawf[0:LOADP, 1, :], op0=ALU.mult, op1=ALU.add)
                v.tensor_copy(V[FIRST][0:LOADP, 0:LOADF], rawf[0:LOADP, 0, :])
                v.tensor_copy(K_c[FIRST][0:LOADP, 0:LOADF], rawf[0:LOADP, 0, :])
                link(v.tensor_copy(V_c[FIRST][0:LOADP, 0:LOADF], rawf[0:LOADP, 1, :]))
                for r in range(R):
                    last = v.tensor_scalar(is_rel[0:LOADP, r, :], rawf[0:LOADP, 2, :], float(r), None, ALU.is_equal)
                link(last)
                v.tensor_reduce(cnt[0:LOADP, :], is_rel[0:LOADP, :, :], AX.X, ALU.add).then_inc(counted, 1)
                dve.wait_ge(summed, 1)
                link(v.tensor_scalar(cnti[:, :], ps[0][:, 0:R], -1.0, float(1 << 20), ALU.mult, ALU.add))
                link(v.tensor_scalar(cnti[:, :], cnti[:, :], GRP - 1, None, ALU.bitwise_and))
                v.tensor_copy(pidxf[:, :], pidx[:, :])
                for c in range(U):
                    wanted = v.tensor_scalar(pad[:, :, c], cnti[:, :], float(c * P), None, ALU.subtract)
                link(wanted)
                link(v.tensor_copy(rkey[:, :], ridx[:, :]))
                v.tensor_scalar(pad[:, :, :], pad[:, :, :], pidxf[:, 0:1], None, ALU.is_gt)
                link(v.tensor_scalar(rkey[:, :], rkey[:, :], float(1 << KSHIFT), float(NODE_PAD) - BIG, ALU.mult, ALU.add))
                link(v.tensor_tensor(pkey[:, :, :], pad[:, :, :], rkey[:, :].rearrange("p (r o) -> p r o", o=1).to_broadcast([P, R, U]),
                                     ALU.mult))
                link(v.tensor_scalar(K[FIRST][:, LOADF:LOADF + R * U], pkey[:, :, :].rearrange("p r c -> p (r c)"), BIG, None, ALU.add))
                for b in range(8):
                    last = v.tensor_scalar(pbit[:, b:b + 1], pidx[:, :], b, 1, ALU.logical_shift_right, ALU.bitwise_and)
                link(last)
                link(v.tensor_scalar(psgn[:, :], pbit[:, :], -2.0, 1.0, ALU.mult, ALU.add))
                link(v.tensor_tensor(pstep[:, 0:7], psgn[:, 0:7], psgn[:, 1:8], ALU.mult))
                link(v.tensor_copy(dump[:, :], dumpi[:, :]))

            @block.tensor
            def _(pe):
                pe.wait_ge(counted, 1)
                nc.tensor.matmul(ps[0][:, 0:R], ones[:, :], cnt[:, :], start=True, stop=True).then_inc(summed, 1)


@contextmanager
def dst_lists(nc, sem, chain_of, ps, ident, dump, K, V, key_a, w_a, gat_a, put_a, rel_a):
    f32, i32 = mybir.dt.float32, mybir.dt.int32
    ALU = mybir.AluOpType
    v = nc.vector
    with ExitStack() as st:
        def tb(name, shape, dt=f32):
            return st.enter_context(nc.sbuf_tensor("n_" + name, shape, dt))
        edge_cols, shift_l, shift_r = tb("edge_cols", [P, 2]), tb("shift_l", [2, P]), tb("shift_r", [2, P])
        near = tb("near", [P, 4])
        up_a, down_a = tb("up_a", [P, FREE]), tb("down_a", [P, FREE])
        one_a, tot_a = tb("one_a", [P, 1, FREE]), tb("tot_a", [P, 1, FREE])
        seg_tmp, seg_small, seg_rows = tb("seg_tmp", [P, 1, FREE]), tb("seg_small", [P, 8]), tb("seg_rows", [4, 2, P])
        lead_a = tb("lead_a", [P, TA])
        keyi, node = tb("keyi", [P, TA], i32), tb("node", [P, TA])
        t1, t2 = tb("t1", [P, TA]), tb("t2", [P, TA])
        relf, reli = tb("relf", [1, GA]), tb("reli", [1, GA], i32)
        asked, turned, step = sem("n_asked"), sem("n_turned"), sem("n_step")
        def vector(dve):
            link = chain_of(dve, step)
            n = neighbours_vector(nc, dve, link, asked, turned, 0, ps, K[0], up_a, down_a,
                                  edge_cols, shift_l, shift_r, near)
            link(v.memset(one_a[:, :, :], 1.0))
            n = totals_vector(nc, dve, link, asked, turned, n, ps, one_a[:, :, :], tot_a[:, :, :],
                              up_a[:, :], down_a[:, :], seg_tmp, seg_small, seg_rows, 1, P, False)
            v.memset(down_a[:, FREE - 1:FREE], 0.0)
            v.reciprocal(tot_a[:, 0, :], tot_a[:, 0, :]).then_inc(asked, 1)
            lists_vector(nc, dve, link, asked, turned, n + 1, ps, TA, (key_a, gat_a, w_a, lead_a))
            link(v.tensor_copy(keyi[:, :], key_a[:, :]))
            link(v.tensor_scalar(keyi[:, :], keyi[:, :], NODE_PAD, None, ALU.bitwise_and))
            link(v.tensor_copy(node[:, :], keyi[:, :]))
            put_rows(nc, link, node, lead_a, dump, t1, t2, put_a, TA, w_a)
            link(v.tensor_copy(reli[:, :], key_a[0:1, 0::U]))
            link(v.tensor_scalar(reli[:, :], reli[:, :], KSHIFT, None, ALU.logical_shift_right))
            link(v.tensor_copy(relf[:, :], reli[:, :]))
            link(v.tensor_scalar(relf[:, :], relf[:, :], float(R - 1), None, ALU.min))
            link(v.tensor_copy(rel_a[:, :], relf[:, :]))

        def tensor(pe):
            n = neighbours_tensor(nc, pe, asked, turned, 0, ps, ident, edge_cols, shift_l, shift_r)
            n = totals_tensor(nc, pe, asked, turned, n, ps, ident, seg_small, seg_rows, 1, P)
            lists_tensor(nc, pe, asked, turned, n + 1, ps, ident, (K[0], V[0], tot_a[:, 0, :], down_a))

        yield vector, tensor


def src_lists(nc, sem, chain_of, ps, ident, dump, K_c, V_c, key_c, gat_c, own_c, put_c, up_c, down_c):
    f32 = mybir.dt.float32
    ALU = mybir.AluOpType
    v = nc.vector
    with ExitStack() as st:
        def tb(name, shape):
            return st.enter_context(nc.sbuf_tensor("l_" + name, shape, f32))
        edge_cols, shift_l, shift_r, near = tb("edge_cols", [P, 2]), tb("shift_l", [2, P]), tb("shift_r", [2, P]), tb("near", [P, 4])
        lead_c, t1, t2 = tb("lead", [P, TC]), tb("t1", [P, TC]), tb("t2", [P, TC])
        asked, turned, step = sem("l_asked"), sem("l_turned"), sem("l_step")
        with nc.Block() as block:
            @block.vector
            def _(dve):
                link = chain_of(dve, step)
                n = neighbours_vector(nc, dve, link, asked, turned, 0, ps, K_c[0], up_c, down_c, edge_cols, shift_l, shift_r, near)
                dve.sem_inc(asked, 1)
                lists_vector(nc, dve, link, asked, turned, n + 1, ps, TC, (key_c, gat_c, lead_c))
                put_rows(nc, link, key_c, lead_c, dump, t1, t2, put_c, TC)
                link(v.tensor_scalar(own_c[:, :], key_c[:, :], float(N - 1), None, ALU.min))

            @block.tensor
            def _(pe):
                n = neighbours_tensor(nc, pe, asked, turned, 0, ps, ident, edge_cols, shift_l, shift_r)
                lists_tensor(nc, pe, asked, turned, n + 1, ps, ident, (K_c[0], V_c[0], down_c))


def pipeline(eng, count, *stages, among=None):
    def step(j, s):
        for lag, stage in stages:
            jj, ss = (j, s - lag) if s >= lag else (j - 1, s - lag + RING)
            b = jj * RING + ss if isinstance(jj, int) else None
            if b is None or 0 <= b < count:
                stage(jj, ss, b)

    for k in range(2 * RING):
        step(k // RING, k % RING)
    done = 2
    if among is not None:
        start, bodies, rounds, work = among
        with eng.Fori(done, start) as j:
            for s in range(RING):
                step(j, s)
        with eng.Fori(0, bodies) as i:
            for k in range(rounds * RING):
                work(i, k)
                step(i * rounds + (start + k // RING), k % RING)
        done = start + bodies * rounds
    with eng.Fori(done, count // RING) as j:
        for s in range(RING):
            step(j, s)
    for k in range(count // RING * RING, count + max(lag for lag, _ in stages)):
        step(k // RING, k % RING)


def after(eng, s, value):
    if not isinstance(value, int) or value > 0:
        eng.wait_ge(s, value)


def two_before(sems, j, s, per=1):
    return (sems[s - 2], per * (j + 1)) if s >= 2 else (sems[s + 2], per * j)


def one_before(sems, j, s, per=1):
    return (sems[s - 1], per * (j + 1)) if s >= 1 else (sems[RING - 1], per * j)


def at_block(j, s):
    return j * RING + s


def norm_stats(nc, dve, j, s, rows, x, stats, aggr, var_ready):
    after(dve, var_ready[s], j)
    for r in range(rows):
        last = nc.vector.bn_stats(stats[s][:, r, :], x[s][:, r, :])
    last.then_inc(aggr[s], 1)


def norm_moments(nc, dve, j, s, rows, stats, mv, aggr, passed, var_ready):
    dve.wait_ge(aggr[s], 2 * j + 1)
    dve.sem_inc(passed, 1)
    for r in range(rows):
        last = nc.vector.bn_aggr(mv[s][:, r, :], stats[s][:, r, :])
    last.then_inc(var_ready[s], 1)


def norm_inverse(nc, dve, j, s, rstd, aggr, std_ready):
    dve.wait_ge(std_ready[s], j + 1)
    nc.vector.reciprocal(rstd[s][:, :], rstd[s][:, :]).then_inc(aggr[s], 1)


def norm_shift(nc, dve, j, s, mv, rstd, nbias, aggr, norm_ready):
    dve.wait_ge(aggr[s], 2 * j + 2)
    nc.vector.scalar_tensor_tensor(out=nbias[s][:, :], in0=mv[s][:, :, 0], scalar=-1.0, in1=rstd[s][:, :],
                                   op0=mybir.AluOpType.mult, op1=mybir.AluOpType.mult).then_inc(norm_ready[s], 1)


def norm_std(nc, act, j, s, mv, rstd, epsc, var_ready, std_ready):
    act.wait_ge(var_ready[s], j + 1)
    nc.scalar.activation(rstd[s][:, :], mv[s][:, :, 1], mybir.ActivationFunctionType.Sqrt,
                         bias=epsc[:, :]).then_inc(std_ready[s], 1)


def norm_rows(nc, act, j, s, rows, x, hid, rstd, nbias, norm_ready, hid_ready):
    act.wait_ge(norm_ready[s], j + 1)
    for r in range(rows):
        last = nc.scalar.activation(hid[s][:, r, :], x[s][:, r, :], mybir.ActivationFunctionType.Relu,
                                    bias=nbias[s][:, r:r + 1], scale=rstd[s][:, r:r + 1])
    last.then_inc(hid_ready[s], 1)


def dense_pass(nc, sem, ps, ident, inp, res, outp, root, bias_bc, epsc, nr, to_sort, gat_a=None, early=None, lists=None):
    f32 = mybir.dt.float32
    ALU, ACT = mybir.AluOpType, mybir.ActivationFunctionType
    v = nc.vector
    nm = f"d{nr}_"
    with ExitStack() as st:
        def ring(name, shape, n=RING):
            return [st.enter_context(nc.sbuf_tensor(f"{nm}{name}{i}", shape, f32)) for i in range(n)]

        def sems(name):
            return [sem(f"{nm}{name}{i}") for i in range(RING)]
        xin, yo = ring("xin", [P, RB, D]), ring("yo", [P, RB, D])
        hidT = ring("hidT", [P, RB, D], 2)
        rin = ring("rin", [P, RB, D]) if nr == 2 else None
        hid = ring("hid", [P, RB, D]) if nr == 1 else None
        stats, bsum = ring("stats", [P, RB, 6]), ring("bsum", [P, D], 1)[0]
        mv, rstd, nbias = ring("mv", [P, RB, 2]), ring("rstd", [P, RB]), ring("nbias", [P, RB])
        loaded, stored, y_ready = sems("loaded"), sems("stored"), sems("y")
        turned, hidT_ready, prod = sems("turned"), sems("hidT"), sems("prod")
        if nr == 1:
            aggr, var_ready, std_ready, norm_ready, hid_ready = (sems("aggr"), sems("var"), sems("std"), sems("norm"),
                                                                 sems("hid"))
            biased = sems("biased")
        else:
            res_ready, col_ready, early_gathered, kept = sems("res"), sems("col"), sems("early_gathered"), sems("kept")
            grow = ring("grow", [P, D])
            gcol = [st.enter_context(nc.sbuf_tensor(f"{nm}gcol{i}", [P, 1], mybir.dt.int32)) for i in range(RING)]
            started = sem(nm + "started")
        chain_of, K, V, psgn, pstep = to_sort
        m, dv = ring("m", [P, FREE // 2], 1)[0], ring("dv", [P, FREE // 2], 1)[0]
        asked, list_turned, sort_step = sem(nm + "asked"), sem(nm + "list_turned"), sem(nm + "sort_step")
        passed, bias_ready = sem(nm + "passed"), sem(nm + "bias")
        per = 16 * nr

        def rows_of(t, j, s, b):
            at = N - BLK if b == NB - 1 else at_block(j, s) * BLK
            return t[bass.ds(at, BLK), :].rearrange("(p r) d -> p r d", r=RB)

        with nc.Block() as block:
            @block.sync
            def _(sp):
                def load(j, s, b):
                    if nr == 1:
                        after(sp, hid_ready[s], j)
                    else:
                        after(sp, turned[s], 2 * j)
                    sp.dma_start(xin[s][:, :, :], rows_of(inp, j, s, b)).then_inc(loaded[s], 16)
                    if nr == 2:
                        after(sp, prod[s], 2 * j)
                        sp.dma_start(rin[s][:, :, :], rows_of(res, j, s, b)).then_inc(loaded[s], 16)
                pipeline(sp, NB, (0, load))

            @block.gpsimd
            def _(pool):
                def bias(j, s, b):
                    pool.wait_ge(loaded[s], per * (j + 1))
                    nc.gpsimd.tensor_tensor(rin[s][:, :, :], rin[s][:, :, :],
                                            bsum[:, :].rearrange("p (o d) -> p o d", o=1).to_broadcast([P, RB, D]),
                                            ALU.add).then_inc(res_ready[s], 1)

                def add(j, s, b):
                    pool.wait_ge(y_ready[s], 2 * (j + 1))
                    nc.gpsimd.tensor_tensor(yo[s][:, :, :], yo[s][:, :, :], bias_bc[:, 0:1, :].to_broadcast([P, RB, D]),
                                            ALU.add).then_inc(biased[s], 1)

                def gather(j, s, b):
                    after(pool, kept[s], j)
                    nc.gpsimd.tensor_copy(gcol[s][:, :], gat_a[:, bass.ds(j * (RING * U) + s, 1)]).then_inc(col_ready[s], 1)
                    pool.wait_ge(col_ready[s], j + 1)
                    pool.sem_inc(started, 1)
                    nc.gpsimd.indirect_dma_start(grow[s][:, :], None, inp, bass.IndirectOffsetOnAxis(ap=gcol[s][:, :], axis=0)).then_inc(early_gathered[s], 16)

                def keep(j, s, b):
                    pool.wait_ge(early_gathered[s], 16 * (j + 1))
                    nc.gpsimd.tensor_copy(early[:, bass.ds(j * U + s, 1), :].rearrange("p o d -> p (o d)"), grow[s][:, :]
                                          ).then_inc(kept[s], 1)

                def store(j, s, b):
                    pool.wait_ge(biased[s], j + 1)
                    if b == NB - 1:
                        pool.wait_ge(*one_before(stored, j, s, 16))
                    pool.dma_start(rows_of(outp, j, s, b), yo[s][:, :, :]).then_inc(stored[s], 16)
                if nr == 2:
                    nc.gpsimd.tensor_tensor(bsum[:, :], bias_bc[:, 1, :], bias_bc[:, 2, :], ALU.add).then_inc(bias_ready, 1)
                    pool.wait_ge(bias_ready, 1)
                    pipeline(pool, NB, (0, bias), (0, gather), (2, keep))
                    for t in range(NB, EARLY * U + 2):
                        if t < EARLY * U:
                            gather(t // U, t % U, None)
                        if t >= NB + 2:
                            keep((t - 2) // U, (t - 2) % U, None)
                else:
                    pipeline(pool, NB, (0, add), (0, store))
                    for s in range(RING):
                        pool.wait_ge(stored[s], 16 * len(range(s, NB, RING)))

            @block.vector
            def _(dve):
                def statistics():
                    for b in range(NB + 1):
                        j, s = b // RING, b % RING
                        if b < NB:
                            dve.wait_ge(loaded[s], per * (j + 1))
                            norm_stats(nc, dve, j, s, RB, xin, stats, aggr, var_ready)
                        yield
                        if b > 0:
                            jb, sb = (b - 1) // RING, (b - 1) % RING
                            norm_inverse(nc, dve, jb, sb, rstd, aggr, std_ready)
                        yield
                        if b < NB:
                            norm_moments(nc, dve, j, s, RB, stats, mv, aggr, passed, var_ready)
                        yield
                        if b > 0:
                            norm_shift(nc, dve, jb, sb, mv, rstd, nbias, aggr, norm_ready)
                        yield

                steps = network(nc, dve, sort_step, asked, list_turned, K, V, m, dv, psgn, pstep, ps[2], ps[3])
                if nr == 1:
                    parts, done, due = statistics(), 0, blocks_due()
                    for step in steps:
                        behind = int(4 * due[step]) - done
                        for _ in range(max(min(behind, 1), behind - 3)):
                            next(parts)
                            done += 1
                    for _ in parts:
                        pass
                    lists[0](dve)
                else:
                    for _ in steps:
                        pass

            @block.scalar
            def _(act):
                def std(j, s, b):
                    norm_std(nc, act, j, s, mv, rstd, epsc, var_ready, std_ready)

                def norm(j, s, b):
                    after(act, turned[s], 2 * j)
                    norm_rows(nc, act, j, s, RB, xin, hid, rstd, nbias, norm_ready, hid_ready)

                def copy_T(j, s, b):
                    after(act, *two_before(prod, j, s, 2))
                    for k in range(2):
                        act.wait_ge(turned[s], 2 * j + k + 1)
                        nc.scalar.activation(hidT[s % 2][:, k * 4:k * 4 + 4, :],
                                             ps[k][:, :].rearrange("p (r d) -> p r d", r=4),
                                             ACT.Copy if nr == 1 else ACT.Relu).then_inc(hidT_ready[s], 1)

                def copy_y(j, s, b):
                    after(act, stored[s], 16 * j)
                    for k in range(2):
                        act.wait_ge(prod[s], 2 * j + k + 1)
                        nc.scalar.activation(yo[s][:, k * 4:k * 4 + 4, :],
                                             ps[4 + 2 * (s % 2) + k][:, :].rearrange("p (r d) -> p r d", r=4),
                                             ACT.Copy).then_inc(y_ready[s], 1)
                def store(j, s, b):
                    act.wait_ge(y_ready[s], 2 * (j + 1))
                    if b == NB - 1:
                        act.wait_ge(*one_before(stored, j, s, 16))
                    act.dma_start(rows_of(outp, j, s, b), yo[s][:, :, :]).then_inc(stored[s], 16)
                if nr == 1:
                    pipeline(act, NB, (2, norm), (3, copy_T), (4, copy_y), (0, std))
                else:
                    pipeline(act, NB, (0, copy_T), (1, copy_y), (2, store))
                    for s in range(RING):
                        act.wait_ge(stored[s], 16 * len(range(s, NB, RING)))

            @block.tensor
            def _(pe):
                def turn(j, s, b):
                    if nr == 1:
                        pe.wait_ge(hid_ready[s], j + 1)
                    else:
                        pe.wait_ge(loaded[s], per * (j + 1))
                    after(pe, *one_before(hidT_ready, j, s, 2))
                    of = (hid if nr == 1 else xin)[s]
                    for k in range(2):
                        for r in range(4):
                            t = nc.tensor.transpose(ps[k][:, r * D:(r + 1) * D], of[:, k * 4 + r, :], ident[:, :])
                        t.then_inc(turned[s], 1)

                def products(j, s, b):
                    after(pe, *two_before(y_ready, j, s, 2))
                    if nr == 2:
                        pe.wait_ge(res_ready[s], j + 1)
                    for k in range(2):
                        pe.wait_ge(hidT_ready[s], 2 * j + k + 1)
                        bank = ps[4 + 2 * (s % 2) + k]
                        for r in range(4):
                            mm = nc.tensor.matmul(bank[:, r * D:(r + 1) * D], hidT[s % 2][:, k * 4 + r, :], root,
                                                  start=True, stop=nr == 1)
                            if nr == 2:
                                mm = nc.tensor.matmul(bank[:, r * D:(r + 1) * D], ident[:, :], rin[s][:, k * 4 + r, :],
                                                      start=False, stop=True)
                        mm.then_inc(prod[s], 1)

                def sort_turn(i, k):
                    if k in SORT_TURNS:
                        pe.wait_ge(asked, i * 2 + (1 + SORT_TURNS.index(k)))
                        network_turn(nc, K, V, ps[2], ps[3], ident).then_inc(list_turned, 1)
                pipeline(pe, NB, (0, turn), (1, products), among=(SORT_START, TURNS // 2, 2, sort_turn))
                if nr == 1:
                    lists[1](pe)


def rgcn_edges(nc, sem, ps, ident, rows, target, W, layer, epsc, key_a, w_a, gat_a, put_a, rel_a, early=None):
    f32, i32 = mybir.dt.float32, mybir.dt.int32
    ALU, ACT = mybir.AluOpType, mybir.ActivationFunctionType
    v = nc.vector
    nm = f"e{layer}_"
    with ExitStack() as st:
        def ring(name, shape, n=RING, dt=f32):
            return [st.enter_context(nc.sbuf_tensor(f"{nm}{name}{i}", shape, dt)) for i in range(n)]

        def sems(name):
            return [sem(f"{nm}{name}{i}") for i in range(RING)]
        xin, msg = ring("xin", [P, U, D]), ring("msg", [P, U, D])
        hid, Sw, CT = ring("hid", [P, U, D], 2), ring("Sw", [P, U, GRP], 2), ring("CT", [P, U, D], 2)
        gidx, pidx, kw = ring("gidx", [P, U], RING, i32), ring("pidx", [P, U], RING, i32), ring("kw", [P, 2, U])
        stats = ring("stats", [P, U, 6])
        mv, rstd, nbias = ring("mv", [P, U, 2]), ring("rstd", [P, U]), ring("nbias", [P, U])
        gidx_ready, gathered, put, kw_ready = sems("gidx"), sems("gathered"), sems("put"), sems("kw")
        pidx_ready, keyT, S_ready, hid_ready = sems("pidx"), sems("keyT"), sems("S"), sems("hid")
        cprod, CT_ready, mprod, msg_ready = sems("cprod"), sems("CT"), sems("mprod"), sems("msg")
        if layer == 0:
            aggr, var_ready, std_ready, norm_ready = sems("aggr"), sems("var"), sems("std"), sems("norm")
        passed, started = sem(nm + "passed"), sem(nm + "started")

        with nc.Block() as block:
            @block.gpsimd
            def _(pool):
                def gather(j, s, b):
                    tiles(j, s, range(U))

                def tiles(j, s, us):
                    if 0 in us:
                        pool.wait_ge(gidx_ready[s], j + 1)
                        after(pool, hid_ready[s], j)
                        pool.sem_inc(started, 1)
                    for u in us:
                        nc.gpsimd.indirect_dma_start(xin[s][:, u, :], None, rows,
                                                     bass.IndirectOffsetOnAxis(ap=gidx[s][:, u:u + 1], axis=0)).then_inc(gathered[s], 16)

                def gather_rest(j, s, b):
                    share = range(s * (RING - 1) * U // RING, (s + 1) * (RING - 1) * U // RING)
                    for slot in range(1, RING):
                        us = [n % U for n in share if n // U == slot - 1]
                        if us and (b is None or b - s + slot < GA):
                            tiles(j, slot, us)

                def scatter(j, s, b):
                    pool.wait_ge(msg_ready[s], j + 1)
                    pool.wait_ge(pidx_ready[s], j + 1)
                    after(pool, *one_before(put, j, s, 16 * U))
                    pool.sem_inc(started, 1)
                    for u in range(U):
                        nc.gpsimd.indirect_dma_start(target, bass.IndirectOffsetOnAxis(ap=pidx[s][:, u:u + 1], axis=0),
                                                     msg[s][:, u, :], None, compute_op=ALU.add).then_inc(put[s], 16)
                pipeline(pool, GA, (0, gather if layer == 0 else gather_rest), (3, scatter))
                for s in range(RING):
                    pool.wait_ge(put[s], 16 * U * len(range(s, GA, RING)))

            @block.vector
            def _(dve):
                def gather_list(j, s, b):
                    if s == 0 and early is not None:
                        return
                    after(dve, gathered[s], 16 * U * j)
                    v.tensor_copy(gidx[s][:, :], gat_a[:, bass.ds(at_block(j, s) * U, U)]).then_inc(gidx_ready[s], 1)

                def prepare(j, s, b):
                    at = bass.ds(at_block(j, s) * U, U)
                    v.tensor_copy(kw[s][:, 0, :], key_a[:, at])
                    v.tensor_copy(kw[s][:, 1, :], w_a[:, at]).then_inc(kw_ready[s], 1)
                    after(dve, put[s], 16 * U * j)
                    v.tensor_copy(pidx[s][:, :], put_a[:, at]).then_inc(pidx_ready[s], 1)
                    if layer == 0:
                        dve.wait_ge(gathered[s], 16 * U * (j + 1))
                        norm_stats(nc, dve, j, s, U, xin, stats, aggr, var_ready)
                        norm_moments(nc, dve, j, s, U, stats, mv, aggr, passed, var_ready)
                        norm_inverse(nc, dve, j, s, rstd, aggr, std_ready)
                        norm_shift(nc, dve, j, s, mv, rstd, nbias, aggr, norm_ready)
                    after(dve, *two_before(cprod, j, s))
                    dve.wait_ge(keyT[s], j + 1)
                    dve.wait_ge(kw_ready[s], j + 1)
                    for u in range(U):
                        eq = v.tensor_scalar(Sw[s % 2][:, u, u * P:GRP], ps[s % 2][:, u * P:GRP], kw[s][:, 0, u:u + 1],
                                             kw[s][:, 1, u:u + 1], ALU.is_equal, ALU.mult)
                    eq.then_inc(S_ready[s], 1)
                pipeline(dve, GA, (0, gather_list), (3, prepare))

            @block.scalar
            def _(act):
                def norm(j, s, b):
                    after(act, *two_before(cprod, j, s))
                    if layer == 0:
                        norm_std(nc, act, j, s, mv, rstd, epsc, var_ready, std_ready)
                        act.wait_ge(norm_ready[s], j + 1)
                        for u in range(U):
                            t = nc.scalar.activation(hid[s % 2][:, u, :], xin[s][:, u, :], ACT.Relu,
                                                     bias=nbias[s][:, u:u + 1], scale=rstd[s][:, u:u + 1])
                        t.then_inc(hid_ready[s], 1)
                    elif s == 0:
                        nc.scalar.activation(hid[s % 2][:, :, :], early[:, bass.ds(j * U, U), :], ACT.Relu).then_inc(hid_ready[s], 1)
                    else:
                        act.wait_ge(gathered[s], 16 * U * (j + 1))
                        nc.scalar.activation(hid[s % 2][:, :, :], xin[s][:, :, :], ACT.Relu).then_inc(hid_ready[s], 1)

                def copies(j, s, b):
                    act.wait_ge(cprod[s], j + 1)
                    after(act, *two_before(mprod, j, s))
                    nc.scalar.activation(CT[s % 2][:, :, :], ps[2 + s % 2][:, :].rearrange("p (u d) -> p u d", u=U),
                                         ACT.Copy).then_inc(CT_ready[s], 1)
                    act.wait_ge(mprod[s], j + 1)
                    after(act, put[s], 16 * U * j)
                    nc.scalar.activation(msg[s][:, :, :], ps[4 + s % 2][:, :].rearrange("p (u d) -> p u d", u=U),
                                         ACT.Copy).then_inc(msg_ready[s], 1)
                pipeline(act, GA, (0, norm), (1, copies))

            @block.tensor
            def _(pe):
                def keys(j, s, b):
                    pe.wait_ge(kw_ready[s], j + 1)
                    after(pe, *two_before(S_ready, j, s))
                    for u in range(U):
                        t = nc.tensor.transpose(ps[s % 2][:, u * P:(u + 1) * P],
                                                kw[s][:, 0, u:u + 1].to_broadcast([P, P]), ident[:, :])
                    t.then_inc(keyT[s], 1)

                def products(j, s, b):
                    rel = pe.value_load(rel_a[0:1, bass.ds(at_block(j, s), 1)], min_val=0, max_val=R - 1)
                    pe.wait_ge(hid_ready[s], j + 1)
                    pe.wait_ge(S_ready[s], j + 1)
                    after(pe, *two_before(CT_ready, j, s))
                    for u in range(U):
                        mm = nc.tensor.matmul(ps[2 + s % 2][:, u * P:GRP], hid[s % 2][:, u, :], Sw[s % 2][:, u, u * P:GRP],
                                              start=u == 0, stop=u == U - 1)
                    mm.then_inc(cprod[s], 1)
                    pe.wait_ge(CT_ready[s], j + 1)
                    after(pe, *two_before(msg_ready, j, s))
                    for u in range(U):
                        mm = nc.tensor.matmul(ps[4 + s % 2][:, u * P:(u + 1) * P], CT[s % 2][:, u, :],
                                              W[:, layer, bass.ds(rel * D, D)], start=True, stop=True)
                    mm.then_inc(mprod[s], 1)
                pipeline(pe, GA, (0, keys), (1, products))


def gat_scores(nc, sem, ps, ident, rows, g_tiles, wg, bias_bc, epsc, gat_c, own_c, score):
    f32, i32 = mybir.dt.float32, mybir.dt.int32
    ALU, ACT = mybir.AluOpType, mybir.ActivationFunctionType
    v = nc.vector
    nm = "s_"
    U2 = 2 * U
    with ExitStack() as st:
        def ring(name, shape, n=RING, dt=f32):
            return [st.enter_context(nc.sbuf_tensor(f"{nm}{name}{i}", shape, dt)) for i in range(n)]

        def sems(name):
            return [sem(f"{nm}{name}{i}") for i in range(RING)]
        xin, hid = ring("xin", [P, U2, D]), ring("hid", [P, U2, D])
        hidT, gout = ring("hidT", [P, U2, D], 2), ring("gout", [P, U, D])
        gidx = ring("gidx", [P, 2, U], RING, i32)
        stats = ring("stats", [P, U2, 6])
        mv, rstd, nbias = ring("mv", [P, U2, 2]), ring("rstd", [P, U2]), ring("nbias", [P, U2])
        gidx_ready, gathered, bias_off, hid_ready = sems("gidx"), sems("gathered"), sems("bias_off"), sems("hid")
        turned, hidT_ready, prod, g_ready = sems("turned"), sems("hidT"), sems("prod"), sems("g")
        score_ready, stored = sems("score"), sems("stored")
        aggr, var_ready, std_ready, norm_ready = sems("aggr"), sems("var"), sems("std"), sems("norm")
        passed, started = sem(nm + "passed"), sem(nm + "started")
        per = 16 * U2

        with nc.Block() as block:
            @block.gpsimd
            def _(pool):
                def gather(j, s, b):
                    pool.wait_ge(gidx_ready[s], j + 1)
                    after(pool, hid_ready[s], j)
                    pool.sem_inc(started, 1)
                    for side in range(2):
                        for u in range(U):
                            nc.gpsimd.indirect_dma_start(
                                xin[s][:, side * U + u, :], None, rows,
                                bass.IndirectOffsetOnAxis(ap=gidx[s][:, side, u:u + 1], axis=0)).then_inc(gathered[s], 16)
                pipeline(pool, GC, (0, gather))

            @block.sync
            def _(sp):
                def store(j, s, b):
                    sp.wait_ge(g_ready[s], j + 1)
                    sp.dma_start(g_tiles[bass.ds(at_block(j, s), 1), :, :, :].rearrange("o q u d -> (o q) u d"),
                                 gout[s][:, :, :]).then_inc(stored[s], 16)
                pipeline(sp, GC, (0, store))
                for s in range(RING):
                    sp.wait_ge(stored[s], 16 * len(range(s, GC, RING)))

            @block.vector
            def _(dve):
                def gather_list(j, s, b):
                    at = bass.ds(at_block(j, s) * U, U)
                    after(dve, gathered[s], per * j)
                    v.tensor_copy(gidx[s][:, 0, :], gat_c[:, at])
                    v.tensor_copy(gidx[s][:, 1, :], own_c[:, at]).then_inc(gidx_ready[s], 1)

                def stat(j, s, b):
                    dve.wait_ge(gathered[s], per * (j + 1))
                    v.tensor_tensor(xin[s][:, :, :], xin[s][:, :, :], bias_bc[:, 2:3, :].to_broadcast([P, U2, D]),
                                    ALU.subtract).then_inc(bias_off[s], 1)
                    dve.wait_ge(bias_off[s], j + 1)
                    norm_stats(nc, dve, j, s, U2, xin, stats, aggr, var_ready)
                    norm_moments(nc, dve, j, s, U2, stats, mv, aggr, passed, var_ready)
                    norm_inverse(nc, dve, j, s, rstd, aggr, std_ready)
                    norm_shift(nc, dve, j, s, mv, rstd, nbias, aggr, norm_ready)

                def keep(j, s, b):
                    dve.wait_ge(prod[s], j + 1)
                    v.tensor_copy(score[:, :, bass.ds(at_block(j, s) * U, U)],
                                  ps[6 + s % 2][:, 0:U * H].rearrange("p (u h) -> p h u", u=U)).then_inc(score_ready[s], 1)
                pipeline(dve, GC, (0, gather_list), (2, stat), (4, keep))

            @block.scalar
            def _(act):
                def norm(j, s, b):
                    after(act, turned[s], 2 * j)
                    norm_std(nc, act, j, s, mv, rstd, epsc, var_ready, std_ready)
                    norm_rows(nc, act, j, s, U2, xin, hid, rstd, nbias, norm_ready, hid_ready)

                def copy_T(j, s, b):
                    after(act, *two_before(prod, j, s))
                    for k in range(2):
                        act.wait_ge(turned[s], 2 * j + k + 1)
                        nc.scalar.activation(hidT[s % 2][:, k * U:(k + 1) * U, :],
                                             ps[2 * (s % 2) + k][:, :].rearrange("p (u d) -> p u d", u=U),
                                             ACT.Copy).then_inc(hidT_ready[s], 1)

                def copy_g(j, s, b):
                    act.wait_ge(prod[s], j + 1)
                    after(act, stored[s], 16 * j)
                    nc.scalar.activation(gout[s][:, :, :], ps[4 + s % 2][:, :].rearrange("p (u d) -> p u d", u=U),
                                         ACT.Copy).then_inc(g_ready[s], 1)
                pipeline(act, GC, (1, copy_T), (0, norm), (2, copy_g))

            @block.tensor
            def _(pe):
                def turn(j, s, b):
                    pe.wait_ge(hid_ready[s], j + 1)
                    after(pe, *two_before(hidT_ready, j, s, 2))
                    for k in range(2):
                        for u in range(U):
                            t = nc.tensor.transpose(ps[2 * (s % 2) + k][:, u * P:(u + 1) * P], hid[s][:, k * U + u, :], ident[:, :])
                        t.then_inc(turned[s], 1)

                def products(j, s, b):
                    pe.wait_ge(hidT_ready[s], 2 * j + 2)
                    after(pe, *two_before(g_ready, j, s))
                    after(pe, *two_before(score_ready, j, s))
                    for u in range(U):
                        nc.tensor.matmul(ps[4 + s % 2][:, u * D:(u + 1) * D], hidT[s % 2][:, u, :], wg[:, 0:D], start=True, stop=True)
                        nc.tensor.matmul(ps[6 + s % 2][:, u * H:(u + 1) * H], hidT[s % 2][:, u, :], wg[:, D:D + H],
                                         start=True, stop=False)
                        mm = nc.tensor.matmul(ps[6 + s % 2][:, u * H:(u + 1) * H], hidT[s % 2][:, U + u, :], wg[:, D + H:D + 2 * H],
                                              start=False, stop=True)
                    mm.then_inc(prod[s], 1)
                pipeline(pe, GC, (0, turn), (1, products))


def gat_softmax(nc, sem, chain_of, ps, ident, up_c, down_c, score):
    f32 = mybir.dt.float32
    ALU, ACT = mybir.AluOpType, mybir.ActivationFunctionType
    v = nc.vector
    PC = TC // U
    step, asked, turned, shifted, exped = sem("sm_step"), sem("sm_asked"), sem("sm_turned"), sem("sm_shifted"), sem("sm_exp")
    with ExitStack() as st:
        def tb(name, shape):
            return st.enter_context(nc.sbuf_tensor("sm_" + name, shape, f32))
        a, b, res = tb("a", [PC, H, FREE]), tb("b", [PC, H, FREE]), tb("res", [PC, H, FREE])
        tmp, small, rows = tb("tmp", [P, 1, FREE]), tb("small", [P, 4 * H]), tb("rows", [H, 2, P])
        up, down = up_c[0:PC, :], down_c[0:PC, :]
        with nc.Block() as block:
            @block.vector
            def _(dve):
                link = chain_of(dve, step)
                dve.wait_ge(turned, 1)
                for h in range(H):
                    cp = v.tensor_copy(a[:, h, :], ps[h][0:PC, :])
                link(cp)
                link(v.scalar_tensor_tensor(out=a[:, :, :], in0=a[:, :, :], scalar=SLOPE, in1=a[:, :, :],
                                            op0=ALU.mult, op1=ALU.max))
                link(v.tensor_copy(b[:, :, :], a[:, :, :]))
                n = totals_vector(nc, dve, link, asked, turned, 1, ps, b[:, :, :], res[:, :, :], up, down,
                                  tmp, small, rows, H, PC, True)
                v.tensor_tensor(a[:, :, :], a[:, :, :], res[:, :, :], ALU.subtract).then_inc(shifted, 1)
                dve.wait_ge(exped, 1)
                link(v.tensor_copy(b[:, :, :], a[:, :, :]))
                n = totals_vector(nc, dve, link, asked, turned, n, ps, b[:, :, :], res[:, :, :], up, down,
                                  tmp, small, rows, H, PC, False)
                link(v.tensor_scalar(res[:, :, :], res[:, :, :], TINY, None, ALU.add))
                link(v.reciprocal(res[:, :, :], res[:, :, :]))
                n += 1
                v.tensor_tensor(a[:, :, :], a[:, :, :], res[:, :, :], ALU.mult).then_inc(asked, 1)
                dve.wait_ge(turned, n)
                for h in range(H):
                    cp = v.tensor_copy(score[:, h, :].rearrange("q (p c) -> q c p", c=U),
                                       ps[4 + h][:, 0:TC].rearrange("q (c p) -> q c p", c=U))
                link(cp)

            @block.scalar
            def _(act):
                act.wait_ge(shifted, 1)
                nc.scalar.activation(a[:, :, :], a[:, :, :], ACT.Exp).then_inc(exped, 1)

            @block.tensor
            def _(pe):
                for h in range(H):
                    for c in range(U):
                        t = nc.tensor.transpose(ps[h][0:PC, c * P:(c + 1) * P], score[:, h, c::U], ident[:, :])
                t.then_inc(turned, 1)
                n = totals_tensor(nc, pe, asked, turned, 0, ps, ident, small, rows, H, PC)
                n = totals_tensor(nc, pe, asked, turned, n, ps, ident, small, rows, H, PC)
                pe.wait_ge(asked, n + 1)
                for h in range(H):
                    for c in range(U):
                        t = nc.tensor.transpose(ps[4 + h][:, c * PC:(c + 1) * PC], a[:, h, c * P:(c + 1) * P], ident[0:PC, 0:PC])
                t.then_inc(turned, 1)


def gat_edges(nc, sem, ps, ident, g_tiles, target, score, key_c, put_c):
    f32, i32 = mybir.dt.float32, mybir.dt.int32
    ALU, ACT = mybir.AluOpType, mybir.ActivationFunctionType
    v = nc.vector
    nm = "g_"
    Q3 = P - 32
    with ExitStack() as st:
        def ring(name, shape, n=RING, dt=f32):
            return [st.enter_context(nc.sbuf_tensor(f"{nm}{name}{i}", shape, dt)) for i in range(n)]

        def sems(name):
            return [sem(f"{nm}{name}{i}") for i in range(RING)]
        gin, msg = ring("gin", [P, U, D]), ring("msg", [P, U, D])
        gs, S, sumT = ring("gs", [P, U, D], 2), ring("S", [P, U, GRP], 2), ring("sumT", [P, U, P], 2)
        carry = ring("carry", [P, GRP], 2)
        pidx, kcol, co = ring("pidx", [P, U], RING, i32), ring("kcol", [P, U]), ring("co", [P, U, H])
        is_last = ring("is_last", [P, 1], 1)[0]
        loaded, slots, keyT, S_ready, scaled = sems("loaded"), sems("slots"), sems("keyT"), sems("S"), sems("scaled")
        pidx_ready, prod, sumT_ready, back = sems("pidx"), sems("prod"), sems("sumT"), sems("back")
        msg_ready, put = sems("msg"), sems("put")
        started, marked = sem(nm + "started"), sem(nm + "marked")

        with nc.Block() as block:
            @block.sync
            def _(sp):
                def load(j, s, b):
                    after(sp, scaled[s], j)
                    sp.dma_start(gin[s][:, :, :], g_tiles[bass.ds(at_block(j, s), 1), :, :, :].rearrange("o q u d -> (o q) u d")
                                 ).then_inc(loaded[s], 16)
                pipeline(sp, GC, (0, load))

            @block.gpsimd
            def _(pool):
                def scatter(j, s, b):
                    pool.wait_ge(msg_ready[s], j + 1)
                    pool.wait_ge(pidx_ready[s], j + 1)
                    pool.sem_inc(started, 1)
                    for u in range(U):
                        nc.gpsimd.indirect_dma_start(target, bass.IndirectOffsetOnAxis(ap=pidx[s][:, u:u + 1], axis=0),
                                                     msg[s][:, u, :], None, compute_op=ALU.add).then_inc(put[s], 16)
                pipeline(pool, GC, (0, scatter))
                for s in range(RING):
                    pool.wait_ge(put[s], 16 * U * len(range(s, GC, RING)))

            @block.vector
            def _(dve):
                def lists(j, s, b):
                    at = bass.ds(at_block(j, s) * U, U)
                    after(dve, S_ready[(s + 1) % RING], j + (s + 1) // RING)
                    v.tensor_copy(kcol[s][:, :], key_c[:, at])
                    v.tensor_copy(co[s][:, :, :], score[:, :, at].rearrange("p h u -> p u h")).then_inc(slots[s], 1)

                def rows(j, s, b):
                    after(dve, put[s], 16 * U * j)
                    v.tensor_copy(pidx[s][:, :], put_c[:, bass.ds(at_block(j, s) * U, U)]).then_inc(pidx_ready[s], 1)

                def prepare(j, s, b):
                    dve.wait_ge(slots[s], j + 1)
                    dve.wait_ge(loaded[s], 16 * (j + 1))
                    after(dve, *two_before(prod, j, s))
                    v.tensor_tensor(gs[s % 2][:, :, :].rearrange("p u (h f) -> p (u h) f", h=H),
                                    gin[s][:, :, :].rearrange("p u (h f) -> p (u h) f", h=H),
                                    co[s][:, :, :].rearrange("p u (h o) -> p (u h) o", o=1).to_broadcast([P, U * H, F]),
                                    ALU.mult).then_inc(scaled[s], 1)
                    dve.wait_ge(keyT[s], j + 1)
                    if b != 0:
                        v.tensor_scalar(carry[s % 2][Q3:P, :], ps[s % 2][Q3:P, :], kcol[s - 1][Q3:P, U - 1:U],
                                        is_last[Q3:P, 0:1], ALU.is_equal, ALU.mult)
                    for u in range(U):
                        eq = v.tensor_scalar(S[s % 2][:, u, u * P:GRP], ps[s % 2][:, u * P:GRP], kcol[s][:, u:u + 1],
                                             None, ALU.is_equal)
                    eq.then_inc(S_ready[s], 1)
                v.tensor_copy(is_last[:, :], ident[:, P - 1:P]).then_inc(marked, 1)
                dve.wait_ge(marked, 1)
                pipeline(dve, GC, (0, lists), (1, prepare), (2, rows))

            @block.scalar
            def _(act):
                def copies(j, s, b):
                    act.wait_ge(prod[s], j + 1)
                    after(act, *two_before(back, j, s))
                    nc.scalar.activation(sumT[s % 2][:, :, :], ps[2 + s % 2][:, :].rearrange("p (u d) -> p u d", u=U),
                                         ACT.Copy).then_inc(sumT_ready[s], 1)
                    act.wait_ge(back[s], j + 1)
                    after(act, put[s], 16 * U * j)
                    nc.scalar.activation(msg[s][:, :, :], ps[4 + s % 2][:, :].rearrange("p (u d) -> p u d", u=U),
                                         ACT.Copy).then_inc(msg_ready[s], 1)
                pipeline(act, GC, (0, copies))

            @block.tensor
            def _(pe):
                def keys(j, s, b):
                    pe.wait_ge(slots[s], j + 1)
                    after(pe, *two_before(S_ready, j, s))
                    for u in range(U):
                        t = nc.tensor.transpose(ps[s % 2][:, u * P:(u + 1) * P], kcol[s][:, u:u + 1].to_broadcast([P, P]), ident[:, :])
                    t.then_inc(keyT[s], 1)

                def sums(j, s, b, us):
                    for u in us:
                        mm = nc.tensor.matmul(ps[2 + s % 2][:, u * P:GRP], gs[s % 2][:, u, :], S[s % 2][:, u, u * P:GRP],
                                              start=u == 0, stop=u == U - 1 and b == 0)
                    return mm

                def first_sums(j, s, b):
                    pe.wait_ge(S_ready[s], j + 1)
                    pe.wait_ge(scaled[s], j + 1)
                    after(pe, *two_before(sumT_ready, j, s))
                    sums(j, s, b, range(U // 2))

                def last_sums(j, s, b):
                    mm = sums(j, s, b, range(U // 2, U))
                    if b == 0:
                        mm.then_inc(prod[s], 1)

                def carried(j, s, b):
                    if b != 0:
                        pe.wait_ge(*one_before(msg_ready, j, s))
                        nc.tensor.matmul(ps[2 + s % 2][:, :], msg[s - 1][Q3:P, U - 1, :], carry[s % 2][Q3:P, :],
                                         start=False, stop=True).then_inc(prod[s], 1)

                def turn_back(j, s, b):
                    pe.wait_ge(sumT_ready[s], j + 1)
                    after(pe, *two_before(msg_ready, j, s))
                    for u in range(U):
                        t = nc.tensor.transpose(ps[4 + s % 2][:, u * D:(u + 1) * D], sumT[s % 2][:, u, :], ident[:, :])
                    t.then_inc(back[s], 1)
                pipeline(pe, GC, (2, first_sums), (3, turn_back), (2, last_sums), (0, keys), (2, carried))


_INS = ["x", "src", "dst", "edge_type_8", "L0_gnn_weights", "L0_gnn_roots", "L0_gnn_biases",
        "L1_gnn_weight", "L1_gnn_att", "L1_gnn_bias"]


def kernel(**inputs):
    import numpy as _np
    import concourse.bacc as _bacc
    from concourse import mybir as _mybir
    from concourse.bass_utils import run_bass_kernel_spmd as _run

    nc = _bacc.Bacc("TRN2", target_bir_lowering=False, num_devices=1)
    arrays, args = {}, []
    for name in _INS:
        a = _np.ascontiguousarray(inputs[name])
        arrays[f"in_{name}"] = a
        args.append(nc.dram_tensor(f"in_{name}", a.shape, _mybir.dt.from_np(a.dtype), kind="ExternalInput").ap())
    args.append(nc.dram_tensor("out_0", (N + DUMP, D), _mybir.dt.float32, kind="ExternalOutput").ap())
    gnn_program(nc, *args)
    r = _run(nc, [arrays], core_ids=[0])
    return r.results[0]["out_0"][:N]
```
